# Optimizing a Trainium2 kernel written in Bass

```python
import numpy as np
import jax
import jax.numpy as jnp

def _softmax(x, axis=-1):
    return jax.nn.softmax(x, axis=axis)

def _gelu(x):
    return jax.nn.gelu(x, approximate=True)

def _silu(x):
    return jax.nn.silu(x)

def _sigmoid(x):
    return jax.nn.sigmoid(x)

def _layernorm(x, axis=-1, eps=1e-05):
    m = jnp.mean(x, axis=axis, keepdims=True)
    v = jnp.var(x, axis=axis, keepdims=True)
    return (x - m) / jnp.sqrt(v + eps)

def _scatter_add(tgt, idx, src, axis=0):
    return tgt.at[idx].add(src)

def _segment_sum(src, seg, n):
    return jax.ops.segment_sum(src, seg, n)
kernel_name = 'mk_flamingo_gated_d2_seqx_r4_f0cb65'

def setup_inputs(seed: int=0):
    np.random.seed(seed)
    _w = jnp.asarray

    def _rec_inputs():
        import jax
        import jax.numpy as jnp
        _rk = jax.random.key(seed)
        x = 7.22e-05 + 1 * jax.random.normal(jax.random.fold_in(_rk, 1), (16, 100, 256), jnp.float32)
        _lenS = 100 - jax.random.randint(jax.random.fold_in(_rk, 7), (16,), 0, max(1, 100 // 4) + 1, jnp.int32)
        _lenS2 = 361 - jax.random.randint(jax.random.fold_in(_rk, 8), (16,), 0, max(1, 361 // 4) + 1, jnp.int32)
        _ctx_1024P = jax.random.normal(jax.random.fold_in(_rk, 11), (16, 16, 256), jnp.float32)
        _ctx_1024c = jax.random.dirichlet(jax.random.fold_in(_rk, 511), 0.3 * jnp.ones((16,), jnp.float32), (16, 361))
        _ctx_1024t = jnp.einsum('bsk,bkd->bsd', _ctx_1024c, _ctx_1024P)
        _ctx_1024t = _ctx_1024t * jax.lax.rsqrt(jnp.mean(jnp.square(_ctx_1024t)) + 1e-12) * 0.953939
        ctx_1024 = 4.13588e-05 + 0.999923 * (_ctx_1024t + 0.3 * jax.random.normal(jax.random.fold_in(_rk, 611), (16, 361, 256), jnp.float32))
        _validS = jnp.arange(100)[None, :] < _lenS[:, None]
        _validS2 = jnp.arange(361)[None, :] < _lenS2[:, None]
        _causal = jnp.tril(jnp.ones((100, 100), dtype=bool))
        mask_Bx1xSxS2_bk1 = jnp.broadcast_to(_validS2[:, None, None, :], (16, 1, 100, 361))
        _g = jax.random.normal(jax.random.fold_in(_rk, 9001), (2, 2), jnp.float32)
        _g = jnp.sign(_g) * jnp.maximum(jnp.abs(_g), 1.0) + (_g == 0) * 1.0
        g_xattn = _g[0]
        g_ffn = _g[1]
        return (x, ctx_1024, mask_Bx1xSxS2_bk1, g_xattn, g_ffn)
    x, ctx_1024, mask_Bx1xSxS2_bk1, g_xattn, g_ffn = _rec_inputs()

    def _L0_xattn_setup():
        import jax, jax.numpy as jnp
        import numpy as np
        B, S, D, H = (4, 512, 256, 16)
        HD = D // H
        key = jax.random.key(seed)
        ks = jax.random.split(key, 12)
        scale = 1.0 / np.sqrt(D)
        inp = {'queries': jax.random.normal(ks[0], (B, S, D), jnp.float32), 'keys': jax.random.normal(ks[1], (B, S, D), jnp.float32), 'values': jax.random.normal(ks[2], (B, S, D), jnp.float32), 'mask': jax.random.randint(ks[3], (B, 1, S, S), 0, 2).astype(bool), 'Wq': jax.random.normal(ks[4], (D, D), jnp.float32) * scale, 'bq': jnp.zeros((D,), jnp.float32), 'Wk': jax.random.normal(ks[5], (D, D), jnp.float32) * scale, 'bk': jnp.zeros((D,), jnp.float32), 'Wv': jax.random.normal(ks[6], (D, D), jnp.float32) * scale, 'bv': jnp.zeros((D,), jnp.float32), 'Wo': jax.random.normal(ks[7], (D, D), jnp.float32) * scale, 'bo': jnp.zeros((D,), jnp.float32)}
        return inp
    _L0_xattn_all = _L0_xattn_setup()
    _L0_xattn_in = {k: v for k, v in _L0_xattn_all.items() if k in ('Wq', 'bq', 'Wk', 'bk', 'Wv', 'bv', 'Wo', 'bo')}
    del _L0_xattn_all

    def _L0_ffn_setup():
        import jax, jax.numpy as jnp
        import numpy as np
        TOP_K = 2
        ROUTE_SCALE = 1.0
        EPS = 1e-20
        B, S, D = (2, 128, 256)
        E = 8
        F = 192
        FS = 192 * 1
        key = jax.random.key(seed)
        ks = jax.random.split(key, 9)
        s = 0.02
        return {'hidden_states': jax.random.normal(ks[0], (B, S, D), dtype=jnp.float32), 'W_gate_router': jax.random.normal(ks[1], (D, E), dtype=jnp.float32) * s, 'expert_bias': jnp.zeros((E,), dtype=jnp.float32), 'Wg': jax.random.normal(ks[2], (E, D, F), dtype=jnp.float32) * s, 'Wu': jax.random.normal(ks[3], (E, D, F), dtype=jnp.float32) * s, 'Wd': jax.random.normal(ks[4], (E, F, D), dtype=jnp.float32) * s, 'Wg_s': jax.random.normal(ks[5], (D, FS), dtype=jnp.float32) * s, 'Wu_s': jax.random.normal(ks[6], (D, FS), dtype=jnp.float32) * s, 'Wd_s': jax.random.normal(ks[7], (FS, D), dtype=jnp.float32) * s}
    _L0_ffn_all = _L0_ffn_setup()
    _L0_ffn_in = {k: v for k, v in _L0_ffn_all.items() if k in ('W_gate_router', 'expert_bias', 'Wg', 'Wu', 'Wd', 'Wg_s', 'Wu_s', 'Wd_s')}
    del _L0_ffn_all

    def _L1_xattn_setup():
        import jax, jax.numpy as jnp
        import numpy as np
        EMBED = 256
        HEADS = 16
        HEAD_DIM = EMBED // HEADS
        key = jax.random.key(seed)
        ks = jax.random.split(key, 7)
        B, Sd, Se = (4, 512, 512)
        dec = jax.random.normal(ks[0], (B, Sd, EMBED), dtype=jnp.float32)
        enc = jax.random.normal(ks[1], (B, Se, EMBED), dtype=jnp.float32)
        scale = 1.0 / np.sqrt(EMBED)
        W_q = jax.random.normal(ks[2], (EMBED, EMBED), dtype=jnp.float32) * scale
        W_k = jax.random.normal(ks[3], (EMBED, EMBED), dtype=jnp.float32) * scale
        W_v = jax.random.normal(ks[4], (EMBED, EMBED), dtype=jnp.float32) * scale
        W_o = jax.random.normal(ks[5], (EMBED, EMBED), dtype=jnp.float32) * scale
        b_o = jax.random.normal(ks[6], (EMBED,), dtype=jnp.float32) * 0.01
        return {'decoder_input': dec, 'encoder_output': enc, 'W_q': W_q, 'W_k': W_k, 'W_v': W_v, 'W_o': W_o, 'b_o': b_o}
    _L1_xattn_all = _L1_xattn_setup()
    _L1_xattn_in = {k: v for k, v in _L1_xattn_all.items() if k in ('W_q', 'W_k', 'W_v', 'W_o', 'b_o')}
    del _L1_xattn_all

    def _L1_ffn_setup():
        import jax, jax.numpy as jnp
        import numpy as np
        B, S, D, F, E, R = (4, 512, 256, 1024, 8, 4)
        key = jax.random.key(seed)
        ks = jax.random.split(key, 8)
        s_in = 1.0 / np.sqrt(D)
        s_ff = 1.0 / np.sqrt(F)
        return {'hidden_states': jax.random.normal(ks[0], (B, S, D), jnp.float32), 'gate_W': jax.random.normal(ks[1], (E, D), jnp.float32) * s_in, 'gate_b': jnp.zeros((E,), jnp.float32), 'wi_W': jax.random.normal(ks[2], (F, D), jnp.float32) * s_in, 'wi_b': jnp.zeros((F,), jnp.float32), 'wo_W': jax.random.normal(ks[3], (D, F), jnp.float32) * s_ff, 'wo_b': jnp.zeros((D,), jnp.float32), 'lora_A': jax.random.normal(ks[4], (E, R, D), jnp.float32) * s_in, 'lora_B': jax.random.normal(ks[5], (E, F, R), jnp.float32) * 0.02}
    _L1_ffn_all = _L1_ffn_setup()
    _L1_ffn_in = {k: v for k, v in _L1_ffn_all.items() if k in ('gate_W', 'gate_b', 'wi_W', 'wi_b', 'wo_W', 'wo_b', 'lora_A', 'lora_B')}
    del _L1_ffn_all
    return {'x': x, 'ctx_1024': ctx_1024, 'mask_Bx1xSxS2_bk1': mask_Bx1xSxS2_bk1, 'g_xattn': g_xattn, 'g_ffn': g_ffn, 'L0_xattn_Wq': _L0_xattn_in['Wq'], 'L0_xattn_bq': _L0_xattn_in['bq'], 'L0_xattn_Wk': _L0_xattn_in['Wk'], 'L0_xattn_bk': _L0_xattn_in['bk'], 'L0_xattn_Wv': _L0_xattn_in['Wv'], 'L0_xattn_bv': _L0_xattn_in['bv'], 'L0_xattn_Wo': _L0_xattn_in['Wo'], 'L0_xattn_bo': _L0_xattn_in['bo'], 'L0_ffn_W_gate_router': _L0_ffn_in['W_gate_router'], 'L0_ffn_expert_bias': _L0_ffn_in['expert_bias'], 'L0_ffn_Wg': _L0_ffn_in['Wg'], 'L0_ffn_Wu': _L0_ffn_in['Wu'], 'L0_ffn_Wd': _L0_ffn_in['Wd'], 'L0_ffn_Wg_s': _L0_ffn_in['Wg_s'], 'L0_ffn_Wu_s': _L0_ffn_in['Wu_s'], 'L0_ffn_Wd_s': _L0_ffn_in['Wd_s'], 'L1_xattn_W_q': _L1_xattn_in['W_q'], 'L1_xattn_W_k': _L1_xattn_in['W_k'], 'L1_xattn_W_v': _L1_xattn_in['W_v'], 'L1_xattn_W_o': _L1_xattn_in['W_o'], 'L1_xattn_b_o': _L1_xattn_in['b_o'], 'L1_ffn_gate_W': _L1_ffn_in['gate_W'], 'L1_ffn_gate_b': _L1_ffn_in['gate_b'], 'L1_ffn_wi_W': _L1_ffn_in['wi_W'], 'L1_ffn_wi_b': _L1_ffn_in['wi_b'], 'L1_ffn_wo_W': _L1_ffn_in['wo_W'], 'L1_ffn_wo_b': _L1_ffn_in['wo_b'], 'L1_ffn_lora_A': _L1_ffn_in['lora_A'], 'L1_ffn_lora_B': _L1_ffn_in['lora_B']}

def reference(x, ctx_1024, mask_Bx1xSxS2_bk1, g_xattn, g_ffn, L0_xattn_Wq, L0_xattn_bq, L0_xattn_Wk, L0_xattn_bk, L0_xattn_Wv, L0_xattn_bv, L0_xattn_Wo, L0_xattn_bo, L0_ffn_W_gate_router, L0_ffn_expert_bias, L0_ffn_Wg, L0_ffn_Wu, L0_ffn_Wd, L0_ffn_Wg_s, L0_ffn_Wu_s, L0_ffn_Wd_s, L1_xattn_W_q, L1_xattn_W_k, L1_xattn_W_v, L1_xattn_W_o, L1_xattn_b_o, L1_ffn_gate_W, L1_ffn_gate_b, L1_ffn_wi_W, L1_ffn_wi_b, L1_ffn_wo_W, L1_ffn_wo_b, L1_ffn_lora_A, L1_ffn_lora_B):
    import jax
    import jax.numpy as jnp

    def _L0_xattn_ref(queries, keys, values, mask, Wq, bq, Wk, bk, Wv, bv, Wo, bo):
        import jax, jax.numpy as jnp
        import numpy as np
        B, S, D, H = (4, 512, 256, 16)
        HD = D // H
        b, sq, d = queries.shape

        def split_heads(x):
            return x.reshape(b, x.shape[1], H, HD).transpose(0, 2, 1, 3)
        q = split_heads(queries @ Wq + bq)
        k = split_heads(keys @ Wk + bk)
        v = split_heads(values @ Wv + bv)
        scores = jnp.einsum('bhqd,bhkd->bhqk', q, k) / jnp.sqrt(jnp.float32(HD))
        scores = jnp.where(mask, jnp.float32(-1000000000000000.0), scores)
        attn = jax.nn.softmax(scores, axis=-1)
        ctx = jnp.einsum('bhqk,bhkd->bhqd', attn, v)
        ctx = ctx.transpose(0, 2, 1, 3).reshape(b, sq, d)
        return ctx @ Wo + bo

    def _L0_ffn_ref(hidden_states, W_gate_router, expert_bias, Wg, Wu, Wd, Wg_s, Wu_s, Wd_s):
        import jax, jax.numpy as jnp
        import numpy as np
        TOP_K = 2
        ROUTE_SCALE = 1.0
        EPS = 1e-20
        B, S, D = (2, 128, 256)
        E = 8
        F = 192
        FS = 192 * 1
        b, s, d = hidden_states.shape
        x = hidden_states.reshape(-1, d)
        T = x.shape[0]
        logits = x @ W_gate_router
        scores = jax.nn.sigmoid(logits.astype(jnp.float32))
        _, sel = jax.lax.top_k(scores + expert_bias, TOP_K)
        top_scores = jnp.take_along_axis(scores, sel, axis=1)
        top_scores = top_scores / (top_scores.sum(-1, keepdims=True) + EPS)
        top_scores = top_scores * ROUTE_SCALE
        shared = jax.nn.silu(x @ Wg_s) * (x @ Wu_s) @ Wd_s
        tok = jnp.repeat(jnp.arange(T), TOP_K)
        exp = sel.reshape(-1)
        w = top_scores.reshape(-1)
        xr = x[tok]
        h = jax.nn.silu(jnp.einsum('nd,edf->enf', xr, Wg)) * jnp.einsum('nd,edf->enf', xr, Wu)
        out_all = jnp.einsum('enf,efd->end', h, Wd)
        routed = out_all[exp, jnp.arange(exp.shape[0])]
        routed = (routed.astype(jnp.float32) * w[:, None]).astype(hidden_states.dtype)
        out = shared.at[tok].add(routed)
        return out.reshape(b, s, d)

    def _L1_xattn_ref(decoder_input, encoder_output, W_q, W_k, W_v, W_o, b_o):
        import jax, jax.numpy as jnp
        import numpy as np
        EMBED = 256
        HEADS = 16
        HEAD_DIM = EMBED // HEADS
        B, Sd, E = decoder_input.shape
        Se = encoder_output.shape[1]
        Q = (decoder_input @ W_q).reshape(B, Sd, HEADS, HEAD_DIM)
        K = (encoder_output @ W_k).reshape(B, Se, HEADS, HEAD_DIM)
        V = (encoder_output @ W_v).reshape(B, Se, HEADS, HEAD_DIM)
        scores = jnp.einsum('bqhd,bkhd->bhqk', Q, K) / jnp.sqrt(jnp.float32(HEAD_DIM))
        attn = jax.nn.softmax(scores, axis=-1)
        out = jnp.einsum('bhqk,bkhd->bqhd', attn, V).reshape(B, Sd, E)
        return out @ W_o + b_o

    def _L1_ffn_ref(hidden_states, gate_W, gate_b, wi_W, wi_b, wo_W, wo_b, lora_A, lora_B):
        import jax, jax.numpy as jnp
        import numpy as np
        B, S, D, F, E, R = (4, 512, 256, 1024, 8, 4)
        x = hidden_states
        logits = jnp.einsum('bsd,ed->bse', x, gate_W) + gate_b
        top1 = jnp.argmax(jax.nn.softmax(logits, axis=-1), axis=-1)
        base = jnp.einsum('bsd,fd->bsf', x, wi_W) + wi_b
        out = jnp.zeros_like(x)
        for i in range(lora_A.shape[0]):
            lora = jnp.einsum('bsr,fr->bsf', jnp.einsum('bsd,rd->bsr', x, lora_A[i]), lora_B[i])
            inter = jax.nn.relu(base + lora)
            expert_out = jnp.einsum('bsf,df->bsd', inter, wo_W) + wo_b
            mask = (top1 == i).astype(x.dtype)[..., None]
            out = out + mask * expert_out
        return out
    x = x + jnp.tanh(g_xattn[0]) * _L0_xattn_ref(_layernorm(x, axis=-1), ctx_1024, ctx_1024, mask_Bx1xSxS2_bk1, L0_xattn_Wq, L0_xattn_bq, L0_xattn_Wk, L0_xattn_bk, L0_xattn_Wv, L0_xattn_bv, L0_xattn_Wo, L0_xattn_bo)
    x = x + jnp.tanh(g_ffn[0]) * _L0_ffn_ref(_layernorm(x, axis=-1), L0_ffn_W_gate_router, L0_ffn_expert_bias, L0_ffn_Wg, L0_ffn_Wu, L0_ffn_Wd, L0_ffn_Wg_s, L0_ffn_Wu_s, L0_ffn_Wd_s)
    x = x + jnp.tanh(g_xattn[1]) * _L1_xattn_ref(_layernorm(x, axis=-1), ctx_1024, L1_xattn_W_q, L1_xattn_W_k, L1_xattn_W_v, L1_xattn_W_o, L1_xattn_b_o)
    x = x + jnp.tanh(g_ffn[1]) * _L1_ffn_ref(_layernorm(x, axis=-1), L1_ffn_gate_W, L1_ffn_gate_b, L1_ffn_wi_W, L1_ffn_wi_b, L1_ffn_wo_W, L1_ffn_wo_b, L1_ffn_lora_A, L1_ffn_lora_B)
    return x

_drawn_inputs = setup_inputs


def setup_inputs(seed=0):
    import zlib

    import numpy as np

    out = dict(_drawn_inputs(seed))
    spreads = {'g_ffn': (-1.0, 0.6),
     'L0_xattn_bq': (0.0, 0.447),
     'L0_xattn_bk': (0.0, 2.0),
     'L0_xattn_bv': (0.0, 0.1),
     'L0_xattn_bo': (0.0, 0.1),
     'L0_ffn_expert_bias': (0.0, 0.8),
     'L1_ffn_gate_b': (0.0, 2.0),
     'L1_ffn_wi_b': (0.0, 0.8),
     'L1_ffn_wo_b': (0.0, 0.642)}
    factors = {'L0_ffn_W_gate_router': 8.0,
     'L0_ffn_Wg': 8.0,
     'L0_ffn_Wu': 8.0,
     'L0_ffn_Wd': 8.0,
     'L0_ffn_Wg_s': 6.019,
     'L0_ffn_Wu_s': 5.87,
     'L0_ffn_Wd_s': 5.852,
     'L1_xattn_b_o': 36.888,
     'L1_ffn_gate_W': 3.39,
     'L1_ffn_lora_A': 3.267,
     'L1_ffn_lora_B': 3.246}
    for name, (base, spread) in spreads.items():
        noise = np.random.default_rng([zlib.crc32(name.encode()), seed]).standard_normal(out[name].shape)
        drawn = base * np.exp(spread * noise) if base else spread * noise
        out[name] = jnp.asarray(drawn.astype(out[name].dtype))
    for name, factor in factors.items():
        out[name] = (out[name] * factor).astype(out[name].dtype)
    return out
```

```python
import concourse.bass as bass
from concourse import mybir
from contextlib import ExitStack

F32 = mybir.dt.float32
BF16 = mybir.dt.bfloat16
U8 = mybir.dt.uint8
U32 = mybir.dt.uint32
ALU = mybir.AluOpType
ACT = mybir.ActivationFunctionType
AX = mybir.AxisListType

B, S, S2, D, H = 16, 100, 361, 256, 16
HD = D // H
P = 128
KT = D // P
HH = H // KT
GB = 4
NG = B // GB
GT = GB * S
NKT = -(-S2 // P)
KROWS = [min(P, S2 - t * P) for t in range(NKT)]
HQ = 4
NHG = H // HQ
E, F = 8, 192
FTOT = F + E * F
NFT0 = -(-F // P) + E * F // P
E1, R1, F1 = 8, 4, 1024
NFT1 = F1 // P
EPS = 1e-5
ROUTE_EPS = 1e-20
MASKED = -1e15
SCALE = float(HD) ** -0.5

KPART = [0, 0, 0, 1, 1, 2]
QPART = [0, 1, 2, 0, 1, 0]
NST = len(KPART)
SROWS = NST * HD
MROWS = 2
KSROWS = SROWS + MROWS


def build(nc, io, out):
    ctx = ExitStack()
    with ctx:
        def sb(name, shape, dt=F32):
            return ctx.enter_context(nc.sbuf_tensor(name, shape, dt))

        def sem(name):
            return ctx.enter_context(nc.semaphore(name))

        def dram(name, shape, dt):
            return nc.dram_tensor(name, shape, dt, kind="Internal").ap()

        ps = ctx.enter_context(nc.psum_tensor("ps", [P, 8, 512], F32))
        x_sb = sb("x_sb", [S, B, D])
        ident = sb("ident", [P, P])
        iota8 = sb("iota8", [S, E])
        w_attn = [{n: sb(f"w{n}{l}", [P, KT, D]) for n in "qkvo"} for l in range(2)]
        bq4 = [sb(f"bq4_{l}", [P, KT]) for l in range(2)]
        bk = [sb(f"bk_{l}", [P, KT]) for l in range(2)]
        bv_b = sb("bv_b", [S, D])
        bo_b = [sb(f"bo_b{l}", [S, D]) for l in range(2)]
        gates = sb("gates", [P, 4])
        stat = sb("stat", [S, GB, 6])
        mean_var = sb("mean_var", [S, GB, 2])
        var_eps = sb("var_eps", [S, GB])
        rstd = sb("rstd", [S, GB])
        neg_half = sb("neg_half", [S, GB])
        xn = sb("xn", [S, GB, D])
        xT = sb("xT", [P, KT, GT])
        xT_all = sb("xT_all", [P, KT, B * S])

        scr_q = dram("scr_q", [B, 3, KT, P, S], BF16)
        scr_k = dram("scr_k", [2, 3, KT, P, S2], BF16)
        scr_w = dram("scr_w", [E, B * S], F32)

        s_const = sem("const_loaded")
        s_x = [sem(f"x_loaded{g}") for g in range(NG)]
        s_wa = [sem(f"attn_weights{l}") for l in range(2)]
        s_wf = [sem(f"ffn_weights{l}") for l in range(2)]
        s_setup = sem("setup_vec")
        s_gates = sem("gates_ready")
        NORMS = ["q0", "f0", "q1", "f1"]
        sn = {p: {n: sem(f"{p}_{n}") for n in ("stat", "mv", "veps", "rstd", "xn", "xnT", "xT")} for p in NORMS}
        sq = [{n: sem(f"q{l}_{n}") for n in ("ready", "f32", "split", "stored")} for l in range(2)]
        AN = ("k_ready", "k1", "k_rest1", "k2", "k3", "v_ready", "v_copied", "bias", "biasT", "s_ready", "max",
              "mT", "msplit", "sT", "exp", "pv", "o_copied", "oT", "rec", "on", "onv", "onT", "onT_copied", "wo",
              "addb", "x")
        sa = [{n: sem(f"a{l}_{n}") for n in AN} for l in range(2)]
        AD = ("ctx", "kst", "kload", "qload", "mload")
        sd = [{n: [sem(f"a{l}_{n}{p}") for p in range(2)] for n in AD} for l in range(2)]
        s0 = {n: sem(f"f0_{n}") for n in ("logit", "sc", "rt", "wT", "wT_copied", "w_stored", "w_bc", "g", "u", "silu",
                                          "gu", "h", "y", "y_copied", "yT", "x")}
        s1 = {n: sem(f"f1_{n}") for n in ("logit", "rt", "rT", "rT_copied", "h_ready", "h", "y", "y_copied", "yT", "x")}
        s_out = sem("out_stored")

        def asb(name, shape, dt=F32):
            return ctx.enter_context(nc.sbuf_tensor(name, shape, dt))

        cT = [asb(f"cT{p}", [P, KT, S2]) for p in range(2)]
        kp = asb("kp", [P, 3, KT, S2], BF16)
        kr = asb("kr", [P, KT, S2])
        KS = [asb(f"KS{p}", [KSROWS, H * S2 + NKT * P - S2], BF16) for p in range(2)]
        QS = [asb(f"QS{p}", [KSROWS, H, S], BF16) for p in range(2)]
        qf = asb("qf", [P, KT, GT])
        qr = asb("qr", [P, KT, GT])
        qp = asb("qp", [P, 3, KT, GT], BF16)
        V1 = [asb(f"V1_{p}", [P, NKT, H, HD + 1]) for p in range(2)]
        prob = asb("prob", [P, NKT, NHG, HQ * S])[:, :, :, :]
        mx = asb("mx", [S, H])
        mp = asb("mp", [H, MROWS, S], BF16)
        masku = [asb(f"masku{p}", [S, S2], U8) for p in range(2)]
        maskTu = [asb(f"maskTu{p}", [P, NKT, S], U8) for p in range(2)]
        biasq = [asb(f"biasq{p}", [S, S2], BF16) for p in range(2)]
        biasT = [asb(f"biasT{p}", [P, NKT, S], BF16) for p in range(2)]
        ident_bf = asb("ident_bf", [P, P], BF16)
        oT_sb = asb("oT_sb", [P, HQ * S])
        rec = asb("rec", [S, H])
        on = asb("on", [S, D])
        onv = asb("onv", [S, D])
        onT = asb("onT", [P, KT, S])
        xb = asb("xb", [S, D])

        Wr = asb("Wr", [P, KT, E])
        ebias = asb("ebias", [S, E])
        Wg = asb("Wg", [P, KT, FTOT])
        Wu = asb("Wu", [P, KT, FTOT])
        Wd = asb("Wd", [P, NFT0, D])
        wbc = prob.rearrange("p t g n -> p (t g n)")[:, 0:E * GT].rearrange("p (e n) -> p e n", e=E)
        sc = asb("sc", [S, GB, E])
        bsc = asb("bsc", [S, GB, E])
        mx8 = asb("mx8", [S, GB, 8])
        ix8 = asb("ix8", [S, GB, 8], U32)
        ixf = asb("ixf", [S, GB, 2])
        oh = asb("oh", [S, 2, GB, E])
        wsel = asb("wsel", [S, GB, E])
        wsum = asb("wsum", [S, GB])
        wrec = asb("wrec", [S, GB])
        wtok = asb("wtok", [S, GB, E])
        wT = asb("wT", [E, GT])
        sg = [asb(f"sg{p}", [P, GT]) for p in range(2)]
        gu = [qr[:, p, :] for p in range(2)]
        hh = [qf[:, p, :] for p in range(2)]
        yT = asb("yT", [P, KT, GT])
        GA = E1 + E1 * R1
        WgA = asb("WgA", [P, KT, GA])
        gb_b = asb("gb_b", [S, E1])
        wiT = Wg[:, :, 0:F1]
        wib = asb("wib", [P, NFT1])
        woT = Wu[:, :, :].rearrange("p k f -> p (k f)")[:, 0:NFT1 * D].rearrange("p (t n) -> p t n", t=NFT1)
        wob = asb("wob", [P, KT])
        BT = asb("BT", [E1 * R1, F1])
        rm = asb("rm", [S, GB, E1 * R1])
        rT_all = asb("rT_all", [E1 * R1, B * S])

        def bc(ap, shape):
            return ap.to_broadcast(shape)

        def keys(n):
            return KROWS[n]

        def tile_rows0(i):
            return F - P if i == 1 else P

        def scaled(i):
            return sum(1 + (t * P // F != (t * P + P - 1) // F) for t in range(i - 1))

        def tile_col0(i):
            return i * P if i < 2 else F + (i - 2) * P

        NCONST = 16 * 12
        NSETUP = 8

        ROUT = 13
        s_held = sem("held_waits")

        def hold(eng, semaphore, value):
            eng.wait_ge(semaphore, value)
            eng.sem_inc(s_held, 1)

        block = ctx.enter_context(nc.Block())

        @block.sync
        def _(sp):
            for g in range(NG):
                sp.dma_start(x_sb[:, g * GB:(g + 1) * GB, :],
                             io["x"][g * GB:(g + 1) * GB].rearrange("b s d -> s b d")).then_inc(s_x[g], 16)

            def ctx_load(l, n, p, idx):
                a, d = sa[l], sd[l]
                if idx is not None:
                    sp.wait_ge(a["v_ready"], 2 * (n - 1))
                    if l == 0:
                        sp.wait_ge(a["biasT"], 2 * (n - 1))
                sp.dma_start(cT[p][:, :, :], io["ctxT"][n].rearrange("(k p) n -> p k n", p=P)).then_inc(d["ctx"][p], 16)
                if l == 0:
                    sp.dma_start(masku[p][:, :], io["mask"][n]).then_inc(d["ctx"][p], 16)
                    sp.dma_start(maskTu[p][:, 0:2, :],
                                 io["maskT"][n, 0:2 * P].rearrange("(t p) q -> p t q", p=P)).then_inc(d["ctx"][p], 16)
                    sp.dma_start(maskTu[p][0:KROWS[2], 2, :], io["maskT"][n, 2 * P:S2]).then_inc(d["ctx"][p], 16)

            def k_store(l, n, p, idx):
                a, d = sa[l], sd[l]
                hold(sp, a["k3"], n + 1)
                if idx is not None:
                    hold(sp, d["kload"][p], 16 * NST * idx)
                sp.dma_start(scr_k[p].rearrange("a k p n -> p a k n"), kp[:, :, :, :]).then_inc(d["kst"][p], 16)

            def stacks_load(l, n, p, idx):
                a, d = sa[l], sd[l]
                hold(sp, d["kst"][p], 16 * (1 if idx is None else idx + 1))
                if idx is not None:
                    sp.wait_ge(a["sT"], 3 * NHG * (n - 1))
                for j in range(NST):
                    sp.dma_start(KS[p][j * HD:(j + 1) * HD, 0:H * S2].rearrange("d (k n) -> d k n", k=KT),
                                 scr_k[p, KPART[j]].rearrange("k (d h) n -> d k (h n)", h=HH)).then_inc(d["kload"][p], 16)
                for j in range(NST):
                    sp.dma_start(QS[p][j * HD:(j + 1) * HD, :, :].rearrange("d (k h) n -> d k (h n)", k=KT),
                                 scr_q[n, QPART[j]].rearrange("k (d h) n -> d k (h n)", h=HH)).then_inc(d["qload"][p], 16)

            def max_load(l, n, p):
                a, d = sa[l], sd[l]
                sp.wait_ge(a["msplit"], MROWS * (n + 1))
                for j in range(MROWS):
                    sp.dma_start(QS[p][SROWS + j:SROWS + j + 1, :, :], mp[:, j, :]).then_inc(d["mload"][p], 16)

            def q_store(l):
                with sp.Fori(0, NG) as g:
                    sp.wait_ge(sq[l]["split"], 4 * (g + 1))
                    for part in range(3):
                        for k in range(KT):
                            sp.dma_start(scr_q[bass.ds(g * GB, GB), part, k].rearrange("b p n -> p b n"),
                                         qp[:, part, k, :].rearrange("p (b n) -> p b n", b=GB)).then_inc(sq[l]["stored"], 16)

            def attn(l):
                a = sa[l]
                if l == 1:
                    sp.wait_ge(sa[0]["x"], B)
                ctx_load(l, 0, 0, None)
                ctx_load(l, 1, 1, None)
                q_store(l)
                sp.wait_ge(sq[l]["stored"], 16 * 3 * KT * NG)
                k_store(l, 0, 0, None)
                stacks_load(l, 0, 0, None)
                k_store(l, 1, 1, None)
                stacks_load(l, 1, 1, None)
                max_load(l, 0, 0)
                with sp.Fori(0, B // 2 - 1) as i:
                    for u in range(2):
                        b = 2 * i + u
                        ctx_load(l, b + 2, u, i + 1)
                        k_store(l, b + 2, u, i + 1)
                        stacks_load(l, b + 2, u, i + 1)
                        max_load(l, b + 1, 1 - u)
                max_load(l, B - 1, 1)

            attn(0)
            with sp.Fori(0, NG) as g:
                sp.wait_ge(s0["wT_copied"], g + 1)
                sp.dma_start(scr_w[:, bass.ds(g * GT, GT)], wT[:, :]).then_inc(s0["w_stored"], 16)
            sp.wait_ge(s0["w_stored"], 16 * NG)
            with sp.Fori(0, NG) as g:
                sp.wait_ge(s0["h"], scaled(NFT0 - 1) * g)
                sp.dma_start(wbc[:, :, :], scr_w[:, bass.ds(g * GT, GT)].partition_broadcast(P)).then_inc(s0["w_bc"], 16)
            attn(1)
            with sp.Fori(0, NG) as g:
                sp.wait_ge(s1["x"], GB * (g + 1))
                sp.dma_start(out[bass.ds(g * GB, GB)].rearrange("b s d -> s b d"),
                             x_sb[:, bass.ds(g * GB, GB), :]).then_inc(s_out, 16)
            sp.wait_ge(s_out, 16 * NG)

        @block.gpsimd
        def _(pool):
            nc.gpsimd.memset(neg_half[:, :], -0.5).then_inc(s_setup, 1)

            def norm(p):
                with pool.Fori(0, NG) as g:
                    hold(pool, sn[p]["mv"], GB * (g + 1))
                    nc.gpsimd.tensor_scalar(var_eps[:, :], mean_var[:, :, 1], EPS, None, ALU.add).then_inc(sn[p]["veps"], 1)
                    pool.wait_ge(sn[p]["veps"], g + 1)
                    if p == "q0":
                        pool.wait_ge(s_setup, NSETUP)
                    pool.wait_ge(sn[p]["xn"], GB * g)
                    nc.gpsimd.tensor_tensor(rstd[:, :], var_eps[:, :], neg_half[:, :], ALU.pow).then_inc(sn[p]["rstd"], 1)

            def bias(n, p, idx):
                a, d = sa[0], sd[0]
                hold(pool, d["ctx"][p], 64 * (1 if idx is None else idx + 1))
                if idx is not None:
                    hold(pool, a["max"], H * (n - 1))
                nc.gpsimd.tensor_scalar(biasq[p][:, :], masku[p][:, :], MASKED, None, ALU.mult).then_inc(a["bias"], 1)

            def biasT_(n, p, idx):
                a, d = sa[0], sd[0]
                if idx is not None:
                    hold(pool, a["sT"], 3 * NHG * (n - 1))
                nc.gpsimd.tensor_scalar(biasT[p][:, 0:2, :], maskTu[p][:, 0:2, :], MASKED, None,
                                        ALU.mult).then_inc(a["biasT"], 1)
                nc.gpsimd.tensor_scalar(biasT[p][0:KROWS[2], 2, :], maskTu[p][0:KROWS[2], 2, :], MASKED, None,
                                        ALU.mult).then_inc(a["biasT"], 1)

            def k3(l, n):
                a = sa[l]
                pool.wait_ge(a["k2"], n + 1)
                nc.gpsimd.tensor_tensor(kp[:, 2, :, :], kr[:, :, :], kp[:, 1, :, :], ALU.subtract).then_inc(a["k3"], 1)

            def attn(l):
                norm(NORMS[2 * l])
                for n in range(2):
                    if l == 0:
                        bias(n, n, None)
                    k3(l, n)
                    if l == 0:
                        biasT_(n, n, None)
                with pool.Fori(0, B // 2 - 1) as i:
                    for u in range(2):
                        n = 2 * i + u + 2
                        if l == 0:
                            bias(n, u, i + 1)
                        k3(l, n)
                        if l == 0:
                            biasT_(n, u, i + 1)

            attn(0)
            pool.wait_ge(sa[0]["x"], B)
            norm("f0")
            with pool.Fori(0, NG) as g:
                pool.wait_ge(s0["w_bc"], 16 * (g + 1))
                for i in range(2, NFT0):
                    pool.wait_ge(s0["gu"], NFT0 * g + i + 1)
                    pool.wait_ge(s0["y"], NFT0 * g + i - 1)
                    e = (i - 2) * P // F
                    own = scaled(NFT0 - 1) * g + scaled(i - 1)
                    if i > 2:
                        pool.wait_ge(s0["h"], own)
                    if ((i - 2) * P + P - 1) // F == e:
                        nc.gpsimd.tensor_tensor(hh[i % 2][:, :], gu[i % 2][:, :], wbc[:, e, :], ALU.mult).then_inc(s0["h"], 1)
                    else:
                        half = F * (e + 1) - (i - 2) * P
                        nc.gpsimd.tensor_tensor(hh[i % 2][0:half, :], gu[i % 2][0:half, :], wbc[0:half, e, :],
                                                ALU.mult).then_inc(s0["h"], 1)
                        pool.wait_ge(s0["h"], own + 1)
                        nc.gpsimd.tensor_tensor(hh[i % 2][half:P, :], gu[i % 2][half:P, :], wbc[half:P, e + 1, :],
                                                ALU.mult).then_inc(s0["h"], 1)
            pool.wait_ge(s0["x"], B)
            attn(1)
            pool.wait_ge(sa[1]["x"], B)
            norm("f1")

        @block.scalar
        def _(act):
            act.dma_start(ident[:, :], io["ident"]).then_inc(s_const, 16)
            act.dma_start(w_attn[0]["k"][:, :, :], io["L0_xattn_Wk"].rearrange("(k p) n -> p k n", p=P)).then_inc(s_wa[0], 16)
            act.dma_start(w_attn[0]["q"][:, :, :], io["L0_xattn_Wq"].rearrange("(k p) n -> p k n", p=P)).then_inc(s_wa[0], 16)
            act.dma_start(bq4[0][:, :], io["L0_xattn_bq"]).then_inc(s_const, 16)
            act.dma_start(bk[0][:, :], io["L0_xattn_bk"]).then_inc(s_const, 16)
            act.dma_start(w_attn[0]["v"][:, :, :], io["L0_xattn_Wv"].rearrange("(k p) n -> p k n", p=P)).then_inc(s_wa[0], 16)
            act.dma_start(w_attn[0]["o"][:, :, :], io["L0_xattn_Wo"].rearrange("(k p) n -> p k n", p=P)).then_inc(s_wa[0], 16)
            act.dma_start(bv_b[:, :], io["L0_xattn_bv"].partition_broadcast(S)).then_inc(s_const, 16)
            act.dma_start(bo_b[0][:, :], io["L0_xattn_bo"].partition_broadcast(S)).then_inc(s_const, 16)
            act.dma_start(bo_b[1][:, :], io["L1_xattn_b_o"].partition_broadcast(S)).then_inc(s_const, 16)
            act.dma_start(gates[:, 0:2], io["g_xattn"].partition_broadcast(P)).then_inc(s_const, 16)
            act.dma_start(gates[:, 2:4], io["g_ffn"].partition_broadcast(P)).then_inc(s_const, 16)
            act.dma_start(iota8[:, :], io["iota8"].partition_broadcast(S)).then_inc(s_const, 16)
            act.dma_start(ebias[:, :], io["L0_ffn_expert_bias"].partition_broadcast(S)).then_inc(s_const, 16)
            act.dma_start(gb_b[:, :], io["L1_ffn_gate_b"].partition_broadcast(S)).then_inc(s_const, 16)
            act.dma_start(wob[:, :], io["L1_ffn_wo_b"]).then_inc(s_const, 16)
            act.dma_start(Wr[:, :, :], io["L0_ffn_W_gate_router"].rearrange("(k p) e -> p k e", p=P)).then_inc(s_wf[0], 16)
            for w, sh, ro in ((Wg, "L0_ffn_Wg_s", "L0_ffn_Wg"), (Wu, "L0_ffn_Wu_s", "L0_ffn_Wu")):
                act.dma_start(w[:, :, 0:F], io[sh].rearrange("(k p) f -> p k f", p=P)).then_inc(s_wf[0], 16)
                for k in range(KT):
                    act.dma_start(w[:, k, F:FTOT].rearrange("p (e f) -> p e f", e=E),
                                  io[ro][:, k * P:(k + 1) * P].rearrange("e p f -> p e f")).then_inc(s_wf[0], 16)
            act.dma_start(Wd[:, 0, :], io["L0_ffn_Wd_s"][0:P]).then_inc(s_wf[0], 16)
            act.dma_start(Wd[0:F - P, 1, :], io["L0_ffn_Wd_s"][P:F]).then_inc(s_wf[0], 16)
            act.dma_start(Wd[:, 2:, :], io["L0_ffn_Wd"].rearrange("e f d -> (e f) d").rearrange("(t p) d -> p t d", p=P)).then_inc(s_wf[0], 16)
            for n, key in (("k", "W_k"), ("q", "W_q"), ("v", "W_v"), ("o", "W_o")):
                act.dma_start(w_attn[1][n][:, :, :], io[f"L1_xattn_{key}"].rearrange("(k p) n -> p k n", p=P)).then_inc(s_wa[1], 16)
            act.dma_start(WgA[:, :, 0:E1], io["gateT"].rearrange("(k p) n -> p k n", p=P)).then_inc(s_wf[1], 16)
            act.dma_start(WgA[:, :, E1:GA], io["loraAT"].rearrange("(k p) n -> p k n", p=P)).then_inc(s_wf[1], 16)
            act.dma_start(wib[:, :], io["L1_ffn_wi_b"]).then_inc(s_wf[1], 16)
            act.dma_start(BT[:, :], io["loraBT"]).then_inc(s_wf[1], 16)
            act.wait_ge(s_const, NCONST)
            nc.scalar.activation(gates[:, :], gates[:, :], ACT.Tanh).then_inc(s_gates, 1)
            nc.scalar.activation(bq4[0][:, :], bq4[0][:, :], ACT.Copy, scale=SCALE).then_inc(s_gates, 1)
            nc.scalar.activation(ident_bf[:, :], ident[:, :], ACT.Copy).then_inc(s_gates, 1)
            act.wait_ge(s_setup, NSETUP)
            act.wait_ge(s_gates, 3)

            def norm(p, keep_all):
                with act.Fori(0, NG) as g:
                    for k in range(KT):
                        act.wait_ge(sn[p]["xnT"], KT * g + k + 1)
                        if keep_all:
                            nc.scalar.activation(xT_all[:, k, bass.ds(g * GT, GT)], ps[:, k, 0:GT], ACT.Copy)
                        nc.scalar.activation(xT[:, k, :], ps[:, k, 0:GT], ACT.Copy).then_inc(sn[p]["xT"], 1)
                    if p == "f0":
                        act.wait_ge(s0["logit"], GB * (g + 1))
                        act.wait_ge(s0["rt"], ROUT * g)
                        nc.scalar.activation(sc[:, :, :], ps[0:S, 4, 0:GB * E], ACT.Sigmoid).then_inc(s0["sc"], 1)
                        act.wait_ge(s0["wT"], GB * (g + 1))
                        act.wait_ge(s0["w_stored"], 16 * g)
                        nc.scalar.activation(wT[:, :], ps[0:E, 5, 0:GT], ACT.Copy).then_inc(s0["wT_copied"], 1)
                    if p == "f1":
                        act.wait_ge(s1["rT"], GB * (g + 1))
                        nc.scalar.activation(rT_all[:, bass.ds(g * GT, GT)], ps[0:E1 * R1, 5, 0:GT], ACT.Copy).then_inc(s1["rT_copied"], 1)
                    if p[0] == "q":
                        l = int(p[1])
                        for k in range(KT):
                            act.wait_ge(sq[l]["ready"], KT * g + k + 1)
                            act.wait_ge(sq[l]["split"], 4 * g)
                            nc.scalar.activation(qf[:, k, :], ps[:, 2 + k, 0:GT], ACT.Identity, scale=SCALE,
                                                 bias=bq4[l][:, k:k + 1]).then_inc(sq[l]["f32"], 1)

            def k_parts(l, n, p, idx):
                a, d = sa[l], sd[l]
                if idx is not None:
                    act.wait_ge(d["kst"][1 - p], 16 * (idx + (1 if p == 1 else 0)))
                elif n == 1:
                    act.wait_ge(d["kst"][0], 16)
                for k in range(KT):
                    act.wait_ge(a["k_ready"], KT * n + k + 1)
                    nc.scalar.activation(kp[:, 0, k, :], ps[:, 4 + k, 0:S2], ACT.Identity,
                                         bias=bk[l][:, k:k + 1]).then_inc(a["k1"], 1)

            def k_second(l, n):
                a = sa[l]
                act.wait_ge(a["k_rest1"], KT * (n + 1))
                nc.scalar.activation(kp[:, 1, :, :], kr[:, :, :], ACT.Copy).then_inc(a["k2"], 1)

            def v_copy(l, n, p):
                a = sa[l]
                act.wait_ge(a["v_ready"], 2 * n + 1)
                nc.scalar.activation(V1[p][:, 0:2, :, 0:HD],
                                     ps[:, 4, :].rearrange("p (t h e) -> p t h e", t=2, h=H), ACT.Copy).then_inc(a["v_copied"], 1)
                act.wait_ge(a["v_ready"], 2 * n + 2)
                nc.scalar.activation(V1[p][0:KROWS[2], 2, :, 0:HD],
                                     ps[0:KROWS[2], 5, 0:D].rearrange("p (h e) -> p h e", h=H), ACT.Copy).then_inc(a["v_copied"], 1)

            def step(l, b, u, i, has_a):
                a = sa[l]
                if has_a:
                    k_parts(l, b + 2, u, i + 1)
                for hg in range(NHG):
                    act.wait_ge(a["pv"], NHG * b + hg + 1)
                    for t in range(NKT):
                        c = hg * NKT + t
                        act.wait_ge(a["sT"], NKT * NHG * b + c + 1)
                        nc.scalar.activation(prob[0:KROWS[t], t, hg, :], ps[0:KROWS[t], c % 2, 0:HQ * S],
                                             ACT.Exp).then_inc(a["exp"], 1)
                    if hg == 0 and has_a:
                        k_second(l, b + 2)
                act.wait_ge(a["pv"], NHG * b + 2 * NHG)
                nc.scalar.activation(oT_sb[:, :], ps[:, 6, 0:HQ * S], ACT.Copy).then_inc(a["o_copied"], 1)
                if has_a:
                    v_copy(l, b + 2, u)
                act.wait_ge(a["onT"], b + 1)
                nc.scalar.activation(onT[:, :, :], ps[:, 7, 0:KT * S], ACT.Copy).then_inc(a["onT_copied"], 1)

            def attn(l):
                norm(NORMS[2 * l], False)
                for n in range(2):
                    k_parts(l, n, n, None)
                    k_second(l, n)
                    v_copy(l, n, n)
                with act.Fori(0, B // 2 - 1) as i:
                    for u in range(2):
                        step(l, 2 * i + u, u, i, True)
                for b in (B - 2, B - 1):
                    step(l, b, b % 2, b // 2, False)

            attn(0)
            act.wait_ge(sa[0]["x"], B)
            norm("f0", True)
            with act.Fori(0, NG) as g:
                for i in range(NFT0):
                    rows = tile_rows0(i)
                    act.wait_ge(s0["g"], NFT0 * g + i + 1)
                    act.wait_ge(s0["gu"], NFT0 * g + max(i - 1, 0))
                    nc.scalar.activation(sg[i % 2][0:rows, :], ps[0:rows, i % 2, 0:GT], ACT.Silu).then_inc(s0["silu"], 1)
                act.wait_ge(s0["y"], NFT0 * (g + 1))
                for k in range(KT):
                    nc.scalar.activation(yT[:, k, :], ps[:, 4 + k, 0:GT], ACT.Copy).then_inc(s0["y_copied"], 1)
            act.wait_ge(s0["x"], B)
            act.dma_start(wiT[:, :, :], io["wiT"].rearrange("(k p) n -> p k n", p=P)).then_inc(s_wf[1], 16)
            act.dma_start(woT[:, :, :], io["woT"].rearrange("(t p) n -> p t n", p=P)).then_inc(s_wf[1], 16)
            attn(1)
            act.wait_ge(sa[1]["x"], B)
            norm("f1", True)
            with act.Fori(0, NG) as g:
                for i in range(NFT1):
                    act.wait_ge(s1["h_ready"], NFT1 * g + i + 1)
                    act.wait_ge(s1["y"], NFT1 * g + i + 1)
                    nc.scalar.activation(hh[i % 2][:, :], ps[:, i % 2, 0:GT], ACT.Relu, bias=wib[:, i:i + 1]).then_inc(s1["h"], 1)
                act.wait_ge(s1["y"], NFT1 * (g + 1) + 2)
                for k in range(KT):
                    nc.scalar.activation(yT[:, k, :], ps[:, 4 + k, 0:GT], ACT.Identity,
                                         bias=wob[:, k:k + 1]).then_inc(s1["y_copied"], 1)

        @block.vector
        def _(dve):
            for p in range(2):
                nc.vector.memset(KS[p][:, :], 1.0).then_inc(s_setup, 1)
                nc.vector.memset(V1[p][:, :, :, :], 1.0).then_inc(s_setup, 1)
            nc.vector.memset(bq4[1][:, :], 0.0).then_inc(s_setup, 1)
            nc.vector.memset(bk[1][:, :], 0.0).then_inc(s_setup, 1)
            nc.vector.memset(ps[:, 6, :], 0.0).then_inc(s_setup, 1)

            def norm(p):
                n = sn[p]
                with dve.Fori(0, NG) as g:
                    for t in range(GB):
                        nc.vector.bn_stats(stat[:, t, :], x_sb[:, g * GB + t, :]).then_inc(n["stat"], 1)
                    hold(dve, n["veps"], g)
                    for t in range(GB):
                        hold(dve, n["stat"], GB * g + t + 1)
                        nc.vector.bn_aggr(mean_var[:, t, :], stat[:, t, :]).then_inc(n["mv"], 1)
                    dve.wait_ge(n["rstd"], g + 1)
                    dve.wait_ge(n["xnT"], KT * g)
                    for t in range(GB):
                        nc.vector.tensor_scalar(xn[:, t, :], x_sb[:, g * GB + t, :], mean_var[:, t, 0:1], rstd[:, t:t + 1],
                                                ALU.subtract, ALU.mult).then_inc(n["xn"], 1)
                    if p[0] == "q":
                        split_q(int(p[1]), g)
                    if p == "f0":
                        route(g)
                    if p == "f1":
                        choose(g)

            def split_q(l, g):
                q = sq[l]
                dve.wait_ge(q["f32"], KT * (g + 1))
                dve.wait_ge(q["stored"], 16 * 3 * KT * g)
                nc.vector.tensor_copy(qp[:, 0, :, :], qf[:, :, :]).then_inc(q["split"], 1)
                dve.wait_ge(q["split"], 4 * g + 1)
                nc.vector.tensor_tensor(qr[:, :, :], qf[:, :, :], qp[:, 0, :, :], ALU.subtract).then_inc(q["split"], 1)
                dve.wait_ge(q["split"], 4 * g + 2)
                nc.vector.tensor_copy(qp[:, 1, :, :], qr[:, :, :]).then_inc(q["split"], 1)
                dve.wait_ge(q["split"], 4 * g + 3)
                nc.vector.tensor_tensor(qp[:, 2, :, :], qr[:, :, :], qp[:, 1, :, :], ALU.subtract).then_inc(q["split"], 1)

            def route(g):
                r = s0["rt"]
                c = ROUT * g
                sh = [S, GB, E]
                dve.wait_ge(s0["sc"], g + 1)
                nc.vector.tensor_tensor(bsc[:, :, :], sc[:, :, :], bc(ebias[:, :].unsqueeze(1), sh), ALU.add).then_inc(r, 1)
                hold(dve, r, c + 1)
                for t in range(GB):
                    nc.vector.max(mx8[:, t, :], bsc[:, t, :]).then_inc(r, 1) if t == GB - 1 else nc.vector.max(mx8[:, t, :], bsc[:, t, :])
                hold(dve, r, c + 2)
                for t in range(GB):
                    x = nc.vector.max_index(ix8[:, t, :], mx8[:, t, :], bsc[:, t, :])
                x.then_inc(r, 1)
                dve.wait_ge(r, c + 3)
                nc.vector.tensor_copy(ixf[:, :, :], ix8[:, :, 0:2]).then_inc(r, 1)
                dve.wait_ge(r, c + 4)
                for j in range(2):
                    nc.vector.tensor_tensor(oh[:, j, :, :], bc(iota8[:, :].unsqueeze(1), sh), bc(ixf[:, :, j:j + 1], sh),
                                            ALU.is_equal).then_inc(r, 1)
                dve.wait_ge(r, c + 6)
                nc.vector.tensor_tensor(wsel[:, :, :], oh[:, 0, :, :], oh[:, 1, :, :], ALU.add).then_inc(r, 1)
                dve.wait_ge(r, c + 7)
                nc.vector.tensor_tensor(wsel[:, :, :], wsel[:, :, :], sc[:, :, :], ALU.mult).then_inc(r, 1)
                dve.wait_ge(r, c + 8)
                nc.vector.reduce_sum(wsum[:, :], wsel[:, :, :], axis=AX.X).then_inc(r, 1)
                dve.wait_ge(r, c + 9)
                nc.vector.tensor_scalar(wsum[:, :], wsum[:, :], ROUTE_EPS, None, ALU.add).then_inc(r, 1)
                dve.wait_ge(r, c + 10)
                nc.vector.reciprocal(wrec[:, :], wsum[:, :]).then_inc(r, 1)
                dve.wait_ge(r, c + 11)
                dve.wait_ge(s0["wT"], GB * g)
                nc.vector.tensor_tensor(wtok[:, :, :], wsel[:, :, :], bc(wrec[:, :].unsqueeze(2), sh), ALU.mult).then_inc(r, 2)

            def choose(g):
                r = s1["rt"]
                c = 7 * g
                sh = [S, GB, E1]
                lg = ps[0:S, 4, 0:GB * GA].rearrange("s (t n) -> s t n", t=GB)
                dve.wait_ge(s1["logit"], GB * (g + 1))
                nc.vector.tensor_tensor(bsc[:, :, :], lg[:, :, 0:E1], bc(gb_b[:, :].unsqueeze(1), sh), ALU.add).then_inc(r, 1)
                hold(dve, r, c + 1)
                for t in range(GB):
                    x = nc.vector.max(mx8[:, t, :], bsc[:, t, :])
                x.then_inc(r, 1)
                hold(dve, r, c + 2)
                for t in range(GB):
                    x = nc.vector.max_index(ix8[:, t, :], mx8[:, t, :], bsc[:, t, :])
                x.then_inc(r, 1)
                dve.wait_ge(r, c + 3)
                nc.vector.tensor_copy(ixf[:, :, :], ix8[:, :, 0:2]).then_inc(r, 1)
                dve.wait_ge(r, c + 4)
                nc.vector.tensor_tensor(oh[:, 0, :, :], bc(iota8[:, :].unsqueeze(1), sh), bc(ixf[:, :, 0:1], sh),
                                        ALU.is_equal).then_inc(r, 1)
                dve.wait_ge(r, c + 5)
                dve.wait_ge(s1["rT"], GB * g)
                for t in range(GB):
                    x = nc.vector.tensor_tensor(rm[:, t, :].rearrange("s (e r) -> s e r", r=R1),
                                                lg[:, t, E1:GA].rearrange("s (e r) -> s e r", r=R1),
                                                bc(oh[:, 0, t, :].unsqueeze(2), [S, E1, R1]), ALU.mult)
                x.then_inc(r, 2)

            def k_rest(l, n):
                a = sa[l]
                dve.wait_ge(a["k3"], n)
                for k in range(KT):
                    dve.wait_ge(a["k1"], KT * n + k + 1)
                    nc.vector.scalar_tensor_tensor(kr[:, k, :], ps[:, 4 + k, 0:S2], bk[l][:, k:k + 1], kp[:, 0, k, :],
                                                   ALU.add, ALU.subtract).then_inc(a["k_rest1"], 1)

            def maxima(l, n, p):
                a = sa[l]
                if l == 0:
                    dve.wait_ge(a["bias"], n + 1)
                hold(dve, a["mT"], n)
                for h in range(H):
                    hold(dve, a["s_ready"], H * n + h + 1) if l == 0 else dve.wait_ge(a["s_ready"], H * n + h + 1)
                    if l == 0:
                        nc.vector.tensor_tensor_reduce(ps[0:S, 2 + h % 2, 0:S2], ps[0:S, 2 + h % 2, 0:S2], biasq[p][:, :], 1.0, -3.0e38,
                                                       ALU.add, ALU.max, mx[:, h:h + 1]).then_inc(a["max"], 1)
                    else:
                        nc.vector.reduce_max(mx[:, h:h + 1], ps[0:S, 2 + h % 2, 0:S2], axis=AX.X).then_inc(a["max"], 1)

            def split_max(l, n, p, idx):
                a, d = sa[l], sd[l]
                dve.wait_ge(a["mT"], n + 1)
                if idx is not None:
                    dve.wait_ge(d["mload"][1 - p], 16 * MROWS * idx)
                nc.vector.tensor_scalar(mp[:, 0, :], ps[0:H, 7, 0:S], -1.0, None, ALU.mult).then_inc(a["msplit"], 1)
                dve.wait_ge(a["msplit"], MROWS * n + 1)
                nc.vector.scalar_tensor_tensor(mp[:, 1, :], ps[0:H, 7, 0:S], -1.0, mp[:, 0, :],
                                               ALU.mult, ALU.subtract).then_inc(a["msplit"], 1)

            def finish(l, b):
                a = sa[l]
                dve.wait_ge(a["oT"], b + 1)
                o = ps[0:S, 7, :].rearrange("q (h c) -> q h c", c=32)
                nc.vector.reciprocal(rec[:, :], o[:, :, HD]).then_inc(a["rec"], 1)
                dve.wait_ge(a["rec"], b + 1)
                dve.wait_ge(a["onT"], b)
                dst = on if l == 0 else onv
                nc.vector.tensor_tensor(dst[:, :].rearrange("q (h e) -> q h e", h=H), o[:, :, 0:HD],
                                        bc(rec[:, :].unsqueeze(2), [S, H, HD]), ALU.mult).then_inc(a["on"], 1)
                if l == 0:
                    dve.wait_ge(a["on"], b + 1)
                    nc.vector.tensor_tensor(onv[:, :], on[:, :], bv_b[:, :], ALU.add).then_inc(a["onv"], 1)
                dve.wait_ge(a["wo"], b + 1)
                nc.vector.tensor_tensor(xb[:, :], ps[0:S, 7, D:2 * D], bo_b[l][:, :], ALU.add).then_inc(a["addb"], 1)
                dve.wait_ge(a["addb"], b + 1)
                nc.vector.scalar_tensor_tensor(x_sb[:, b, :], xb[:, :], gates[0:S, l:l + 1], x_sb[:, b, :],
                                               ALU.mult, ALU.add).then_inc(a["x"], 1)

            def attn(l):
                norm(NORMS[2 * l])
                for n in range(2):
                    k_rest(l, n)
                maxima(l, 0, 0)
                split_max(l, 0, 0, None)
                with dve.Fori(0, B // 2 - 1) as i:
                    for u in range(2):
                        b = 2 * i + u
                        k_rest(l, b + 2)
                        maxima(l, b + 1, 1 - u)
                        split_max(l, b + 1, 1 - u, i + 1)
                        finish(l, b)
                maxima(l, B - 1, 1)
                split_max(l, B - 1, 1, B // 2)
                finish(l, B - 2)
                finish(l, B - 1)

            dve.wait_ge(s_const, NCONST)
            for g in range(NG):
                dve.wait_ge(s_x[g], 16)
            dve.wait_ge(s_gates, 3)
            attn(0)
            dve.wait_ge(sa[0]["x"], B)
            norm("f0")

            def residual(s, l, g):
                for t in range(GB):
                    dve.wait_ge(s["yT"], KT * g + t // 2 + 1)
                    nc.vector.scalar_tensor_tensor(x_sb[:, g * GB + t, :], ps[0:S, 6 + t // 2, (t % 2) * D:(t % 2 + 1) * D],
                                                   gates[0:S, 2 + l:3 + l], x_sb[:, g * GB + t, :],
                                                   ALU.mult, ALU.add).then_inc(s["x"], 1)

            with dve.Fori(0, NG) as g:
                for i in range(NFT0):
                    rows = tile_rows0(i)
                    dve.wait_ge(s0["silu"], NFT0 * g + i + 1)
                    dve.wait_ge(s0["u"], NFT0 * g + i + 1)
                    if i < 2:
                        dve.wait_ge(s0["y"], NFT0 * g)
                        dst = hh[i % 2]
                    else:
                        dve.wait_ge(s0["h"], scaled(NFT0 - 1) * g + scaled(max(i - 2, 1)))
                        dst = gu[i % 2]
                    nc.vector.tensor_tensor(dst[0:rows, :], ps[0:rows, 2 + i % 2, 0:GT], sg[i % 2][0:rows, :],
                                            ALU.mult).then_inc(s0["gu"], 1)
                residual(s0, 0, g)
            dve.wait_ge(s0["x"], B)
            attn(1)
            dve.wait_ge(sa[1]["x"], B)
            norm("f1")
            with dve.Fori(0, NG) as g:
                residual(s1, 1, g)

        @block.tensor
        def _(pe):
            mm = nc.tensor.matmul

            def norm(p, extra):
                n = sn[p]
                with pe.Fori(0, NG) as g:
                    pe.wait_ge(n["xn"], GB * (g + 1))
                    pe.wait_ge(n["xT"], KT * g)
                    for k in range(KT):
                        for t in range(GB):
                            x = nc.tensor.transpose(ps[:, k, t * S:(t + 1) * S], xn[:, t, k * P:(k + 1) * P], ident[0:S, 0:S])
                        x.then_inc(n["xnT"], 1)
                    pe.wait_ge(n["xT"], KT * (g + 1))
                    extra(g)

            def project_q(l):
                def run(g):
                    pe.wait_ge(sq[l]["f32"], KT * g)
                    for m in range(KT):
                        for k in range(KT):
                            x = mm(ps[:, 2 + m, 0:GT], w_attn[l]["q"][:, k, m * P:(m + 1) * P], xT[:, k, :],
                                   start=k == 0, stop=k == KT - 1)
                        x.then_inc(sq[l]["ready"], 1)
                return run

            def project_k(l, n, p, idx):
                a, d = sa[l], sd[l]
                pe.wait_ge(d["ctx"][p], (64 if l == 0 else 16) * (1 if idx is None else idx + 1))
                if idx is not None or n == 1:
                    pe.wait_ge(a["v_copied"], 2 * n)
                for m in range(KT):
                    for k in range(KT):
                        x = mm(ps[:, 4 + m, 0:S2], w_attn[l]["k"][:, k, m * P:(m + 1) * P], cT[p][:, k, :],
                               start=k == 0, stop=k == KT - 1)
                    x.then_inc(a["k_ready"], 1)

            def project_v(l, n, p):
                a = sa[l]
                pe.wait_ge(a["k_rest1"], KT * (n + 1))
                for t in range(NKT):
                    dst = ps[0:KROWS[t], 4 + t // 2, (t % 2) * D:(t % 2 + 1) * D]
                    for k in range(KT):
                        x = mm(dst, cT[p][:, k, t * P:t * P + KROWS[t]], w_attn[l]["v"][:, k, :],
                               start=k == 0, stop=k == KT - 1)
                    if t > 0:
                        x.then_inc(a["v_ready"], 1)

            def score(l, n, p, h):
                a = sa[l]
                pe.wait_ge(a["max"], H * n + h + 1 - 2) if not (isinstance(n, int) and H * n + h < 2) else None
                mm(ps[0:S, 2 + h % 2, 0:S2], QS[p][0:SROWS, h, :], KS[p][0:SROWS, h * S2:(h + 1) * S2],
                   start=True, stop=True).then_inc(a["s_ready"], 1)

            def turn_max(l, n, b):
                a = sa[l]
                pe.wait_ge(a["max"], H * (n + 1))
                if b is not None:
                    pe.wait_ge(a["msplit"], MROWS * n)
                    pe.wait_ge(a["x"], b)
                nc.tensor.transpose(ps[0:H, 7, 0:S], mx[:, :], ident[0:S, 0:S]).then_inc(a["mT"], 1)

            def score_T(l, b, p, hg, t):
                a = sa[l]
                c = hg * NKT + t
                pe.wait_ge(a["exp"], NKT * NHG * b + c + 1)
                dst = ps[:, c % 2, 0:HQ * S]
                if l == 0:
                    rows = KROWS[t]
                    mm(dst, ident_bf[0:rows, :], bc(biasT[p][0:rows, t, :].unsqueeze(1), [rows, HQ, S]),
                       start=True, stop=False)
                for j in range(HQ):
                    h = HQ * hg + j
                    x = mm(ps[:, c % 2, j * S:(j + 1) * S], KS[p][:, h * S2 + t * P:h * S2 + (t + 1) * P], QS[p][:, h, :],
                           start=l == 1, stop=l == 1 or j == HQ - 1)
                x.then_inc(a["sT"], 1)

            def weigh(l, b, p, hg):
                a = sa[l]
                for t in range(NKT):
                    pe.wait_ge(a["exp"], NKT * NHG * b + hg * NKT + t + 1 + 2)
                    for j in range(HQ):
                        x = mm(ps[32 * j:32 * j + HD + 1, 6, hg * S:(hg + 1) * S], V1[p][0:KROWS[t], t, HQ * hg + j, :],
                               prob[0:KROWS[t], t, hg, j * S:(j + 1) * S], start=t == 0, stop=t == NKT - 1)
                x.then_inc(a["pv"], 1)

            def finish(l, b, last_n):
                a = sa[l]
                pe.wait_ge(a["o_copied"], b + 1)
                pe.wait_ge(a["msplit"], MROWS * (last_n + 1))
                pe.wait_ge(a["x"], b)
                for hg in range(NHG):
                    x = nc.tensor.transpose(ps[0:S, 7, hg * P:(hg + 1) * P], oT_sb[:, hg * S:(hg + 1) * S], ident[:, :])
                x.then_inc(a["oT"], 1)
                pe.wait_ge(a["on"], b + 1)
                if l == 0:
                    pe.wait_ge(a["onv"], b + 1)
                for k in range(KT):
                    x = nc.tensor.transpose(ps[:, 7, k * S:(k + 1) * S], onv[:, k * P:(k + 1) * P], ident[0:S, 0:S])
                x.then_inc(a["onT"], 1)
                pe.wait_ge(a["onT_copied"], b + 1)
                for k in range(KT):
                    x = mm(ps[0:S, 7, D:2 * D], onT[:, k, :], w_attn[l]["o"][:, k, :], start=k == 0, stop=k == KT - 1)
                x.then_inc(a["wo"], 1)

            def stacks(l, n, p, idx):
                d = sd[l]
                v = 16 * NST * (1 if idx is None else idx + 1)
                pe.wait_ge(d["kload"][p], v)
                pe.wait_ge(d["qload"][p], v)

            def step(l, b, u, i, has_a, has_b):
                d = sd[l]
                if has_a:
                    project_k(l, b + 2, u, i + 1)
                if has_b:
                    stacks(l, b + 1, 1 - u, i + u)
                if l == 0:
                    pe.wait_ge(sa[l]["biasT"], 2 * (b + 1))
                pe.wait_ge(d["mload"][u], 16 * MROWS * (i + 1))
                for hg in range(NHG):
                    for t in range(NKT):
                        if has_b:
                            score(l, b + 1, 1 - u, HQ * hg + t)
                        score_T(l, b, u, hg, t)
                    if has_b:
                        score(l, b + 1, 1 - u, HQ * hg + NKT)
                    if hg > 0:
                        weigh(l, b, u, hg - 1)
                weigh(l, b, u, NHG - 1)
                if has_b:
                    turn_max(l, b + 1, b)
                if has_a:
                    project_v(l, b + 2, u)
                finish(l, b, b + 1 if has_b else B - 1)

            def attn(l):
                pe.wait_ge(s_wa[l], 16 * 4)
                norm(NORMS[2 * l], project_q(l))
                pe.sem_inc(sa[l]["exp"], 2)
                pe.sem_inc(sa[l]["pv"], NHG)
                for n in range(2):
                    project_k(l, n, n, None)
                    project_v(l, n, n)
                stacks(l, 0, 0, None)
                for h in range(H):
                    score(l, 0, 0, h)
                turn_max(l, 0, None)
                with pe.Fori(0, B // 2 - 1) as i:
                    for u in range(2):
                        step(l, 2 * i + u, u, i, True, True)
                step(l, B - 2, 0, B // 2 - 1, False, True)
                step(l, B - 1, 1, B // 2 - 1, False, False)

            def turn_y(s, g):
                pe.wait_ge(s["y_copied"], KT * (g + 1))
                pe.wait_ge(s["x"], GB * g)
                for t in range(GB):
                    for k in range(KT):
                        x = nc.tensor.transpose(ps[0:S, 6 + t // 2, (t % 2) * D + k * P:(t % 2) * D + (k + 1) * P],
                                                yT[:, k, t * S:(t + 1) * S], ident[:, :])
                    if t % 2:
                        x.then_inc(s["yT"], 1)

            pe.wait_ge(s_const, NCONST)
            pe.wait_ge(s_setup, NSETUP)
            pe.wait_ge(s_gates, 3)
            attn(0)
            pe.wait_ge(sa[0]["x"], B)
            pe.wait_ge(s_wf[0], 16 * 10)

            def router(g):
                pe.wait_ge(s0["sc"], g)
                for t in range(GB):
                    for k in range(KT):
                        x = mm(ps[0:S, 4, t * E:(t + 1) * E], xT[:, k, t * S:(t + 1) * S], Wr[:, k, :], start=k == 0, stop=k == KT - 1)
                    x.then_inc(s0["logit"], 1)
                pe.wait_ge(s0["rt"], ROUT * (g + 1))
                pe.wait_ge(s0["wT_copied"], g)
                for t in range(GB):
                    nc.tensor.transpose(ps[0:E, 5, t * S:(t + 1) * S], wtok[:, t, :], ident[0:S, 0:S]).then_inc(s0["wT"], 1)

            norm("f0", router)

            def up0(i, g):
                rows, col = tile_rows0(i), tile_col0(i)
                tok = bass.ds(g * GT, GT)
                hold(pe, s0["silu"], NFT0 * g + max(i - 1, 0))
                for k in range(KT):
                    x = mm(ps[0:rows, i % 2, 0:GT], Wg[:, k, col:col + rows], xT_all[:, k, tok], start=k == 0, stop=k == KT - 1)
                x.then_inc(s0["g"], 1)
                hold(pe, s0["gu"], NFT0 * g + max(i - 1, 0))
                for k in range(KT):
                    x = mm(ps[0:rows, 2 + i % 2, 0:GT], Wu[:, k, col:col + rows], xT_all[:, k, tok], start=k == 0, stop=k == KT - 1)
                x.then_inc(s0["u"], 1)

            def down0(i, g):
                rows = tile_rows0(i)
                if i == 0:
                    pe.wait_ge(s0["y_copied"], KT * g)
                if i < 2:
                    pe.wait_ge(s0["gu"], NFT0 * g + i + 1)
                else:
                    pe.wait_ge(s0["h"], scaled(NFT0 - 1) * g + scaled(i))
                for m in range(KT):
                    x = mm(ps[:, 4 + m, 0:GT], Wd[0:rows, i, m * P:(m + 1) * P], hh[i % 2][0:rows, :],
                           start=i == 0, stop=i == NFT0 - 1)
                x.then_inc(s0["y"], 1)

            with pe.Fori(0, NG) as g:
                for i in range(NFT0):
                    up0(i, g)
                    if i > 1:
                        down0(i - 2, g)
                down0(NFT0 - 2, g)
                down0(NFT0 - 1, g)
                turn_y(s0, g)
            pe.wait_ge(s0["x"], B)
            attn(1)
            pe.wait_ge(sa[1]["x"], B)
            pe.wait_ge(s_wf[1], 16 * 6)

            def gate(g):
                pe.wait_ge(s1["rt"], 7 * g)
                for t in range(GB):
                    for k in range(KT):
                        x = mm(ps[0:S, 4, t * GA:(t + 1) * GA], xT[:, k, t * S:(t + 1) * S], WgA[:, k, :], start=k == 0, stop=k == KT - 1)
                    x.then_inc(s1["logit"], 1)
                pe.wait_ge(s1["rt"], 7 * (g + 1))
                pe.wait_ge(s1["rT_copied"], g)
                for t in range(GB):
                    nc.tensor.transpose(ps[0:E1 * R1, 5, t * S:(t + 1) * S], rm[:, t, :], ident[0:S, 0:S]).then_inc(s1["rT"], 1)

            norm("f1", gate)
            pe.wait_ge(s1["rT_copied"], NG)
            pe.sem_inc(s1["y"], 2)

            def up1(i, g):
                tok = bass.ds(g * GT, GT)
                pe.wait_ge(s1["h"], NFT1 * g + max(i - 1, 0))
                for k in range(KT):
                    mm(ps[:, i % 2, 0:GT], wiT[:, k, i * P:(i + 1) * P], xT_all[:, k, tok], start=k == 0, stop=False)
                mm(ps[:, i % 2, 0:GT], BT[:, i * P:(i + 1) * P], rT_all[:, tok], start=False, stop=True).then_inc(s1["h_ready"], 1)

            def down1(i, g):
                if i == 0:
                    pe.wait_ge(s1["y_copied"], KT * g)
                pe.wait_ge(s1["h"], NFT1 * g + i + 1)
                for m in range(KT):
                    x = mm(ps[:, 4 + m, 0:GT], woT[:, i, m * P:(m + 1) * P], hh[i % 2][:, :],
                           start=i == 0, stop=i == NFT1 - 1)
                x.then_inc(s1["y"], 1)

            with pe.Fori(0, NG) as g:
                for i in range(NFT1):
                    up1(i, g)
                    if i > 0:
                        down1(i - 1, g)
                down1(NFT1 - 1, g)
                turn_y(s1, g)


_DIRECT = ["x", "g_xattn", "g_ffn", "L0_xattn_Wv", "L0_xattn_bv", "L0_xattn_Wo", "L0_xattn_bo",
           "L0_ffn_W_gate_router", "L0_ffn_expert_bias", "L0_ffn_Wg", "L0_ffn_Wu", "L0_ffn_Wd", "L0_ffn_Wg_s",
           "L0_ffn_Wu_s", "L0_ffn_Wd_s", "L1_xattn_W_v", "L1_xattn_W_o", "L1_xattn_b_o", "L1_ffn_gate_b",
           "L1_ffn_wi_b", "L1_ffn_wo_b"]


def kernel(**inputs):
    import numpy as np
    import concourse.bacc as bacc
    from concourse.bass_utils import run_bass_kernel_spmd

    a = {n: np.asarray(v) for n, v in inputs.items()}
    lay = {n: a[n] for n in _DIRECT}

    def by_dim(w):
        return w.reshape(w.shape[:-1] + (KT, HH, HD)).swapaxes(-1, -2).reshape(w.shape)

    for n in ("L0_xattn_Wq", "L0_xattn_bq", "L0_xattn_Wk", "L0_xattn_bk", "L1_xattn_W_q", "L1_xattn_W_k"):
        lay[n] = by_dim(a[n])
    for n in ("L0_xattn_bq", "L0_xattn_bk"):
        lay[n] = lay[n].reshape(-1, P).T
    for n in ("L1_ffn_wi_b", "L1_ffn_wo_b"):
        lay[n] = a[n].reshape(-1, P).T
    lay["ctxT"] = a["ctx_1024"].transpose(0, 2, 1)
    mask = a["mask_Bx1xSxS2_bk1"].reshape(B, S, S2)
    lay["mask"], lay["maskT"] = mask, mask.transpose(0, 2, 1)
    lay["gateT"] = a["L1_ffn_gate_W"].T
    lay["loraAT"] = a["L1_ffn_lora_A"].reshape(E1 * R1, D).T
    lay["loraBT"] = a["L1_ffn_lora_B"].transpose(0, 2, 1).reshape(E1 * R1, F1)
    lay["wiT"], lay["woT"] = a["L1_ffn_wi_W"].T, a["L1_ffn_wo_W"].T
    lay["ident"] = np.eye(P, dtype=np.float32)
    lay["iota8"] = np.arange(E, dtype=np.float32)

    nc = bacc.Bacc("TRN2", target_bir_lowering=False, num_devices=1)
    arrays, io = {}, {}
    for n, v in lay.items():
        v = np.ascontiguousarray(v)
        arrays[f"in_{n}"] = v
        io[n] = nc.dram_tensor(f"in_{n}", v.shape, mybir.dt.from_np(v.dtype), kind="ExternalInput").ap()
    out = nc.dram_tensor("out", (B, S, D), F32, kind="ExternalOutput").ap()
    build(nc, io, out)
    r = run_bass_kernel_spmd(nc, [arrays], core_ids=[0])
    return r.results[0]["out"]
```

```python
import concourse.bass as bass
from concourse import mybir
from contextlib import ExitStack

F32 = mybir.dt.float32
BF16 = mybir.dt.bfloat16
U8 = mybir.dt.uint8
U32 = mybir.dt.uint32
ALU = mybir.AluOpType
ACT = mybir.ActivationFunctionType
AX = mybir.AxisListType

B, S, S2, D, H = 16, 100, 361, 256, 16
HD = D // H
P = 128
KT = D // P
HH = H // KT
GB = 4
NG = B // GB
GT = GB * S
NKT = -(-S2 // P)
KROWS = [min(P, S2 - t * P) for t in range(NKT)]
HQ = 4
NHG = H // HQ
E, F = 8, 192
FTOT = F + E * F
NFT0 = -(-F // P) + E * F // P
E1, R1, F1 = 8, 4, 1024
NFT1 = F1 // P
EPS = 1e-5
ROUTE_EPS = 1e-20
MASKED = -1e15
SCALE = float(HD) ** -0.5

KPART = [0, 0, 0, 1, 1, 2]
QPART = [0, 1, 2, 0, 1, 0]
NST = len(KPART)
SROWS = NST * HD
MROWS = 2
KSROWS = SROWS + MROWS


def build(nc, io, out):
    ctx = ExitStack()
    with ctx:
        def sb(name, shape, dt=F32):
            return ctx.enter_context(nc.sbuf_tensor(name, shape, dt))

        def sem(name):
            return ctx.enter_context(nc.semaphore(name))

        def dram(name, shape, dt):
            return nc.dram_tensor(name, shape, dt, kind="Internal").ap()

        ps = ctx.enter_context(nc.psum_tensor("ps", [P, 8, 512], F32))
        x_sb = sb("x_sb", [S, B, D])
        ident = sb("ident", [P, P])
        iota8 = sb("iota8", [S, E])
        w_attn = [{n: sb(f"w{n}{l}", [P, KT, D]) for n in "qkvo"} for l in range(2)]
        bq4 = [sb(f"bq4_{l}", [P, KT]) for l in range(2)]
        bk = [sb(f"bk_{l}", [P, KT]) for l in range(2)]
        bv_b = sb("bv_b", [S, D])
        bo_b = [sb(f"bo_b{l}", [S, D]) for l in range(2)]
        gates = sb("gates", [P, 4])
        stat = sb("stat", [S, B, 6])
        mean_var = sb("mean_var", [S, B, 2])
        var_eps = sb("var_eps", [S, B])
        rstd = sb("rstd", [S, B])
        neg_half = sb("neg_half", [S, B])
        xn = sb("xn", [S, GB, D])
        xT = sb("xT", [P, KT, B * S])

        scr_q = dram("scr_q", [B, NST, KT, P, S], BF16)
        scr_k = dram("scr_k", [2, NST, KT, P, S2], BF16)
        scr_w = dram("scr_w", [E, B * S], F32)

        s_const = sem("const_loaded")
        s_x = [sem(f"x_loaded{g}") for g in range(NG)]
        s_wa = [sem(f"attn_weights{l}") for l in range(2)]
        s_wf = [sem(f"ffn_weights{l}") for l in range(2)]
        s_setup = sem("setup_vec")
        s_gates = sem("gates_ready")
        NORMS = ["q0", "f0", "q1", "f1"]
        sn = {p: {n: sem(f"{p}_{n}") for n in ("stat", "mv", "veps", "rstd", "xn", "xnT", "xT")} for p in NORMS}
        sq = [{n: sem(f"q{l}_{n}") for n in ("ready", "f32", "split", "stored")} for l in range(2)]
        AN = ("k_ready", "k1", "k_rest1", "k2", "k3", "v_ready", "v_copied", "bias", "biasT", "s_ready", "max",
              "mT", "msplit", "sT", "exp", "pv", "o_copied", "oT", "rec", "on", "onv", "onT", "onT_copied", "wo",
              "addb", "x")
        sa = [{n: sem(f"a{l}_{n}") for n in AN} for l in range(2)]
        AD = ("ctx", "kst", "mload")
        sd = [{n: [sem(f"a{l}_{n}{p}") for p in range(2)] for n in AD} for l in range(2)]
        for l in range(2):
            sd[l]["kload"] = [[sem(f"a{l}_kload{half}{p}") for p in range(2)] for half in range(2)]
        s0 = {n: sem(f"f0_{n}") for n in ("lgT", "lg_copied", "lg", "sc", "rt", "wT", "wT_copied", "w_stored", "w_bc",
                                          "g", "u", "silu", "gu", "h", "y", "y_copied", "yT", "x")}
        s1 = {n: sem(f"f1_{n}") for n in ("lgT", "lg_copied", "lg", "rt", "rT", "rT_copied", "h_ready", "h", "y",
                                          "y_copied", "yT", "x")}
        s_out = sem("out_stored")

        GA = E1 * R1 + E1
        with ExitStack() as parts:
            def psb(name, shape, dt=F32):
                return parts.enter_context(nc.sbuf_tensor(name, shape, dt))

            kp = psb("kp", [P, 3, KT, S2], BF16)
            kr = psb("kr", [P, KT, S2])
            qp = psb("qp", [P, 3, KT, GT], BF16)
        lgT = ctx.enter_context(nc.sbuf_tensor("lgT", [GA, B * S], F32))
        wrT = ctx.enter_context(nc.sbuf_tensor("wrT", [E1 * R1, B * S], F32))
        wT, rT = wrT[0:E, :], wrT[:, :]

        def asb(name, shape, dt=F32):
            return ctx.enter_context(nc.sbuf_tensor(name, shape, dt))

        cT = [asb(f"cT{p}", [P, KT, S2]) for p in range(2)]
        KS = [asb(f"KS{p}", [KSROWS, H * S2 + NKT * P - S2], BF16) for p in range(2)]
        QS = [asb(f"QS{p}", [KSROWS, H, S], BF16) for p in range(2)]
        qf = asb("qf", [P, KT, GT])
        qr = asb("qr", [P, KT, GT])
        V1 = [asb(f"V1_{p}", [P, NKT, H, HD + 1]) for p in range(2)]
        prob = asb("prob", [P, NKT, NHG, HQ * S])[:, :, :, :]
        mx = asb("mx", [S, H])
        mp = asb("mp", [H, MROWS, S], BF16)
        masku = [asb(f"masku{p}", [S, S2], U8) for p in range(2)]
        maskTu = [asb(f"maskTu{p}", [P, NKT, S], U8) for p in range(2)]
        biasq = [asb(f"biasq{p}", [S, S2], BF16) for p in range(2)]
        biasT = [asb(f"biasT{p}", [P, NKT, S], BF16) for p in range(2)]
        ident_bf = asb("ident_bf", [P, P], BF16)
        oT_sb = asb("oT_sb", [P, HQ * S])
        rec = asb("rec", [S, H])
        on = asb("on", [S, D])
        onv = asb("onv", [S, D])
        onT = asb("onT", [P, KT, S])
        xb = asb("xb", [S, D])

        Wr = asb("Wr", [P, KT, E])
        ebias = asb("ebias", [S, E])
        Wg = asb("Wg", [P, KT, FTOT])
        Wu = asb("Wu", [P, KT, FTOT])
        Wd = asb("Wd", [P, NFT0, D])
        wbc = prob.rearrange("p t g n -> p (t g n)")[:, 0:E * GT].rearrange("p (e n) -> p e n", e=E)
        sc = asb("sc", [S, B, E])
        bsc = asb("bsc", [S, B, E])
        mx8 = asb("mx8", [S, B, 8])
        ix8 = asb("ix8", [S, B, 8], U32)
        ixf = asb("ixf", [S, B, 2])
        oh = asb("oh", [S, 2, B, E])
        wsel = asb("wsel", [S, B, E])
        wsum = asb("wsum", [S, B])
        wrec = asb("wrec", [S, B])
        wtok = asb("wtok", [S, B, E])
        sg = [asb(f"sg{p}", [P, GT]) for p in range(2)]
        gu = [qr[:, p, :] for p in range(2)]
        hh = [qf[:, p, :] for p in range(2)]
        yT = asb("yT", [P, KT, GT])
        WgA = asb("WgA", [P, KT, GA])
        gb_b = asb("gb_b", [S, E1])
        wiT = Wg[:, :, 0:F1]
        wib = asb("wib", [P, NFT1])
        woT = Wu[:, :, :].rearrange("p k f -> p (k f)")[:, 0:NFT1 * D].rearrange("p (t n) -> p t n", t=NFT1)
        wob = asb("wob", [P, KT])
        BT = asb("BT", [E1 * R1, F1])
        rm = asb("rm", [S, B, E1 * R1])

        def bc(ap, shape):
            return ap.to_broadcast(shape)

        def keys(n):
            return KROWS[n]

        def tile_rows0(i):
            return F - P if i == 1 else P

        def scaled(i):
            return sum(1 + (t * P // F != (t * P + P - 1) // F) for t in range(i - 1))

        def tile_col0(i):
            return i * P if i < 2 else F + (i - 2) * P

        NCONST = 16 * 12
        NSETUP = 8

        s_held = sem("held_waits")
        START = 1
        COUNTED = [v for d in (*sn.values(), *sq, *sa, s0, s1) for v in d.values()]

        block = ctx.enter_context(nc.Block())

        @block.sync
        def _(sp):
            for g in range(NG):
                sp.dma_start(x_sb[:, g * GB:(g + 1) * GB, :],
                             io["x"][g * GB:(g + 1) * GB].rearrange("b s d -> s b d")).then_inc(s_x[g], 16)

            def ctx_load(l, n, p, fresh):
                a, d = sa[l], sd[l]
                if not fresh:
                    sp.wait_ge(a["v_ready"], START + 2 * (n - 1))
                    sp.sem_inc(s_held, 1)
                    if l == 0:
                        sp.wait_ge(a["biasT"], START + n - 1)
                        sp.sem_inc(s_held, 1)
                sp.dma_start(cT[p][:, :, :], io["ctxT"][n]).then_inc(d["ctx"][p], 16)
                if l == 0:
                    sp.dma_start(masku[p][:, :], io["mask"][n]).then_inc(d["ctx"][p], 16)
                    sp.dma_start(maskTu[p][:, :, :], io["maskT"][n]).then_inc(d["ctx"][p], 16)

            def k_store(l, n, p, idx):
                a, d = sa[l], sd[l]
                sp.wait_ge(a["k3"], START + n + 1)
                if idx > 0 if isinstance(idx, int) else True:
                    for half in range(2):
                        sp.wait_ge(d["kload"][half][p], 32 * idx)
                sp.sem_inc(s_held, 1)
                for j in range(NST):
                    sp.dma_start(scr_k[p, j].rearrange("k p n -> p k n"), kp[:, KPART[j], :, :]).then_inc(d["kst"][p], 16)

            def stack_load(l, n, p, idx, half, fresh):
                a, d = sa[l], sd[l]
                if half == 0:
                    sp.wait_ge(d["kst"][p], 16 * NST * (idx + 1))
                    sp.sem_inc(s_held, 1)
                if not fresh:
                    sp.wait_ge(a["sT"], START + NKT * NHG * (n - 2) + NKT * NHG // 2 * (half + 1))
                    sp.sem_inc(s_held, 1)
                c = slice(half * HH * S2, (half + 1) * HH * S2)
                sp.dma_start(KS[p][0:SROWS, c],
                             scr_k[p].rearrange("j k (d h) n -> (j k d) (h n)", h=H)[:, c]).then_inc(d["kload"][half][p], 16)
                c = slice(half * HH * S, (half + 1) * HH * S)
                sp.dma_start(QS[p][0:SROWS].rearrange("r h n -> r (h n)")[:, c],
                             scr_q[n].rearrange("j k (d h) n -> (j k d) (h n)", h=H)[:, c]).then_inc(d["kload"][half][p], 16)

            def q_store(l, g):
                sp.wait_ge(sq[l]["split"], START + 4 * (g + 1))
                sp.sem_inc(s_held, 1)
                for j in range(NST):
                    for k in range(KT):
                        sp.dma_start(scr_q[bass.ds(g * GB, GB), j, k].rearrange("b p n -> p b n"),
                                     qp[:, QPART[j], k, :].rearrange("p (b n) -> p b n", b=GB)).then_inc(sq[l]["stored"], 16)

            def step(l, b, u, i, has_ctx, has_k):
                if has_k:
                    k_store(l, b + 2, u, i + 1)
                    stack_load(l, b + 2, u, i + 1, 0, False)
                if has_ctx:
                    ctx_load(l, b + 3, 1 - u, False)
                if has_k:
                    stack_load(l, b + 2, u, i + 1, 1, False)

            def attn(l):
                if l == 1:
                    sp.wait_ge(sa[0]["x"], START + B)
                ctx_load(l, 0, 0, True)
                ctx_load(l, 1, 1, True)
                with sp.Fori(0, NG) as g:
                    q_store(l, g)
                sp.wait_ge(sq[l]["stored"], START + 16 * NST * KT * NG)
                for n in range(2):
                    k_store(l, n, n, 0)
                    for half in range(2):
                        stack_load(l, n, n, 0, half, True)
                ctx_load(l, 2, 0, False)
                with sp.Fori(0, B // 2 - 2) as i:
                    for u in range(2):
                        step(l, 2 * i + u, u, i, True, True)
                for b in range(B - 4, B - 2):
                    step(l, b, b % 2, b // 2, b + 3 < B, True)

            attn(0)
            sp.wait_ge(s0["wT_copied"], START + 1)
            sp.dma_start(scr_w, wT[:, :]).then_inc(s0["w_stored"], 16)
            sp.wait_ge(s0["w_stored"], START + 16)
            with sp.Fori(0, NG) as g:
                sp.wait_ge(s0["h"], START + scaled(NFT0 - 1) * g)
                sp.sem_inc(s_held, 1)
                sp.dma_start(wbc[:, :, :], scr_w[:, bass.ds(g * GT, GT)].partition_broadcast(P)).then_inc(s0["w_bc"], 16)
            attn(1)
            with sp.Fori(0, NG) as g:
                sp.wait_ge(s1["x"], START + GB * (g + 1))
                sp.sem_inc(s_held, 1)
                sp.dma_start(out[bass.ds(g * GB, GB)].rearrange("b s d -> s b d"),
                             x_sb[:, bass.ds(g * GB, GB), :]).then_inc(s_out, 16)
            sp.wait_ge(s_out, 16 * NG)

        @block.gpsimd
        def _(pool):
            nc.gpsimd.memset(neg_half[:, :], -0.5).then_inc(s_setup, 1)
            for c in COUNTED:
                pool.sem_inc(c, START)

            def norm(p):
                pool.wait_ge(sn[p]["mv"], START + B)
                nc.gpsimd.tensor_scalar(var_eps[:, :], mean_var[:, :, 1], EPS, None, ALU.add).then_inc(sn[p]["veps"], 1)
                pool.wait_ge(sn[p]["veps"], START + 1)
                pool.wait_ge(s_setup, NSETUP)
                nc.gpsimd.tensor_tensor(rstd[:, :], var_eps[:, :], neg_half[:, :], ALU.pow).then_inc(sn[p]["rstd"], 1)

            def bias(n, p, idx, fresh):
                a, d = sa[0], sd[0]
                pool.wait_ge(d["ctx"][p], 48 * (idx + 1))
                pool.sem_inc(s_held, 1)
                if not fresh:
                    pool.wait_ge(a["max"], START + H * (n - 1))
                    pool.sem_inc(s_held, 1)
                nc.gpsimd.tensor_scalar(biasq[p][:, :], masku[p][:, :], MASKED, None, ALU.mult).then_inc(a["bias"], 1)

            def biasT_(n, p, fresh):
                a, d = sa[0], sd[0]
                if not fresh:
                    pool.wait_ge(a["sT"], START + 3 * NHG * (n - 1))
                    pool.sem_inc(s_held, 1)
                nc.gpsimd.tensor_scalar(biasT[p][:, :, :], maskTu[p][:, :, :], MASKED, None, ALU.mult).then_inc(a["biasT"], 1)

            def k3(l, n):
                a = sa[l]
                pool.wait_ge(a["k2"], START + n + 1)
                nc.gpsimd.tensor_tensor(kp[:, 2, :, :], kr[:, :, :], kp[:, 1, :, :], ALU.subtract).then_inc(a["k3"], 1)

            def attn(l):
                norm(NORMS[2 * l])
                for n in range(2):
                    if l == 0:
                        bias(n, n, 0, True)
                        biasT_(n, n, True)
                    k3(l, n)
                with pool.Fori(0, B // 2 - 1) as i:
                    for u in range(2):
                        n = 2 * i + u + 2
                        k3(l, n)
                        if l == 0:
                            bias(n, u, i + 1, False)
                            biasT_(n, u, False)

            attn(0)
            pool.wait_ge(sa[0]["x"], START + B)
            norm("f0")
            with pool.Fori(0, NG) as g:
                pool.wait_ge(s0["w_bc"], START + 16 * (g + 1))
                for i in range(2, NFT0):
                    pool.wait_ge(s0["gu"], START + NFT0 * g + i + 1)
                    pool.wait_ge(s0["y"], START + NFT0 * g + i - 1)
                    e = (i - 2) * P // F
                    own = scaled(NFT0 - 1) * g + scaled(i - 1)
                    if i > 2:
                        pool.wait_ge(s0["h"], START + own)
                    if ((i - 2) * P + P - 1) // F == e:
                        nc.gpsimd.tensor_tensor(hh[i % 2][:, :], gu[i % 2][:, :], wbc[:, e, :], ALU.mult).then_inc(s0["h"], 1)
                    else:
                        half = F * (e + 1) - (i - 2) * P
                        nc.gpsimd.tensor_tensor(hh[i % 2][0:half, :], gu[i % 2][0:half, :], wbc[0:half, e, :],
                                                ALU.mult).then_inc(s0["h"], 1)
                        pool.wait_ge(s0["h"], START + own + 1)
                        nc.gpsimd.tensor_tensor(hh[i % 2][half:P, :], gu[i % 2][half:P, :], wbc[half:P, e + 1, :],
                                                ALU.mult).then_inc(s0["h"], 1)
            pool.wait_ge(s0["x"], START + B)
            attn(1)
            pool.wait_ge(sa[1]["x"], START + B)
            norm("f1")

        @block.scalar
        def _(act):
            act.dma_start(ident[:, :], io["ident"]).then_inc(s_const, 16)
            act.dma_start(w_attn[0]["k"][:, :, :], io["L0_xattn_Wk"].rearrange("(k p) n -> p k n", p=P)).then_inc(s_wa[0], 16)
            act.dma_start(w_attn[0]["q"][:, :, :], io["L0_xattn_Wq"].rearrange("(k p) n -> p k n", p=P)).then_inc(s_wa[0], 16)
            act.dma_start(bq4[0][:, :], io["L0_xattn_bq"]).then_inc(s_const, 16)
            act.dma_start(bk[0][:, :], io["L0_xattn_bk"]).then_inc(s_const, 16)
            act.dma_start(w_attn[0]["v"][:, :, :], io["L0_xattn_Wv"].rearrange("(k p) n -> p k n", p=P)).then_inc(s_wa[0], 16)
            act.dma_start(w_attn[0]["o"][:, :, :], io["L0_xattn_Wo"].rearrange("(k p) n -> p k n", p=P)).then_inc(s_wa[0], 16)
            act.dma_start(bv_b[:, :], io["L0_xattn_bv"].partition_broadcast(S)).then_inc(s_const, 16)
            act.dma_start(bo_b[0][:, :], io["L0_xattn_bo"].partition_broadcast(S)).then_inc(s_const, 16)
            act.dma_start(bo_b[1][:, :], io["L1_xattn_b_o"].partition_broadcast(S)).then_inc(s_const, 16)
            act.dma_start(gates[:, 0:2], io["g_xattn"].partition_broadcast(P)).then_inc(s_const, 16)
            act.dma_start(gates[:, 2:4], io["g_ffn"].partition_broadcast(P)).then_inc(s_const, 16)
            act.dma_start(iota8[:, :], io["iota8"].partition_broadcast(S)).then_inc(s_const, 16)
            act.dma_start(ebias[:, :], io["L0_ffn_expert_bias"].partition_broadcast(S)).then_inc(s_const, 16)
            act.dma_start(gb_b[:, :], io["L1_ffn_gate_b"].partition_broadcast(S)).then_inc(s_const, 16)
            act.dma_start(wob[:, :], io["L1_ffn_wo_b"]).then_inc(s_const, 16)
            act.dma_start(Wr[:, :, :], io["L0_ffn_W_gate_router"].rearrange("(k p) e -> p k e", p=P)).then_inc(s_wf[0], 16)
            for w, sh, ro in ((Wg, "L0_ffn_Wg_s", "L0_ffn_Wg"), (Wu, "L0_ffn_Wu_s", "L0_ffn_Wu")):
                act.dma_start(w[:, :, 0:F], io[sh].rearrange("(k p) f -> p k f", p=P)).then_inc(s_wf[0], 16)
                for k in range(KT):
                    act.dma_start(w[:, k, F:FTOT].rearrange("p (e f) -> p e f", e=E),
                                  io[ro][:, k * P:(k + 1) * P].rearrange("e p f -> p e f")).then_inc(s_wf[0], 16)
            act.dma_start(Wd[:, 0, :], io["L0_ffn_Wd_s"][0:P]).then_inc(s_wf[0], 16)
            act.dma_start(Wd[0:F - P, 1, :], io["L0_ffn_Wd_s"][P:F]).then_inc(s_wf[0], 16)
            act.dma_start(Wd[:, 2:, :], io["L0_ffn_Wd"].rearrange("e f d -> (e f) d").rearrange("(t p) d -> p t d", p=P)).then_inc(s_wf[0], 16)
            for n, key in (("k", "W_k"), ("q", "W_q"), ("v", "W_v"), ("o", "W_o")):
                act.dma_start(w_attn[1][n][:, :, :], io[f"L1_xattn_{key}"].rearrange("(k p) n -> p k n", p=P)).then_inc(s_wa[1], 16)
            act.dma_start(WgA[:, :, 0:E1 * R1], io["loraAT"].rearrange("(k p) n -> p k n", p=P)).then_inc(s_wf[1], 16)
            act.dma_start(WgA[:, :, E1 * R1:GA], io["gateT"].rearrange("(k p) n -> p k n", p=P)).then_inc(s_wf[1], 16)
            act.dma_start(wib[:, :], io["L1_ffn_wi_b"]).then_inc(s_wf[1], 16)
            act.dma_start(BT[:, :], io["loraBT"]).then_inc(s_wf[1], 16)
            act.wait_ge(s_const, NCONST)
            nc.scalar.activation(gates[:, :], gates[:, :], ACT.Tanh).then_inc(s_gates, 1)
            nc.scalar.activation(bq4[0][:, :], bq4[0][:, :], ACT.Copy, scale=SCALE).then_inc(s_gates, 1)
            nc.scalar.activation(ident_bf[:, :], ident[:, :], ACT.Copy).then_inc(s_gates, 1)
            act.wait_ge(s_setup, NSETUP)
            act.wait_ge(s_gates, 3)

            def norm(p, more):
                with act.Fori(0, NG // 2) as j:
                    for u in range(2):
                        g = 2 * j + u
                        act.wait_ge(sn[p]["xnT"], START + GB * (g + 1))
                        nc.scalar.activation(xT[:, :, bass.ds(g * GT, GT)], ps[:, 2 * u:2 * u + KT, 0:GT],
                                             ACT.Copy).then_inc(sn[p]["xT"], 1)
                        more(g, u)

            def copy_q(l):
                def run(g, u):
                    act.wait_ge(sq[l]["split"], START + 4 * g)
                    for k in range(KT):
                        act.wait_ge(sq[l]["ready"], START + KT * g + k + 1)
                        nc.scalar.activation(qf[:, k, :], ps[:, 4 + k, 0:GT], ACT.Identity, scale=SCALE,
                                             bias=bq4[l][:, k:k + 1]).then_inc(sq[l]["f32"], 1)
                return run

            def copy_logits(s, n):
                def run(g, u):
                    act.wait_ge(s["lgT"], START + g + 1)
                    nc.scalar.activation(lgT[0:n, bass.ds(g * GT, GT)], ps[0:n, 4 + u, 0:GT], ACT.Copy).then_inc(s["lg_copied"], 1)
                return run

            def k_first(l, n, m, stored):
                a, d = sa[l], sd[l]
                if m == 0 and stored is not None:
                    act.wait_ge(d["kst"][stored[0]], 16 * NST * stored[1])
                act.wait_ge(a["k_ready"], START + KT * n + m + 1)
                nc.scalar.activation(kp[:, 0, m, :], ps[:, 4 + m, 0:S2], ACT.Identity, bias=bk[l][:, m:m + 1]).then_inc(a["k1"], 1)

            def k_second(l, n):
                a = sa[l]
                act.wait_ge(a["k_rest1"], START + KT * (n + 1))
                nc.scalar.activation(kp[:, 1, :, :], kr[:, :, :], ACT.Copy).then_inc(a["k2"], 1)

            def v_copy(l, n, p, part):
                a = sa[l]
                act.wait_ge(a["v_ready"], START + 2 * n + part + 1)
                if part == 0:
                    nc.scalar.activation(V1[p][:, 0:2, :, 0:HD],
                                         ps[:, 4, :].rearrange("p (t h e) -> p t h e", t=2, h=H), ACT.Copy).then_inc(a["v_copied"], 1)
                else:
                    nc.scalar.activation(V1[p][0:KROWS[2], 2, :, 0:HD],
                                         ps[0:KROWS[2], 5, 0:D].rearrange("p (h e) -> p h e", h=H), ACT.Copy).then_inc(a["v_copied"], 1)

            def copy_o(l, b):
                a = sa[l]
                act.wait_ge(a["pv"], START + NHG * (b + 2))
                nc.scalar.activation(oT_sb[:, :], ps[:, 6, 0:HQ * S], ACT.Copy).then_inc(a["o_copied"], 1)

            def copy_on(l, b):
                a = sa[l]
                act.wait_ge(a["onT"], START + b + 1)
                nc.scalar.activation(onT[:, :, :], ps[:, 7, 0:KT * S], ACT.Copy).then_inc(a["onT_copied"], 1)

            def exps(l, b, hg):
                a = sa[l]
                act.wait_ge(a["pv"], START + NHG * b + hg + 1)
                for t in range(NKT):
                    c = hg * NKT + t
                    act.wait_ge(a["sT"], START + NKT * NHG * b + c + 1)
                    nc.scalar.activation(prob[0:KROWS[t], t, hg, :], ps[0:KROWS[t], c % 2, 0:HQ * S],
                                         ACT.Exp).then_inc(a["exp"], 1)

            def max_load(l, n, p):
                a, d = sa[l], sd[l]
                act.wait_ge(a["msplit"], START + MROWS * (n + 1))
                for j in range(MROWS):
                    act.dma_start(QS[p][SROWS + j:SROWS + j + 1, :, :], mp[:, j, :]).then_inc(d["mload"][p], 16)

            def step(l, b, u, i, has_o, has_k, has_b):
                if has_o:
                    copy_o(l, b - 1)
                if has_k:
                    for m in range(KT):
                        k_first(l, b + 2, m, (1 - u, i + 1 + u))
                exps(l, b, 0)
                if has_o:
                    copy_on(l, b - 1)
                if has_k:
                    k_second(l, b + 2)
                exps(l, b, 1)
                if has_b:
                    v_copy(l, b + 1, 1 - u, 0)
                exps(l, b, 2)
                if has_b:
                    v_copy(l, b + 1, 1 - u, 1)
                exps(l, b, 3)
                if has_b:
                    max_load(l, b + 1, 1 - u)

            def attn(l):
                norm(NORMS[2 * l], copy_q(l))
                for n in range(2):
                    for m in range(KT):
                        k_first(l, n, m, (0, 1) if n else None)
                    k_second(l, n)
                for part in range(2):
                    v_copy(l, 0, 0, part)
                max_load(l, 0, 0)
                step(l, 0, 0, 0, False, True, True)
                step(l, 1, 1, 0, True, True, True)
                with act.Fori(1, B // 2 - 1) as i:
                    for u in range(2):
                        step(l, 2 * i + u, u, i, True, True, True)
                for b in (B - 2, B - 1):
                    step(l, b, b % 2, b // 2, True, False, b + 1 < B)
                copy_o(l, B - 1)
                copy_on(l, B - 1)

            attn(0)
            act.wait_ge(sa[0]["x"], START + B)
            norm("f0", copy_logits(s0, E))
            act.wait_ge(s0["lg"], START + 1)
            nc.scalar.activation(sc[:, :, :], ps[0:S, 6, 0:B * E], ACT.Sigmoid).then_inc(s0["sc"], 1)
            act.wait_ge(s0["wT"], START + 1)
            nc.scalar.activation(wT[:, :].rearrange("e (g n) -> e g n", g=NG), ps[0:E, 0:NG, 0:GT], ACT.Copy).then_inc(s0["wT_copied"], 1)
            with act.Fori(0, NG) as g:
                for i in range(NFT0):
                    rows = tile_rows0(i)
                    act.wait_ge(s0["g"], START + NFT0 * g + i + 1)
                    act.wait_ge(s0["gu"], START + NFT0 * g + max(i - 1, 0))
                    nc.scalar.activation(sg[i % 2][0:rows, :], ps[0:rows, i % 2, 0:GT], ACT.Silu).then_inc(s0["silu"], 1)
                act.wait_ge(s0["y"], START + NFT0 * (g + 1))
                nc.scalar.activation(yT[:, :, :], ps[:, 4:4 + KT, 0:GT], ACT.Copy).then_inc(s0["y_copied"], 1)
            act.wait_ge(s0["x"], START + B)
            act.dma_start(wiT[:, :, :], io["wiT"].rearrange("(k p) n -> p k n", p=P)).then_inc(s_wf[1], 16)
            act.dma_start(woT[:, :, :], io["woT"].rearrange("(t p) n -> p t n", p=P)).then_inc(s_wf[1], 16)
            attn(1)
            act.wait_ge(sa[1]["x"], START + B)
            norm("f1", copy_logits(s1, GA))
            act.wait_ge(s1["rT"], START + 1)
            nc.scalar.activation(rT[:, :].rearrange("e (g n) -> e g n", g=NG), ps[0:E1 * R1, 0:NG, 0:GT], ACT.Copy).then_inc(s1["rT_copied"], 1)
            with act.Fori(0, NG) as g:
                for i in range(NFT1):
                    act.wait_ge(s1["h_ready"], START + NFT1 * g + i + 1)
                    act.wait_ge(s1["y"], START + NFT1 * g + i + 1)
                    nc.scalar.activation(hh[i % 2][:, :], ps[:, i % 2, 0:GT], ACT.Relu, bias=wib[:, i:i + 1]).then_inc(s1["h"], 1)
                act.wait_ge(s1["y"], START + NFT1 * (g + 1) + 2)
                for k in range(KT):
                    nc.scalar.activation(yT[:, k, :], ps[:, 4 + k, 0:GT], ACT.Identity,
                                         bias=wob[:, k:k + 1]).then_inc(s1["y_copied"], 1)

        @block.vector
        def _(dve):
            for p in range(2):
                nc.vector.memset(KS[p][:, :], 1.0).then_inc(s_setup, 1)
                nc.vector.memset(V1[p][:, :, :, :], 1.0).then_inc(s_setup, 1)
            nc.vector.memset(bq4[1][:, :], 0.0).then_inc(s_setup, 1)
            nc.vector.memset(bk[1][:, :], 0.0).then_inc(s_setup, 1)
            nc.vector.memset(ps[:, 6, :], 0.0).then_inc(s_setup, 1)

            def stats(p, b, done, count):
                n = sn[p]
                dve.wait_ge(done, START + count)
                dve.sem_inc(s_held, 1)
                nc.vector.bn_stats(stat[:, b, :], x_sb[:, b, :]).then_inc(n["stat"], 1)

            def stats_end(p):
                n = sn[p]
                dve.wait_ge(n["stat"], START + B)
                for b in range(B):
                    nc.vector.bn_aggr(mean_var[:, b, :], stat[:, b, :]).then_inc(n["mv"], 1)

            def norm(p, more):
                n = sn[p]
                dve.wait_ge(n["rstd"], START + 1)
                with dve.Fori(0, NG // 2) as j:
                    for u in range(2):
                        g = 2 * j + u
                        dve.wait_ge(n["xnT"], START + GB * g)
                        for t in range(GB):
                            b = g * GB + t
                            nc.vector.tensor_scalar(xn[:, t, :], x_sb[:, b, :], mean_var[:, bass.ds(b, 1), 0], rstd[:, bass.ds(b, 1)],
                                                    ALU.subtract, ALU.mult).then_inc(n["xn"], 1)
                        more(g, u)

            def split_q(l):
                def run(g, u):
                    q = sq[l]
                    dve.wait_ge(q["f32"], START + KT * (g + 1))
                    dve.wait_ge(q["stored"], START + 16 * NST * KT * g)
                    nc.vector.tensor_copy(qp[:, 0, :, :], qf[:, :, :]).then_inc(q["split"], 1)
                    dve.wait_ge(q["split"], START + 4 * g + 1)
                    nc.vector.tensor_tensor(qr[:, :, :], qf[:, :, :], qp[:, 0, :, :], ALU.subtract).then_inc(q["split"], 1)
                    dve.wait_ge(q["split"], START + 4 * g + 2)
                    nc.vector.tensor_copy(qp[:, 1, :, :], qr[:, :, :]).then_inc(q["split"], 1)
                    dve.wait_ge(q["split"], START + 4 * g + 3)
                    nc.vector.tensor_tensor(qp[:, 2, :, :], qr[:, :, :], qp[:, 1, :, :], ALU.subtract).then_inc(q["split"], 1)
                return run

            def pick(r, n):
                sh = [S, B, E]
                dve.wait_ge(r, START + 1)
                for t in range(B):
                    x = nc.vector.max(mx8[:, t, :], bsc[:, t, :])
                x.then_inc(r, 1)
                dve.wait_ge(r, START + 2)
                for t in range(B):
                    x = nc.vector.max_index(ix8[:, t, :], mx8[:, t, :], bsc[:, t, :])
                x.then_inc(r, 1)
                dve.wait_ge(r, START + 3)
                nc.vector.tensor_copy(ixf[:, :, :], ix8[:, :, 0:2]).then_inc(r, 1)
                dve.wait_ge(r, START + 4)
                for j in range(n):
                    nc.vector.tensor_tensor(oh[:, j, :, :], bc(iota8[:, :].unsqueeze(1), sh), bc(ixf[:, :, j:j + 1], sh),
                                            ALU.is_equal).then_inc(r, 1)

            def route():
                r = s0["rt"]
                sh = [S, B, E]
                dve.wait_ge(s0["sc"], START + 1)
                nc.vector.tensor_tensor(bsc[:, :, :], sc[:, :, :], bc(ebias[:, :].unsqueeze(1), sh), ALU.add).then_inc(r, 1)
                pick(r, 2)
                dve.wait_ge(r, START + 6)
                nc.vector.tensor_tensor(wsel[:, :, :], oh[:, 0, :, :], oh[:, 1, :, :], ALU.add).then_inc(r, 1)
                dve.wait_ge(r, START + 7)
                nc.vector.tensor_tensor(wsel[:, :, :], wsel[:, :, :], sc[:, :, :], ALU.mult).then_inc(r, 1)
                dve.wait_ge(r, START + 8)
                nc.vector.reduce_sum(wsum[:, :], wsel[:, :, :], axis=AX.X).then_inc(r, 1)
                dve.wait_ge(r, START + 9)
                nc.vector.tensor_scalar(wsum[:, :], wsum[:, :], ROUTE_EPS, None, ALU.add).then_inc(r, 1)
                dve.wait_ge(r, START + 10)
                nc.vector.reciprocal(wrec[:, :], wsum[:, :]).then_inc(r, 1)
                dve.wait_ge(r, START + 11)
                nc.vector.tensor_tensor(wtok[:, :, :], wsel[:, :, :], bc(wrec[:, :].unsqueeze(2), sh), ALU.mult).then_inc(r, 1)

            def choose():
                r = s1["rt"]
                dve.wait_ge(s1["lg"], START + 2)
                for k in range(2):
                    lg = ps[0:S, 6 + k, 0:HH * GA].rearrange("s (t n) -> s t n", n=GA)
                    x = nc.vector.tensor_tensor(bsc[:, k * HH:(k + 1) * HH, :], lg[:, :, E1 * R1:GA],
                                                bc(gb_b[:, :].unsqueeze(1), [S, HH, E1]), ALU.add)
                x.then_inc(r, 1)
                pick(r, 1)
                dve.wait_ge(r, START + 5)
                for t in range(B):
                    lg = ps[0:S, 6 + t // HH, (t % HH) * GA:(t % HH) * GA + E1 * R1]
                    x = nc.vector.tensor_tensor(rm[:, t, :].rearrange("s (e r) -> s e r", r=R1),
                                                lg.rearrange("s (e r) -> s e r", r=R1),
                                                bc(oh[:, 0, t, :].unsqueeze(2), [S, E1, R1]), ALU.mult)
                x.then_inc(r, 1)

            def k_rest(l, n, m):
                a = sa[l]
                if m == 0:
                    dve.wait_ge(a["k3"], START + n)
                dve.wait_ge(a["k1"], START + KT * n + m + 1)
                nc.vector.scalar_tensor_tensor(kr[:, m, :], ps[:, 4 + m, 0:S2], bk[l][:, m:m + 1], kp[:, 0, m, :],
                                               ALU.add, ALU.subtract).then_inc(a["k_rest1"], 1)

            def maxima(l, n, p, h0, h1):
                a = sa[l]
                if h0 == 0:
                    if l == 0:
                        dve.wait_ge(a["bias"], START + n + 1)
                        dve.sem_inc(s_held, 1)
                    dve.wait_ge(a["mT"], START + n)
                    dve.sem_inc(s_held, 1)
                for h in range(h0, h1):
                    if l == 0:
                        dve.wait_ge(a["s_ready"], START + H * n + h + 1)
                        dve.sem_inc(s_held, 1)
                        nc.vector.tensor_tensor_reduce(ps[0:S, 2 + h % 2, 0:S2], ps[0:S, 2 + h % 2, 0:S2], biasq[p][:, :], 1.0,
                                                       -3.0e38, ALU.add, ALU.max, mx[:, h:h + 1]).then_inc(a["max"], 1)
                    else:
                        dve.wait_ge(a["s_ready"], START + H * n + h + 1)
                        nc.vector.reduce_max(mx[:, h:h + 1], ps[0:S, 2 + h % 2, 0:S2], axis=AX.X).then_inc(a["max"], 1)

            def split_max(l, n, loaded):
                a, d = sa[l], sd[l]
                dve.wait_ge(a["mT"], START + n + 1)
                if loaded is not None:
                    dve.wait_ge(d["mload"][loaded[0]], 16 * MROWS * loaded[1])
                nc.vector.tensor_scalar(mp[:, 0, :], ps[0:H, 7, 0:S], -1.0, None, ALU.mult).then_inc(a["msplit"], 1)
                dve.wait_ge(a["msplit"], START + MROWS * n + 1)
                nc.vector.scalar_tensor_tensor(mp[:, 1, :], ps[0:H, 7, 0:S], -1.0, mp[:, 0, :],
                                               ALU.mult, ALU.subtract).then_inc(a["msplit"], 1)

            def divide(l, b):
                a = sa[l]
                dve.wait_ge(a["oT"], START + b + 1)
                o = ps[0:S, 7, :].rearrange("q (h c) -> q h c", c=32)
                nc.vector.reciprocal(rec[:, :], o[:, :, HD]).then_inc(a["rec"], 1)
                dve.wait_ge(a["rec"], START + b + 1)
                dve.wait_ge(a["onT"], START + b)
                dst = on if l == 0 else onv
                nc.vector.tensor_tensor(dst[:, :].rearrange("q (h e) -> q h e", h=H), o[:, :, 0:HD],
                                        bc(rec[:, :].unsqueeze(2), [S, H, HD]), ALU.mult).then_inc(a["on"], 1)
                if l == 0:
                    dve.wait_ge(a["on"], START + b + 1)
                    nc.vector.tensor_tensor(onv[:, :], on[:, :], bv_b[:, :], ALU.add).then_inc(a["onv"], 1)

            def add_attention(l, b):
                a = sa[l]
                dve.wait_ge(a["wo"], START + b + 1)
                nc.vector.tensor_tensor(xb[:, :], ps[0:S, 7, D:2 * D], bo_b[l][:, :], ALU.add).then_inc(a["addb"], 1)
                dve.wait_ge(a["addb"], START + b + 1)
                nc.vector.scalar_tensor_tensor(x_sb[:, b, :], xb[:, :], gates[0:S, l:l + 1], x_sb[:, b, :],
                                               ALU.mult, ALU.add).then_inc(a["x"], 1)

            def step(l, b, u, i, has_o, has_k, has_b):
                p = NORMS[2 * l + 1]
                if has_k:
                    k_rest(l, b + 2, 0)
                if has_o:
                    divide(l, b - 1)
                if has_k:
                    k_rest(l, b + 2, 1)
                if has_b:
                    maxima(l, b + 1, 1 - u, 0, 8)
                if has_o:
                    add_attention(l, b - 1)
                if has_b:
                    maxima(l, b + 1, 1 - u, 8, 12)
                if has_o:
                    stats(p, b - 1, sa[l]["x"], b)
                if has_b:
                    maxima(l, b + 1, 1 - u, 12, H)
                if has_b:
                    split_max(l, b + 1, (u, i + 1))

            def attn(l):
                norm(NORMS[2 * l], split_q(l))
                for n in range(2):
                    for m in range(KT):
                        k_rest(l, n, m)
                maxima(l, 0, 0, 0, H)
                split_max(l, 0, None)
                step(l, 0, 0, 0, False, True, True)
                step(l, 1, 1, 0, True, True, True)
                with dve.Fori(1, B // 2 - 1) as i:
                    for u in range(2):
                        step(l, 2 * i + u, u, i, True, True, True)
                for b in (B - 2, B - 1):
                    step(l, b, b % 2, b // 2, True, False, b + 1 < B)
                divide(l, B - 1)
                add_attention(l, B - 1)
                stats(NORMS[2 * l + 1], B - 1, sa[l]["x"], B)
                stats_end(NORMS[2 * l + 1])

            dve.wait_ge(s_const, NCONST)
            for g in range(NG):
                dve.wait_ge(s_x[g], 16)
                for t in range(GB):
                    x = nc.vector.bn_stats(stat[:, g * GB + t, :], x_sb[:, g * GB + t, :]).then_inc(sn["q0"]["stat"], 1)
            stats_end("q0")
            dve.wait_ge(s_gates, 3)
            attn(0)
            dve.wait_ge(sa[0]["x"], START + B)
            norm("f0", lambda g, u: None)
            route()

            def residual(s, l, g):
                for t in range(GB):
                    b = g * GB + t
                    dve.wait_ge(s["yT"], START + KT * g + t // 2 + 1)
                    nc.vector.scalar_tensor_tensor(x_sb[:, b, :], ps[0:S, 6 + t // 2, (t % 2) * D:(t % 2 + 1) * D],
                                                   gates[0:S, 2 + l:3 + l], x_sb[:, b, :],
                                                   ALU.mult, ALU.add).then_inc(s["x"], 1)
                if l == 0:
                    for t in range(GB):
                        stats("q1", g * GB + t, s["x"], g * GB + t + 1)

            with dve.Fori(0, NG) as g:
                for i in range(NFT0):
                    rows = tile_rows0(i)
                    dve.wait_ge(s0["silu"], START + NFT0 * g + i + 1)
                    dve.wait_ge(s0["u"], START + NFT0 * g + i + 1)
                    if i < 2:
                        dve.wait_ge(s0["y"], START + NFT0 * g)
                        dst = hh[i % 2]
                    else:
                        dve.wait_ge(s0["h"], START + scaled(NFT0 - 1) * g + scaled(max(i - 2, 1)))
                        dst = gu[i % 2]
                    nc.vector.tensor_tensor(dst[0:rows, :], ps[0:rows, 2 + i % 2, 0:GT], sg[i % 2][0:rows, :],
                                            ALU.mult).then_inc(s0["gu"], 1)
                residual(s0, 0, g)
            stats_end("q1")
            dve.wait_ge(s0["x"], START + B)
            attn(1)
            dve.wait_ge(sa[1]["x"], START + B)
            norm("f1", lambda g, u: None)
            choose()
            with dve.Fori(0, NG) as g:
                residual(s1, 1, g)

        @block.tensor
        def _(pe):
            mm = nc.tensor.matmul

            def norm(p, more):
                n = sn[p]
                with pe.Fori(0, NG // 2) as j:
                    for u in range(2):
                        g = 2 * j + u
                        pe.wait_ge(n["xT"], START + g)
                        for t in range(GB):
                            pe.wait_ge(n["xn"], START + GB * g + t + 1)
                            for k in range(KT):
                                x = nc.tensor.transpose(ps[:, 2 * u + k, t * S:(t + 1) * S], xn[:, t, k * P:(k + 1) * P], ident[0:S, 0:S])
                            x.then_inc(n["xnT"], 1)
                        pe.wait_ge(n["xT"], START + g + 1)
                        more(g, u)

            def project_q(l):
                def run(g, u):
                    pe.wait_ge(sq[l]["f32"], START + KT * g)
                    for m in range(KT):
                        for k in range(KT):
                            x = mm(ps[:, 4 + m, 0:GT], w_attn[l]["q"][:, k, m * P:(m + 1) * P], xT[:, k, bass.ds(g * GT, GT)],
                                   start=k == 0, stop=k == KT - 1)
                        x.then_inc(sq[l]["ready"], 1)
                return run

            def logits(s, w, n):
                def run(g, u):
                    pe.wait_ge(s["lg_copied"], START + g)
                    for k in range(KT):
                        x = mm(ps[0:n, 4 + u, 0:GT], w[:, k, :], xT[:, k, bass.ds(g * GT, GT)], start=k == 0, stop=k == KT - 1)
                    x.then_inc(s["lgT"], 1)
                return run

            def project_k(l, n, p, idx, m):
                a, d = sa[l], sd[l]
                if m == 0:
                    pe.wait_ge(d["ctx"][p], (48 if l == 0 else 16) * (idx + 1))
                if not isinstance(n, int) or n >= 2:
                    pe.wait_ge(a["v_copied"], START + 2 * (n - 2) + m + 1)
                elif n == 1:
                    pe.wait_ge(a["k_rest1"], START + m + 1)
                for k in range(KT):
                    x = mm(ps[:, 4 + m, 0:S2], w_attn[l]["k"][:, k, m * P:(m + 1) * P], cT[p][:, k, :],
                           start=k == 0, stop=k == KT - 1)
                x.then_inc(a["k_ready"], 1)

            def project_v(l, n, p, part, last_k):
                a = sa[l]
                pe.wait_ge(a["k_rest1"], START + KT * last_k + part + 1)
                for t in ((0, 1), (2,))[part]:
                    dst = ps[0:KROWS[t], 4 + t // 2, (t % 2) * D:(t % 2 + 1) * D]
                    for k in range(KT):
                        x = mm(dst, cT[p][:, k, t * P:t * P + KROWS[t]], w_attn[l]["v"][:, k, :],
                               start=k == 0, stop=k == KT - 1)
                x.then_inc(a["v_ready"], 1)

            def score(l, n, p, h):
                a = sa[l]
                if not isinstance(n, int) or H * n + h >= 2:
                    pe.wait_ge(a["max"], START + H * n + h + 1 - 2)
                mm(ps[0:S, 2 + h % 2, 0:S2], QS[p][0:SROWS, h, :], KS[p][0:SROWS, h * S2:(h + 1) * S2],
                   start=True, stop=True).then_inc(a["s_ready"], 1)

            def turn_max(l, n, done):
                a = sa[l]
                pe.wait_ge(a["max"], START + H * (n + 1))
                if done is not None:
                    pe.wait_ge(a["msplit"], START + MROWS * n)
                    pe.wait_ge(a["x"], START + done)
                nc.tensor.transpose(ps[0:H, 7, 0:S], mx[:, :], ident[0:S, 0:S]).then_inc(a["mT"], 1)

            def score_T(l, b, p, hg, t):
                a = sa[l]
                c = hg * NKT + t
                pe.wait_ge(a["exp"], START + NKT * NHG * b + c + 1)
                dst = ps[:, c % 2, 0:HQ * S]
                if l == 0:
                    rows = KROWS[t]
                    mm(dst, ident_bf[0:rows, :], bc(biasT[p][0:rows, t, :].unsqueeze(1), [rows, HQ, S]),
                       start=True, stop=False)
                for j in range(HQ):
                    h = HQ * hg + j
                    x = mm(ps[:, c % 2, j * S:(j + 1) * S], KS[p][:, h * S2 + t * P:h * S2 + (t + 1) * P], QS[p][:, h, :],
                           start=l == 1, stop=l == 1 or j == HQ - 1)
                x.then_inc(a["sT"], 1)

            def weigh(l, b, p, hg):
                a = sa[l]
                for t in range(NKT):
                    pe.wait_ge(a["exp"], START + NKT * NHG * b + hg * NKT + t + 1 + 2)
                    for j in range(HQ):
                        x = mm(ps[32 * j:32 * j + HD + 1, 6, hg * S:(hg + 1) * S], V1[p][0:KROWS[t], t, HQ * hg + j, :],
                               prob[0:KROWS[t], t, hg, j * S:(j + 1) * S], start=t == 0, stop=t == NKT - 1)
                x.then_inc(a["pv"], 1)

            def turn_o(l, b, last_n):
                a = sa[l]
                pe.wait_ge(a["o_copied"], START + b + 1)
                pe.wait_ge(a["msplit"], START + MROWS * (last_n + 1))
                pe.wait_ge(a["x"], START + b)
                for hg in range(NHG):
                    x = nc.tensor.transpose(ps[0:S, 7, hg * P:(hg + 1) * P], oT_sb[:, hg * S:(hg + 1) * S], ident[:, :])
                x.then_inc(a["oT"], 1)

            def turn_on(l, b):
                a = sa[l]
                pe.wait_ge(a["on"], START + b + 1)
                if l == 0:
                    pe.wait_ge(a["onv"], START + b + 1)
                for k in range(KT):
                    x = nc.tensor.transpose(ps[:, 7, k * S:(k + 1) * S], onv[:, k * P:(k + 1) * P], ident[0:S, 0:S])
                x.then_inc(a["onT"], 1)

            def project_o(l, b):
                a = sa[l]
                pe.wait_ge(a["onT_copied"], START + b + 1)
                for k in range(KT):
                    x = mm(ps[0:S, 7, D:2 * D], onT[:, k, :], w_attn[l]["o"][:, k, :], start=k == 0, stop=k == KT - 1)
                x.then_inc(a["wo"], 1)

            def step(l, b, u, i, has_o, has_k, has_b):
                a, d = sa[l], sd[l]
                if has_k:
                    project_k(l, b + 2, u, i + 1, 0)
                    project_k(l, b + 2, u, i + 1, 1)
                if has_o:
                    turn_o(l, b - 1, b)
                if l == 0:
                    pe.wait_ge(a["biasT"], START + b + 1)
                pe.wait_ge(d["mload"][u], 16 * MROWS * (i + 1))
                for hg in range(NHG):
                    if has_b and hg % 2 == 0:
                        pe.wait_ge(d["kload"][hg // 2][1 - u], 32 * (i + u + 1))
                    for t in range(NKT):
                        if has_b:
                            score(l, b + 1, 1 - u, HQ * hg + t)
                        score_T(l, b, u, hg, t)
                    if has_b:
                        score(l, b + 1, 1 - u, HQ * hg + NKT)
                    if hg == 0 and has_o:
                        turn_on(l, b - 1)
                    if hg > 0:
                        weigh(l, b, u, hg - 1)
                    if hg == 1 and has_o:
                        project_o(l, b - 1)
                    if hg in (1, 2) and has_b:
                        project_v(l, b + 1, 1 - u, hg - 1, b + 2 if has_k else B - 1)
                weigh(l, b, u, NHG - 1)
                if has_b:
                    turn_max(l, b + 1, b)

            def attn(l):
                pe.wait_ge(s_wa[l], 16 * 4)
                norm(NORMS[2 * l], project_q(l))
                pe.wait_ge(sq[l]["f32"], START + KT * NG)
                pe.sem_inc(sa[l]["exp"], 2)
                pe.sem_inc(sa[l]["pv"], NHG)
                for n in range(2):
                    for m in range(KT):
                        project_k(l, n, n, 0, m)
                for part in range(2):
                    project_v(l, 0, 0, part, 1)
                for half in range(2):
                    pe.wait_ge(sd[l]["kload"][half][0], 32)
                for h in range(H):
                    score(l, 0, 0, h)
                turn_max(l, 0, None)
                step(l, 0, 0, 0, False, True, True)
                step(l, 1, 1, 0, True, True, True)
                with pe.Fori(1, B // 2 - 1) as i:
                    for u in range(2):
                        step(l, 2 * i + u, u, i, True, True, True)
                for b in (B - 2, B - 1):
                    step(l, b, b % 2, b // 2, True, False, b + 1 < B)
                turn_o(l, B - 1, B - 1)
                turn_on(l, B - 1)
                project_o(l, B - 1)

            def turn_y(s, g, copies):
                pe.wait_ge(s["y_copied"], START + copies * (g + 1))
                pe.wait_ge(s["x"], START + GB * g)
                for t in range(GB):
                    for k in range(KT):
                        x = nc.tensor.transpose(ps[0:S, 6 + t // 2, (t % 2) * D + k * P:(t % 2) * D + (k + 1) * P],
                                                yT[:, k, t * S:(t + 1) * S], ident[:, :])
                    if t % 2:
                        x.then_inc(s["yT"], 1)

            pe.wait_ge(s_const, NCONST)
            pe.wait_ge(s_setup, NSETUP)
            pe.wait_ge(s_gates, 3)
            attn(0)
            pe.wait_ge(sa[0]["x"], START + B)
            pe.wait_ge(s_wf[0], 16 * 10)
            norm("f0", logits(s0, Wr, E))
            pe.wait_ge(s0["lg_copied"], START + NG)
            for b in range(B):
                x = nc.tensor.transpose(ps[0:S, 6, b * E:(b + 1) * E], lgT[0:E, b * S:(b + 1) * S], ident[0:E, 0:E])
            x.then_inc(s0["lg"], 1)
            pe.wait_ge(s0["rt"], START + 12)
            for b in range(B):
                x = nc.tensor.transpose(ps[0:E, b // GB, (b % GB) * S:(b % GB + 1) * S], wtok[:, b, :], ident[0:S, 0:S])
            x.then_inc(s0["wT"], 1)
            pe.wait_ge(s0["wT_copied"], START + 1)

            def up0(i, g):
                rows, col = tile_rows0(i), tile_col0(i)
                tok = bass.ds(g * GT, GT)
                pe.wait_ge(s0["silu"], START + NFT0 * g + max(i - 1, 0))
                pe.sem_inc(s_held, 1)
                for k in range(KT):
                    x = mm(ps[0:rows, i % 2, 0:GT], Wg[:, k, col:col + rows], xT[:, k, tok], start=k == 0, stop=k == KT - 1)
                x.then_inc(s0["g"], 1)
                pe.wait_ge(s0["gu"], START + NFT0 * g + max(i - 1, 0))
                pe.sem_inc(s_held, 1)
                for k in range(KT):
                    x = mm(ps[0:rows, 2 + i % 2, 0:GT], Wu[:, k, col:col + rows], xT[:, k, tok], start=k == 0, stop=k == KT - 1)
                x.then_inc(s0["u"], 1)

            def down0(i, g):
                rows = tile_rows0(i)
                if i == 0:
                    pe.wait_ge(s0["y_copied"], START + g)
                if i < 2:
                    pe.wait_ge(s0["gu"], START + NFT0 * g + i + 1)
                else:
                    pe.wait_ge(s0["h"], START + scaled(NFT0 - 1) * g + scaled(i))
                for m in range(KT):
                    x = mm(ps[:, 4 + m, 0:GT], Wd[0:rows, i, m * P:(m + 1) * P], hh[i % 2][0:rows, :],
                           start=i == 0, stop=i == NFT0 - 1)
                x.then_inc(s0["y"], 1)

            with pe.Fori(0, NG) as g:
                for i in range(NFT0):
                    up0(i, g)
                    if i > 1:
                        down0(i - 2, g)
                down0(NFT0 - 2, g)
                down0(NFT0 - 1, g)
                turn_y(s0, g, 1)
            pe.wait_ge(s0["x"], START + B)
            attn(1)
            pe.wait_ge(sa[1]["x"], START + B)
            pe.wait_ge(s_wf[1], 16 * 6)
            norm("f1", logits(s1, WgA, GA))
            pe.wait_ge(s1["lg_copied"], START + NG)
            for b in range(B):
                x = nc.tensor.transpose(ps[0:S, 6 + b // HH, (b % HH) * GA:(b % HH + 1) * GA], lgT[:, b * S:(b + 1) * S], ident[0:GA, 0:GA])
                if b % HH == HH - 1:
                    x.then_inc(s1["lg"], 1)
            pe.wait_ge(s1["rt"], START + 6)
            for b in range(B):
                x = nc.tensor.transpose(ps[0:E1 * R1, b // GB, (b % GB) * S:(b % GB + 1) * S], rm[:, b, :], ident[0:S, 0:S])
            x.then_inc(s1["rT"], 1)
            pe.wait_ge(s1["rT_copied"], START + 1)
            pe.sem_inc(s1["y"], 2)

            def up1(i, g):
                tok = bass.ds(g * GT, GT)
                pe.wait_ge(s1["h"], START + NFT1 * g + max(i - 1, 0))
                for k in range(KT):
                    mm(ps[:, i % 2, 0:GT], wiT[:, k, i * P:(i + 1) * P], xT[:, k, tok], start=k == 0, stop=False)
                mm(ps[:, i % 2, 0:GT], BT[:, i * P:(i + 1) * P], rT[:, tok], start=False, stop=True).then_inc(s1["h_ready"], 1)

            def down1(i, g):
                if i == 0:
                    pe.wait_ge(s1["y_copied"], START + KT * g)
                pe.wait_ge(s1["h"], START + NFT1 * g + i + 1)
                for m in range(KT):
                    x = mm(ps[:, 4 + m, 0:GT], woT[:, i, m * P:(m + 1) * P], hh[i % 2][:, :],
                           start=i == 0, stop=i == NFT1 - 1)
                x.then_inc(s1["y"], 1)

            with pe.Fori(0, NG) as g:
                for i in range(NFT1):
                    up1(i, g)
                    if i > 0:
                        down1(i - 1, g)
                down1(NFT1 - 1, g)
                turn_y(s1, g, KT)


_DIRECT = ["x", "g_xattn", "g_ffn", "L0_xattn_Wv", "L0_xattn_bv", "L0_xattn_Wo", "L0_xattn_bo",
           "L0_ffn_W_gate_router", "L0_ffn_expert_bias", "L0_ffn_Wg", "L0_ffn_Wu", "L0_ffn_Wd", "L0_ffn_Wg_s",
           "L0_ffn_Wu_s", "L0_ffn_Wd_s", "L1_xattn_W_v", "L1_xattn_W_o", "L1_xattn_b_o", "L1_ffn_gate_b",
           "L1_ffn_wi_b", "L1_ffn_wo_b"]


def kernel(**inputs):
    import numpy as np
    import concourse.bacc as bacc
    from concourse.bass_utils import run_bass_kernel_spmd

    a = {n: np.asarray(v) for n, v in inputs.items()}
    lay = {n: a[n] for n in _DIRECT}

    def by_dim(w):
        return w.reshape(w.shape[:-1] + (H, HD)).swapaxes(-1, -2).reshape(w.shape)

    for n in ("L0_xattn_Wq", "L0_xattn_bq", "L0_xattn_Wk", "L0_xattn_bk", "L1_xattn_W_q", "L1_xattn_W_k"):
        lay[n] = by_dim(a[n])
    for n in ("L0_xattn_bq", "L0_xattn_bk"):
        lay[n] = lay[n].reshape(-1, P).T
    for n in ("L1_ffn_wi_b", "L1_ffn_wo_b"):
        lay[n] = a[n].reshape(-1, P).T
    lay["ctxT"] = a["ctx_1024"].reshape(B, S2, KT, P).transpose(0, 3, 2, 1)
    mask = a["mask_Bx1xSxS2_bk1"].reshape(B, S, S2)
    lay["mask"] = mask
    rows = np.zeros((B, NKT * P, S), mask.dtype)
    rows[:, :S2] = mask.transpose(0, 2, 1)
    lay["maskT"] = rows.reshape(B, NKT, P, S).transpose(0, 2, 1, 3)
    lay["gateT"] = a["L1_ffn_gate_W"].T
    lay["loraAT"] = a["L1_ffn_lora_A"].reshape(E1 * R1, D).T
    lay["loraBT"] = a["L1_ffn_lora_B"].transpose(0, 2, 1).reshape(E1 * R1, F1)
    lay["wiT"], lay["woT"] = a["L1_ffn_wi_W"].T, a["L1_ffn_wo_W"].T
    lay["ident"] = np.eye(P, dtype=np.float32)
    lay["iota8"] = np.arange(E, dtype=np.float32)

    nc = bacc.Bacc("TRN2", target_bir_lowering=False, num_devices=1)
    arrays, io = {}, {}
    for n, v in lay.items():
        v = np.ascontiguousarray(v)
        arrays[f"in_{n}"] = v
        io[n] = nc.dram_tensor(f"in_{n}", v.shape, mybir.dt.from_np(v.dtype), kind="ExternalInput").ap()
    out = nc.dram_tensor("out", (B, S, D), F32, kind="ExternalOutput").ap()
    build(nc, io, out)
    r = run_bass_kernel_spmd(nc, [arrays], core_ids=[0])
    return r.results[0]["out"]
```

```python
import concourse.bass as bass
from concourse import mybir
from contextlib import ExitStack

F32 = mybir.dt.float32
F32R = mybir.dt.float32r
BF16 = mybir.dt.bfloat16
U8 = mybir.dt.uint8
U32 = mybir.dt.uint32
ALU = mybir.AluOpType
ACT = mybir.ActivationFunctionType
AX = mybir.AxisListType

B, S, S2, D, H = 16, 100, 361, 256, 16
HD = D // H
P = 128
KT = D // P
HH = H // KT
GB = 4
NG = B // GB
GT = GB * S
NKT = -(-S2 // P)
KROWS = [min(P, S2 - t * P) for t in range(NKT)]
HQ = 4
NHG = H // HQ
SBANKS = (2, 3)
SBANKS0 = (2, 3, 0, 1)
Q3_AT = (7, 10)
QBANK = (0, 2, 6, 6)
E, F = 8, 192
FTOT = F + E * F
NFT0 = -(-F // P) + E * F // P
E1, R1, F1 = 8, 4, 1024
NFT1 = F1 // P
EPS = 1e-5
ROUTE_EPS = 1e-20
MASKED = -1e15
SCALE = float(HD) ** -0.5

KPART = [0, 1, 2, 0, 1, 0]
QPART = [0, 0, 0, 1, 1, 2]
NST = len(KPART)
KRUNS = [(0, 3), (3, 2), (5, 1)]
SROWS = NST * HD
MROWS = 2
KSROWS = SROWS + MROWS


def build(nc, io, out):
    ctx = ExitStack()
    with ctx:
        def sb(name, shape, dt=F32):
            return ctx.enter_context(nc.sbuf_tensor(name, shape, dt))

        def sem(name):
            return ctx.enter_context(nc.semaphore(name))

        def dram(name, shape, dt):
            return nc.dram_tensor(name, shape, dt, kind="Internal").ap()

        ps = ctx.enter_context(nc.psum_tensor("ps", [P, 8, 512], F32))
        x_sb = sb("x_sb", [S, B, D])
        ident = sb("ident", [P, P])
        iota8 = sb("iota8", [S, E])
        w_attn = [{n: sb(f"w{n}{l}", [P, KT, D]) for n in "qko"} for l in range(2)]
        bq4 = [sb(f"bq4_{l}", [P, KT]) for l in range(2)]
        bk = [sb(f"bk_{l}", [P, KT]) for l in range(2)]
        bv_b = sb("bv_b", [S, D])
        bo_b = [sb(f"bo_b{l}", [S, D]) for l in range(2)]
        gates = sb("gates", [P, 4])
        stat = sb("stat", [S, B, 6])
        mean_var = sb("mean_var", [S, B, 2])
        var_eps = sb("var_eps", [S, B])
        rstd = sb("rstd", [S, B])
        neg_half = sb("neg_half", [S, B])
        xn = sb("xn", [S, GB, D])
        xT = sb("xT", [P, KT, B * S])

        scr_q = dram("scr_q", [NST, KT, P, B * S], BF16)
        scr_k = dram("scr_k", [2, NST, KT, P, S2], BF16)
        scr_ones = dram("scr_ones", [MROWS, H * S2 + NKT * P - S2], BF16)
        scr_pad = dram("scr_pad", [SROWS, NKT * P - S2], BF16)
        scr_w = dram("scr_w", [E, B * S], F32)

        s_started = sem("counts_started")
        s_ident = sem("ident_loaded")
        s_bias = sem("key_query_bias_loaded")
        s_const = sem("const_loaded")
        s_x = [sem(f"x_or_router_weights_loaded{g}") for g in range(NG)]
        s_wbc = s_x
        s_wa = [{n: sem(f"attn{l}_w{n}") for n in "kqvo"} for l in range(2)]
        s_wq = [sem(f"wq_scaled{l}") for l in range(2)]
        s_wf = [sem(f"ffn_weights{l}") for l in range(2)]
        s_setup = sem("setup_vec")
        s_gates = sem("gates_ready")
        s_wg = sem("router_and_gate_weights_loaded")
        Q0, F0, Q1, F1N = range(4)
        GE = NG - 1
        NBANKS = ((6, 2, 6, 2), (2, 2, 2, 6), (6, 6, 6, 6), (2, 2, 2, 6))
        LBANK = (4, 5, 4, 6)
        PARTS = ((0, GE), (GE, NG))
        LORA_RUNS = ((0, 1), (1, GE), (GE, NG))
        NORM_AT = (6, 8, 10)
        sn = {n: sem(f"norm_{n}") for n in ("stat", "mv", "veps", "rstd", "xn", "xnT", "xT")}
        sq = [{n: sem(f"q_{n}{u}") for n in ("ready", "q1", "rest1", "q2", "q3", "stored")} for u in range(2)]
        JQ = NG // 2
        AN = ("k_ready", "k1", "k_rest1", "k2", "k3", "v_ready", "v_copied", "bias", "biasT", "s_ready", "max",
              "mhi", "msplit", "mT", "mp", "sT", "exp", "pv", "o_copied", "oT", "rec", "on", "onv", "onT", "onT_copied", "wo",
              "addb", "x")
        sa = [{n: sem(f"a{l}_{n}") for n in AN if l == 0 or n not in ("bias", "biasT", "onv")} for l in range(2)]
        sd = {n: [sem(f"a_{n}{p}") for p in range(2)] for n in ("ctx", "kst", "mload")}
        sd["kload"] = [[sem(f"a_kload{half}{p}") for p in range(2)] for half in range(2)]
        s_mask = [sem(f"mask_loaded{p}") for p in range(2)]
        sc_hi, sc_lo = sem("context_hi"), sem("context_lo")
        IB = B // 2
        s0 = {n: sem(f"f0_{n}") for n in ("lgT", "lg_copied", "lg", "sc", "rt", "wT", "wT_copied", "w_stored",
                                          "g", "u", "silu", "gu", "h", "y", "y_copied", "yT", "x",
                                          "whi", "wlo", "xh", "xl", "hi", "lo")}
        s1 = {n: sem(f"f1_{n}") for n in ("lgT", "lg_copied", "lg", "rt", "rT", "rT_copied", "h_ready", "h", "y",
                                          "y_copied", "yT", "x", "whi", "wlo", "xh", "xl", "hi", "lo", "rTl")}
        s_ones = sem("ones_kept")
        s_rows = sem("stack_rows_restored")
        s_vones = sem("value_ones_restored")
        s_out = sem("out_stored")

        GA = E1 * R1 + E1
        T = {}

        def overlay(place, *groups):
            base, end = nc.sbuf_base, nc.sbuf_base
            for group in groups:
                with ExitStack() as scope:
                    for name, shape, dt in group:
                        T[name] = scope.enter_context(nc.sbuf_tensor(name, shape, dt))
                    end = max(end, nc.sbuf_base)
            ctx.enter_context(nc.sbuf_tensor(place, [P, (end - base) // 4], F32))

        def asb(name, shape, dt=F32):
            return ctx.enter_context(nc.sbuf_tensor(name, shape, dt))

        overlay("parts_place",
                [("kp", [P, 3, KT, S2], BF16), ("kr", [P, KT, S2], F32)]
                + [(f"qr{u}", [P, KT, GT], F32) for u in range(2)] + [(f"qp{u}", [P, 3, KT, GT], BF16) for u in range(2)],
                [("lgT", [GA, B * S], F32), ("wrT", [E1 * R1, B * S], F32)] + [(f"gu{p}", [P, GT], F32) for p in range(2)]
                + [(f"hh{p}", [P, GT], F32) for p in range(2)] + [("yT", [P, KT, GT], F32)],
                [("lgT_place", [GA, B * S], F32), ("wrT_place", [E1 * R1, B * S], F32)]
                + [(f"gu{p}_place", [P, GT], F32) for p in range(2)] + [(f"hlo{p}", [P, GT], F32R) for p in range(2)])
        overlay("weight_place",
                [("Wg", [P, KT, FTOT], F32), ("Wu", [P, KT, FTOT], F32), ("Wd", [P, NFT0, D], F32)],
                [("Wgl", [P, KT, FTOT], F32R), ("Wul", [P, KT, FTOT], F32R), ("Wdl", [P, NFT0, D], F32R)],
                [("wiT", [P, KT, F1], F32), ("woT", [P, NFT1, D], F32), ("BT", [E1 * R1, F1], F32)],
                [("wil", [P, KT, F1], F32R), ("wol", [P, NFT1, D], F32R), ("BTl", [E1 * R1, F1], F32R)])
        overlay("prob_place",
                [("prob", [P, NKT, NHG, HQ * S], F32)],
                [("wbc", [P, E, GT], F32), ("xh", [P, KT, GT], F32R), ("xl", [P, KT, GT], F32R)])
        overlay("stack_place",
                [t for p in range(2) for t in (
                    (f"KS{p}", [KSROWS, H * S2 + NKT * P - S2], BF16), (f"QS{p}", [KSROWS, H, S], BF16),
                    (f"V1_{p}", [P, NKT, H, HD + 1], F32), (f"masku{p}", [S, S2], U8), (f"maskTu{p}", [P, NKT, S], U8),
                    (f"biasq{p}", [S, S2], BF16), (f"biasT{p}", [P, NKT, S], BF16))]
                + [("oT_sb", [P, HQ * S], F32), ("on", [S, D], F32), ("onv", [S, D], F32), ("onT", [P, KT, S], F32),
                   ("xb", [S, D], F32)],
                [(f"hhi{p}", [P, GT], F32R) for p in range(2)]
                + [("Wgh", [P, KT, FTOT], F32R), ("Wuh", [P, KT, FTOT], F32R), ("Wdh", [P, NFT0, D], F32R)],
                [(f"hhi{p}_place", [P, GT], F32) for p in range(2)]
                + [("wih", [P, KT, F1], F32R), ("BTh", [E1 * R1, F1], F32R), ("woh", [P, NFT1, D], F32R),
                   ("rTh", [E1 * R1, B * S], F32R), ("rTl", [E1 * R1, B * S], F32R)])
        kp, kr, lgT, yT, prob, wbc, xh, xl = (T[n] for n in ("kp", "kr", "lgT", "yT", "prob", "wbc", "xh", "xl"))
        qr, qp, gu, hh, hlo, hhi, KS, QS, masku, maskTu, biasq, biasT = (
            [T[f"{n}{p}"] for p in range(2)]
            for n in ("qr", "qp", "gu", "hh", "hlo", "hhi", "KS", "QS", "masku", "maskTu", "biasq", "biasT"))
        V1 = [T[f"V1_{p}"] for p in range(2)]
        wT, wrT = T["wrT"][0:E, :], T["wrT"]
        Wg, Wu, Wd, Wgh, Wuh, Wdh, Wgl, Wul, Wdl = (T[f"W{n}{part}"] for part in ("", "h", "l") for n in "gud")
        wiT, woT, BT, wih, woh, BTh, wil, wol, BTl = (
            T[n] for n in ("wiT", "woT", "BT", "wih", "woh", "BTh", "wil", "wol", "BTl"))
        rTh, rTl, oT_sb, on, onv, onT, xb = (T[n] for n in ("rTh", "rTl", "oT_sb", "on", "onv", "onT", "xb"))

        overlay("context_place",
                [(f"cT{p}", [P, KT, NKT * P], F32) for p in range(2)] + [(f"wv{l}", [P, KT, D], F32) for l in range(2)],
                [(f"cTl{p}", [P, KT, NKT * P], F32R) for p in range(2)] + [(f"wvl{l}", [P, KT, D], F32R) for l in range(2)])
        cT, cTl = ([T[f"{n}{p}"] for p in range(2)] for n in ("cT", "cTl"))
        cTh = [asb(f"cTh{p}", [P, KT, NKT * P], F32R) for p in range(2)]
        wvh = asb("wvh", [P, KT, D], F32R)
        wvl = [T[f"wvl{l}"] for l in range(2)]
        for l in range(2):
            w_attn[l]["v"] = T[f"wv{l}"]
        mx = asb("mx", [S, H])
        mxb = asb("mxb", [S, H], BF16)
        mxs = asb("mxs", [S, MROWS * H])
        mp = asb("mp", [MROWS * H, S], BF16)
        ident_bf = asb("ident_bf", [P, P], BF16)
        rec = asb("rec", [S, H])
        ahead = asb("ahead", [P, 1])

        Wr = asb("Wr", [P, KT, E])
        ebias = asb("ebias", [S, E])
        sc = asb("sc", [S, B, E])
        bsc = asb("bsc", [S, B, E])
        mx8 = asb("mx8", [S, B, 8])
        ix8 = asb("ix8", [S, B, 8], U32)
        ixf = asb("ixf", [S, B, 2])
        oh = asb("oh", [S, 2, B, E])
        wsel = asb("wsel", [S, B, E])
        wsum = asb("wsum", [S, B])
        wrec = asb("wrec", [S, B])
        wtok = asb("wtok", [S, B, E])
        sg = [asb(f"sg{p}", [P, GT]) for p in range(2)]
        WgA = asb("WgA", [P, KT, GA])
        gb_b = asb("gb_b", [S, E1])
        wib = asb("wib", [P, NFT1])
        wob = asb("wob", [P, KT])
        rm = asb("rm", [S, B, E1 * R1])

        EARLY = ([(Wgh[:, k, :], Wg[:, k, :], Wgl[:, k, :]) for k in range(KT)],
                 [(wih[:, :, :], wiT[:, :, :], wil[:, :, :]), (BTh[:, :], BT[:, :], BTl[:, :])])

        def bc(ap, shape):
            return ap.to_broadcast(shape)

        def tile_rows0(i):
            return F - P if i == 1 else P

        def scaled(i):
            return sum(1 + (t * P // F != (t * P + P - 1) // F) for t in range(i - 1))

        def tile_col0(i):
            return i * P if i < 2 else F + (i - 2) * P

        NCONST = 16 * 9
        NSETUP = 9

        s_held = sem("held_waits")
        START = 1
        def v_parts(l, n):
            return START + l * (B + 1) + n + 2

        def ctx_width(l, n):
            return NKT * P if l == 0 and isinstance(n, int) and n < 2 else S2

        COUNTED = [sc_hi, sc_lo] + [v for d in (sn, *sq, sa[0], s0, sa[1], s1) for v in d.values()]

        block = ctx.enter_context(nc.Block())

        @block.sync
        def _(sp):
            def ctx_load(l, n, p, fresh):
                a, d = sa[l], sd
                if not fresh:
                    sp.wait_ge(a["v_ready"], START + 2 * (n - 1))
                    sp.sem_inc(s_held, 1)
                sp.dma_start(cT[p][:, :, 0:S2], io["ctxT"][n]).then_inc(d["ctx"][p], 16)

            def mask_load(n, p, fresh):
                if not fresh:
                    sp.wait_ge(sa[0]["biasT"], START + n - 1)
                    sp.sem_inc(s_held, 1)
                sp.dma_start(masku[p][:, :], io["mask"][n]).then_inc(s_mask[p], 16)
                sp.dma_start(maskTu[p][:, :, :], io["maskT"][n]).then_inc(s_mask[p], 16)

            def k_store(l, n, p, idx):
                a, d = sa[l], sd
                if idx > 0 if isinstance(idx, int) else True:
                    for half in range(2):
                        sp.wait_ge(d["kload"][half][p], 32 * idx)
                for j, parts in reversed(KRUNS):
                    if parts == 1:
                        sp.wait_ge(a["k1"], START + KT * (n + 1))
                    elif parts == 2:
                        sp.wait_ge(a["k2"], START + n + 1)
                    else:
                        sp.wait_ge(a["k3"], START + n + 1)
                    sp.sem_inc(s_held, 1)
                    sp.dma_start(scr_k[p, j:j + parts].rearrange("j k p n -> p (j k) n"),
                                 kp[:, 0:parts, :, :].rearrange("p j k n -> p (j k) n")).then_inc(d["kst"][p], 16)

            def k_load(l, n, p, idx, half, fresh):
                a, d = sa[l], sd
                if half == 0:
                    sp.wait_ge(d["kst"][p], 16 * len(KRUNS) * (idx + 1))
                    sp.sem_inc(s_held, 1)
                if not fresh:
                    sp.wait_ge(a["sT"], START + NKT * NHG * (n - 2) + NKT * NHG // 2 * (half + 1))
                    sp.sem_inc(s_held, 1)
                c = slice(half * HH * S2, (half + 1) * HH * S2)
                sp.dma_start(KS[p][0:SROWS, c],
                             scr_k[p].rearrange("j k (d h) n -> (j k d) (h n)", h=H)[:, c]).then_inc(d["kload"][half][p], 16)

            def q_load(l, n, p, half):
                hs = slice(half * HH, (half + 1) * HH)
                sp.dma_start(QS[p][0:SROWS, hs, :],
                             scr_q[:, :, :, bass.ds(n * S, S)].rearrange("j k (d h) n -> (j k d) h n", h=H)[:, hs]).then_inc(sd["kload"][half][p], 16)

            def q_store(l, g):
                u = g % 2
                q = sq[u]
                for r in range(NST):
                    if QPART[r] == 0:
                        sp.wait_ge(q["q1"], START + KT * (l * JQ + g // 2 + 1))
                    elif QPART[r] == 1:
                        sp.wait_ge(q["q2"], START + l * JQ + g // 2 + 1)
                    else:
                        sp.wait_ge(q["q3"], START + l * JQ + g // 2 + 1)
                    sp.dma_start(scr_q[r, :, :, g * GT:(g + 1) * GT].rearrange("k p n -> p k n"),
                                 qp[u][:, QPART[r], :, :]).then_inc(q["stored"], 16)

            def x_load():
                for g in range(NG):
                    sp.dma_start(x_sb[:, g * GB:(g + 1) * GB, :],
                                 io["x"][g * GB:(g + 1) * GB].rearrange("b s d -> s b d")).then_inc(s_x[g], 16)

            def small_vectors():
                sp.dma_start(bv_b[:, :], io["L0_xattn_bv"].partition_broadcast(S)).then_inc(s_const, 16)
                sp.dma_start(bo_b[0][:, :], io["L0_xattn_bo"].partition_broadcast(S)).then_inc(s_const, 16)
                sp.dma_start(bo_b[1][:, :], io["L1_xattn_b_o"].partition_broadcast(S)).then_inc(s_const, 16)
                sp.dma_start(gates[:, 0:2], io["g_xattn"].partition_broadcast(P)).then_inc(s_const, 16)
                sp.dma_start(gates[:, 2:4], io["g_ffn"].partition_broadcast(P)).then_inc(s_const, 16)
                sp.dma_start(iota8[:, :], io["iota8"].partition_broadcast(S)).then_inc(s_const, 16)
                sp.dma_start(ebias[:, :], io["L0_ffn_expert_bias"].partition_broadcast(S)).then_inc(s_const, 16)
                sp.dma_start(gb_b[:, :], io["L1_ffn_gate_b"].partition_broadcast(S)).then_inc(s_const, 16)
                sp.dma_start(wob[:, :], io["L1_ffn_wo_b"]).then_inc(s_const, 16)

            def ffn0_weights(j):
                if j == 0:
                    sp.dma_start(Wr[:, :, :], io["L0_ffn_W_gate_router"].rearrange("(k p) e -> p k e", p=P)).then_inc(s_wg, 16)
                w, sh, ro = ((Wg, "L0_ffn_Wg_s", "L0_ffn_Wg"), (Wu, "L0_ffn_Wu_s", "L0_ffn_Wu"))[j]
                loaded = (s_wg, s_wf[0])[j]
                sp.dma_start(w[:, :, 0:F], io[sh].rearrange("(k p) f -> p k f", p=P)).then_inc(loaded, 16)
                for k in range(KT):
                    sp.dma_start(w[:, k, F:FTOT].rearrange("p (e f) -> p e f", e=E),
                                 io[ro][:, k * P:(k + 1) * P].rearrange("e p f -> p e f")).then_inc(loaded, 16)

            def later_weights():
                ffn0_weights(1)
                sp.dma_start(Wd[:, 0, :], io["L0_ffn_Wd_s"][0:P]).then_inc(s_wf[0], 16)
                sp.dma_start(Wd[0:F - P, 1, :], io["L0_ffn_Wd_s"][P:F]).then_inc(s_wf[0], 16)
                sp.dma_start(Wd[:, 2:, :], io["L0_ffn_Wd"].rearrange("e f d -> (e f) d").rearrange("(t p) d -> p t d", p=P)).then_inc(s_wf[0], 16)
                for n in "kqvo":
                    sp.dma_start(w_attn[1][n][:, :, :], io[f"L1_xattn_W_{n}"].rearrange("(k p) n -> p k n", p=P)).then_inc(s_wa[1][n], 16)
                sp.dma_start(WgA[:, :, 0:E1 * R1], io["loraAT"].rearrange("(k p) n -> p k n", p=P)).then_inc(s_wf[1], 16)
                sp.dma_start(WgA[:, :, E1 * R1:GA], io["gateT"].rearrange("(k p) n -> p k n", p=P)).then_inc(s_wf[1], 16)
                sp.dma_start(wib[:, :], io["L1_ffn_wi_b"]).then_inc(s_wf[1], 16)

            def step(l, b, u, i, has_ctx, has_k):
                if has_k:
                    k_store(l, b + 2, u, i + 1)
                if has_ctx:
                    ctx_load(l, b + 3, 1 - u, False)
                if has_k:
                    for half in range(2):
                        k_load(l, b + 2, u, i + 1, half, False)
                        q_load(l, b + 2, u, half)
                if l == 0 and has_ctx:
                    mask_load(b + 3, 1 - u, False)

            def attn(l):
                if l == 1:
                    sp.wait_ge(sa[0]["x"], START + B)
                ctx_load(l, 0, 0, True)
                if l == 0:
                    x_load()
                ctx_load(l, 1, 1, True)
                if l == 0:
                    for n in range(2):
                        mask_load(n, n, True)
                    small_vectors()
                    sp.wait_ge(s_started, 3)
                    sp.wait_ge(s_setup, NSETUP)
                    sp.dma_start(KS[0][SROWS:KSROWS, :], KS[1][SROWS:KSROWS, :]).then_inc(s_rows, 16)
                    sp.dma_start(KS[0][0:SROWS, H * S2:], KS[1][0:SROWS, H * S2:]).then_inc(s_rows, 16)
                    sp.dma_start(scr_ones, KS[1][SROWS:KSROWS, :]).then_inc(s_ones, 16)
                    sp.dma_start(scr_pad, KS[1][0:SROWS, H * S2:]).then_inc(s_ones, 16)
                if l == 1:
                    sp.wait_ge(s0["y"], START + NFT0 * NG)
                    sp.wait_ge(s_ones, 32)
                    for p in range(2):
                        sp.dma_start(KS[p][SROWS:KSROWS, :], scr_ones).then_inc(s_rows, 16)
                        sp.dma_start(KS[p][0:SROWS, H * S2:], scr_pad).then_inc(s_rows, 16)
                k_store(l, 0, 0, l * IB)
                q_store(l, 0)
                ctx_load(l, 2, 0, False)
                for half in range(2):
                    k_load(l, 0, 0, l * IB, half, True)
                sp.wait_ge(sq[0]["stored"], START + 16 * NST * (l * JQ + 1))
                for half in range(2):
                    q_load(l, 0, 0, half)
                k_store(l, 1, 1, l * IB)
                q_store(l, 1)
                for half in range(2):
                    k_load(l, 1, 1, l * IB, half, True)
                    q_load(l, 1, 1, half)
                if l == 0:
                    mask_load(2, 0, False)
                for g in range(2, NG):
                    q_store(l, g)
                for u in range(2):
                    sp.wait_ge(sq[u]["stored"], START + 16 * NST * JQ * (l + 1))
                with sp.Fori(0, B // 2 - 2) as i:
                    for u in range(2):
                        step(l, 2 * i + u, u, i + l * IB, True, True)
                for b in range(B - 4, B - 2):
                    if l == 0 and b == B - 4:
                        ffn0_weights(0)
                    step(l, b, b % 2, b // 2 + l * IB, b + 3 < B, True)
                if l == 0:
                    later_weights()

            attn(0)
            def store_router(part):
                t = slice(PARTS[part][0] * GT, PARTS[part][1] * GT)
                sp.wait_ge(s0["wT_copied"], START + part + 1)
                sp.dma_start(scr_w[:, t], wT[:, t]).then_inc(s0["w_stored"], 16)
                sp.wait_ge(s0["w_stored"], START + 16 * (part + 1))

            def load_router(g):
                for j in range(E // 2):
                    e = slice(2 * j, 2 * j + 2)
                    sp.dma_start(wbc[:, e, :], scr_w[e, bass.ds(g * GT, GT)].partition_broadcast(P)).then_inc(s_wbc[j], 16)

            store_router(0)
            load_router(0)
            store_router(1)
            with sp.Fori(1, NG) as g:
                sp.wait_ge(s0["h"], START + scaled(NFT0 - 1) * g)
                sp.sem_inc(s_held, 1)
                load_router(g)
            attn(1)
            with sp.Fori(0, NG) as g:
                sp.wait_ge(s1["x"], START + GB * (g + 1))
                sp.sem_inc(s_held, 1)
                sp.dma_start(out[bass.ds(g * GB, GB)].rearrange("b s d -> s b d"),
                             x_sb[:, bass.ds(g * GB, GB), :]).then_inc(s_out, 16)
            sp.wait_ge(s_out, 16 * NG)

        @block.gpsimd
        def _(pool):
            nc.gpsimd.memset(neg_half[:, :], -0.5).then_inc(s_setup, 1)
            for c in COUNTED[0::3]:
                pool.sem_inc(c, START)
            pool.sem_inc(s_started, 1)
            pool.wait_ge(s_started, 3)

            def norm(p, g):
                t = slice(g * GB, (g + 1) * GB)
                pool.wait_ge(sn["mv"], START + B * p + GB * (g + 1))
                nc.gpsimd.tensor_scalar(var_eps[:, t], mean_var[:, t, 1], EPS, None, ALU.add).then_inc(sn["veps"], 1)
                pool.wait_ge(sn["veps"], START + NG * p + g + 1)
                nc.gpsimd.tensor_tensor(rstd[:, t], var_eps[:, t], neg_half[:, t], ALU.pow).then_inc(sn["rstd"], 1)

            def bias(n, p, idx, fresh):
                a, d = sa[0], sd
                pool.wait_ge(s_mask[p], 32 * (idx + 1))
                pool.sem_inc(s_held, 1)
                if not fresh:
                    pool.wait_ge(a["max"], START + H * (n - 1))
                    pool.sem_inc(s_held, 1)
                nc.gpsimd.tensor_scalar(biasq[p][:, :], masku[p][:, :], MASKED, None, ALU.mult).then_inc(a["bias"], 1)

            def biasT_(n, p, fresh):
                a, d = sa[0], sd
                if not fresh:
                    pool.wait_ge(a["sT"], START + 3 * NHG * (n - 1))
                    pool.sem_inc(s_held, 1)
                nc.gpsimd.tensor_scalar(biasT[p][:, :, :], maskTu[p][:, :, :], MASKED, None, ALU.mult).then_inc(a["biasT"], 1)

            def k3(l, n):
                a = sa[l]
                pool.wait_ge(a["k2"], START + n + 1)
                nc.gpsimd.tensor_tensor(kp[:, 2, :, :], kr[:, :, :], kp[:, 1, :, :], ALU.subtract).then_inc(a["k3"], 1)

            def attn(l):
                def split_q(g):
                    u = g % 2
                    q = sq[u]
                    pool.wait_ge(q["q2"], START + l * JQ + g // 2 + 1)
                    nc.gpsimd.tensor_tensor(qp[u][:, 2, :, :], qr[u][:, :, :], qp[u][:, 1, :, :], ALU.subtract).then_inc(q["q3"], 1)

                if l == 0:
                    nc.gpsimd.memset(KS[1][:, :], 1.0).then_inc(s_setup, 1)
                    for p in range(2):
                        nc.gpsimd.memset(V1[p][:, :, :, :], 1.0).then_inc(s_setup, 1)
                    for g in range(NG - 1):
                        norm(Q0, g)
                    k3(l, 0)
                    norm(Q0, NG - 1)
                    split_q(0)
                    bias(0, 0, 0, True)
                else:
                    pool.wait_ge(s0["y"], START + NFT0 * NG)
                    for p in range(2):
                        nc.gpsimd.memset(V1[p][:, :, :, HD:HD + 1], 1.0).then_inc(s_vones, 1)
                    k3(l, 0)
                    split_q(0)
                    norm(Q1, GE)
                k3(l, 1)
                split_q(1)
                if l == 0:
                    biasT_(0, 0, True)
                    bias(1, 1, 0, True)
                split_q(2)
                split_q(3)
                if l == 0:
                    biasT_(1, 1, True)
                with pool.Fori(0, B // 2 - 1) as i:
                    for u in range(2):
                        n = 2 * i + u + 2
                        k3(l, n)
                        if l == 0:
                            bias(n, u, i + 1, False)
                            biasT_(n, u, False)
                for g in range(GE):
                    norm(2 * l + 1, g)

            attn(0)
            pool.wait_ge(sa[0]["x"], START + B)
            norm(F0, GE)

            def scale_hidden(g, last):
                for i in range(2, NFT0):
                    pool.wait_ge(s0["gu"], START + NFT0 * g + i + 1)
                    pool.wait_ge(s0["y"], START + NFT0 * g + i - 1)
                    e = (i - 2) * P // F
                    pool.wait_ge(s_wbc[e // 2], 16 + 16 * (g + 1))
                    own = scaled(NFT0 - 1) * g + scaled(i - 1)
                    if i > 2:
                        pool.wait_ge(s0["h"], START + own)
                    if ((i - 2) * P + P - 1) // F == e:
                        nc.gpsimd.tensor_tensor(hh[i % 2][:, :], gu[i % 2][:, :], wbc[:, e, :], ALU.mult).then_inc(s0["h"], 1)
                    else:
                        half = F * (e + 1) - (i - 2) * P
                        nc.gpsimd.tensor_tensor(hh[i % 2][0:half, :], gu[i % 2][0:half, :], wbc[0:half, e, :],
                                                ALU.mult).then_inc(s0["h"], 1)
                        pool.wait_ge(s_wbc[(e + 1) // 2], 16 + 16 * (g + 1))
                        pool.wait_ge(s0["h"], START + own + 1)
                        nc.gpsimd.tensor_tensor(hh[i % 2][half:P, :], gu[i % 2][half:P, :], wbc[half:P, e + 1, :],
                                                ALU.mult).then_inc(s0["h"], 1)
                    if last and i + 3 in NORM_AT:
                        pool.wait_ge(s0["h"], START + scaled(NFT0 - 1) * g + scaled(i))
                        norm(Q1, NORM_AT.index(i + 3))
                        pool.wait_ge(sn["rstd"], START + NG * Q1 + NORM_AT.index(i + 3) + 1)

            with pool.Fori(0, NG - 1) as g:
                scale_hidden(g, False)
            scale_hidden(NG - 1, True)
            attn(1)
            pool.wait_ge(sa[1]["x"], START + B)
            norm(F1N, GE)

        @block.scalar
        def _(act):
            w0 = [w_attn[0][n] for n in "kqvo"]
            act.dma_start(w0[0][:, :, :], io["L0_xattn_Wk"].rearrange("(k p) n -> p k n", p=P)).then_inc(s_wa[0]["k"], 16)
            act.dma_start(bk[0][:, :], io["L0_xattn_bk"]).then_inc(s_bias, 16)
            act.dma_start(bq4[0][:, :], io["L0_xattn_bq"]).then_inc(s_bias, 16)
            act.dma_start(ident[:, :], io["ident"]).then_inc(s_ident, 16)
            act.dma_start(w0[1][:, :, :], io["L0_xattn_Wq"].rearrange("(k p) n -> p k n", p=P)).then_inc(s_wa[0]["q"], 16)
            act.dma_start(w0[2][:, :, :], io["L0_xattn_Wv"].rearrange("(k p) n -> p k n", p=P)).then_inc(s_wa[0]["v"], 16)
            act.dma_start(w0[3][:, :, :], io["L0_xattn_Wo"].rearrange("(k p) n -> p k n", p=P)).then_inc(s_wa[0]["o"], 16)
            act.wait_ge(s_started, 3)
            act.wait_ge(s_bias, 32)
            nc.scalar.activation(bq4[0][:, :], bq4[0][:, :], ACT.Copy, scale=SCALE).then_inc(s_wq[0], 1)

            def norm(p, g):
                act.wait_ge(sn["xnT"], START + GB + B * p + GB * (g + 1))
                bank = NBANKS[p][g]
                nc.scalar.activation(xT[:, :, g * GT:(g + 1) * GT], ps[:, bank:bank + KT, 0:GT], ACT.Copy).then_inc(sn["xT"], 1)

            def scale_q(l):
                act.wait_ge(s_wa[l]["q"], 16)
                nc.scalar.activation(w_attn[l]["q"][:, :, :], w_attn[l]["q"][:, :, :], ACT.Copy, scale=SCALE).then_inc(s_wq[l], 1)

            def q_first(l, g):
                u, j = g % 2, g // 2
                q = sq[u]
                act.wait_ge(q["stored"], START + 16 * NST * (l * JQ + j))
                for m in range(KT):
                    act.wait_ge(q["ready"], START + KT * (l * JQ + j) + m + 1)
                    nc.scalar.activation(qp[u][:, 0, m, :], ps[:, QBANK[g] + m, 0:GT], ACT.Identity,
                                         bias=bq4[l][:, m:m + 1]).then_inc(q["q1"], 1)

            def q_second(l, g):
                u, j = g % 2, g // 2
                q = sq[u]
                act.wait_ge(q["rest1"], START + KT * (l * JQ + j + 1))
                nc.scalar.activation(qp[u][:, 1, :, :], qr[u][:, :, :], ACT.Copy).then_inc(q["q2"], 1)

            def copy_logits(l, g):
                s, n = ffn[l], (E, GA)[l]
                act.wait_ge(s["lgT"], START + g + 1)
                nc.scalar.activation(lgT[0:n, g * GT:(g + 1) * GT], ps[0:n, LBANK[g], 0:GT], ACT.Copy).then_inc(s["lg_copied"], 1)

            def ctx_high(l, n, p, idx):
                act.wait_ge(sd["ctx"][p], 16 * (idx + 1))
                c = ctx_width(l, n)
                nc.scalar.activation(cTh[p][:, :, 0:c], cT[p][:, :, 0:c], ACT.Copy).then_inc(sc_hi, 1)

            def split_first(l):
                act.wait_ge(s_wa[l]["v"], 16)
                nc.scalar.activation(wvh[:, :, :], w_attn[l]["v"][:, :, :], ACT.Copy).then_inc(sc_hi, 1)
                ctx_high(l, 0, 0, l * IB)

            def k_first(l, n, m, stored):
                a, d = sa[l], sd
                if m == 0 and stored is not None:
                    act.wait_ge(d["kst"][stored[0]], 16 * len(KRUNS) * stored[1])
                act.wait_ge(a["k_ready"], START + KT * n + m + 1)
                nc.scalar.activation(kp[:, 0, m, :], ps[:, 4 + m, 0:S2], ACT.Identity, bias=bk[l][:, m:m + 1]).then_inc(a["k1"], 1)

            def k_second(l, n):
                a = sa[l]
                act.wait_ge(a["k_rest1"], START + KT * (n + 1))
                nc.scalar.activation(kp[:, 1, :, :], kr[:, :, :], ACT.Copy).then_inc(a["k2"], 1)

            def v_copy(l, n, p, part):
                a = sa[l]
                act.wait_ge(a["v_ready"], START + 2 * n + part + 1)
                if part == 0:
                    nc.scalar.activation(V1[p][:, 0:2, :, 0:HD],
                                         ps[:, 4, :].rearrange("p (t h e) -> p t h e", t=2, h=H), ACT.Copy).then_inc(a["v_copied"], 1)
                else:
                    nc.scalar.activation(V1[p][0:KROWS[2], 2, :, 0:HD],
                                         ps[0:KROWS[2], 5, 0:D].rearrange("p (h e) -> p h e", h=H), ACT.Copy).then_inc(a["v_copied"], 1)

            def copy_o(l, b):
                a = sa[l]
                act.wait_ge(a["pv"], START + NHG * (b + 2))
                nc.scalar.activation(oT_sb[:, :], ps[:, 6, 0:HQ * S], ACT.Copy).then_inc(a["o_copied"], 1)

            def copy_on(l, b):
                a = sa[l]
                act.wait_ge(a["onT"], START + b + 1)
                nc.scalar.activation(onT[:, :, :], ps[:, 7, 0:KT * S], ACT.Copy).then_inc(a["onT_copied"], 1)

            def exps(l, b, hg, tiles):
                a = sa[l]
                if 0 in tiles:
                    act.wait_ge(a["pv"], START + NHG * b + hg + 1)
                for t in tiles:
                    c = hg * NKT + t
                    act.wait_ge(a["sT"], START + NKT * NHG * b + c + 1)
                    nc.scalar.activation(prob[0:KROWS[t], t, hg, :], ps[0:KROWS[t], c % 2, 0:HQ * S],
                                         ACT.Exp).then_inc(a["exp"], 1)

            def max_load(l, n, p, loaded, bank):
                a, d = sa[l], sd
                act.wait_ge(a["mT"], START + n + 1)
                if loaded is not None:
                    act.wait_ge(d["mload"][loaded[0]], 16 * loaded[1])
                nc.scalar.activation(mp[:, :], ps[0:MROWS * H, bank, 0:S], ACT.Copy).then_inc(a["mp"], 1)
                act.wait_ge(a["mp"], START + n + 1)
                act.dma_start(QS[p][SROWS:KSROWS, :, :], mp[:, :]).then_inc(d["mload"][p], 16)

            def step(l, b, u, i, has_o, has_k, has_2, has_b):
                exps(l, b, 0, (0,))
                if has_2:
                    k_second(l, b + 2)
                exps(l, b, 0, (1, 2))
                if has_o:
                    copy_on(l, b - 1)
                exps(l, b, 1, range(NKT))
                if has_b:
                    for part in range(2):
                        v_copy(l, b + 1, 1 - u, part)
                    if has_2:
                        ctx_high(l, b + 2, u, i + 1)
                else:
                    high(ffn[l], *EARLY[l][1][:2])
                    norm(2 * l + 1, 0)
                exps(l, b, 2, range(NKT))
                if not has_b:
                    norm(2 * l + 1, 1)
                exps(l, b, 3, range(NKT))
                if has_b:
                    max_load(l, b + 1, 1 - u, (u, i + 1), 7)
                if has_k:
                    k_first(l, b + 3, 0, (u, i + 2))
                copy_o(l, b)
                if has_k:
                    k_first(l, b + 3, 1, None)

            def attn(l):
                if l == 1:
                    act.wait_ge(s0["w_stored"], START + 32)
                for m in range(KT):
                    k_first(l, 0, m, (1, IB) if l else None)
                if l == 0:
                    scale_q(l)
                k_second(l, 0)
                if l == 0:
                    norm(Q0, 0)
                    act.wait_ge(s_setup, NSETUP)
                    split_first(0)
                    norm(Q0, 1)
                q_first(l, 0)
                q_second(l, 0)
                if l == 0:
                    norm(Q0, 2)
                    norm(Q0, 3)
                for part in range(2):
                    v_copy(l, 0, 0, part)
                if l == 0:
                    ctx_high(0, 1, 1, 0)
                for m in range(KT):
                    k_first(l, 1, m, (0, l * IB + 1))
                k_second(l, 1)
                q_first(l, 1)
                if l == 1:
                    norm(Q1, GE)
                q_second(l, 1)
                if l == 0:
                    act.wait_ge(s_ident, 16)
                    nc.scalar.activation(ident_bf[:, :], ident[:, :], ACT.Copy).then_inc(s_gates, 1)
                    act.wait_ge(s_const, NCONST)
                    nc.scalar.activation(gates[:, :], gates[:, :], ACT.Tanh).then_inc(s_gates, 1)
                q_first(l, 2)
                for m in range(KT):
                    k_first(l, 2, m, (1, l * IB + 1))
                q_second(l, 2)
                q_first(l, 3)
                max_load(l, 0, 0, (1, IB) if l else None, 0)
                nc.scalar.activation(ahead[:, :], gates[:, 0:1], ACT.Exp)
                q_second(l, 3)
                step(l, 0, 0, l * IB, False, True, True, True)
                step(l, 1, 1, l * IB, True, True, True, True)
                with act.Fori(1, B // 2 - 2) as i:
                    for u in range(2):
                        step(l, 2 * i + u, u, i + l * IB, True, True, True, True)
                for b in range(B - 4, B):
                    if b == B - 1:
                        if l == 0:
                            act.wait_ge(s_wg, 16 * 4)
                        else:
                            act.wait_ge(s_wf[1], 16 * 6)
                        high(ffn[l], *EARLY[l][0][:2])
                    step(l, b, b % 2, b // 2 + l * IB, True, b + 3 < B, b + 2 < B, b + 1 < B)
                norm(2 * l + 1, 2)
                for g in range(2):
                    copy_logits(l, g)
                if l == 0:
                    act.wait_ge(s_wf[0], 16 * 6)
                    high(s0, Wuh[:, 0, :], Wu[:, 0, :])
                else:
                    tokens_high(s1, 0, "h_ready", NFT1)
                copy_on(l, B - 1)
                copy_logits(l, 2)
                if l == 0:
                    high(s0, Wuh[:, 1, :], Wu[:, 1, :])
                    tokens_high(s0, 0, "u", NFT0)

            def high(s, dst, src):
                nc.scalar.activation(dst, src, ACT.Copy).then_inc(s["whi"], 1)

            def tokens_high(s, g, ups, count):
                act.wait_ge(s[ups], START + count * g)
                nc.scalar.activation(xh[:, :, :], xT[:, :, bass.ds(g * GT, GT)], ACT.Copy).then_inc(s["xh"], 1)

            ffn = (s0, s1)
            attn(0)

            def scores(part):
                b0, b1 = (g * GB for g in PARTS[part])
                act.wait_ge(s0["lg"], START + part + 1)
                nc.scalar.activation(sc[:, b0:b1, :], ps[0:S, 6 + part, 0:(b1 - b0) * E], ACT.Sigmoid).then_inc(s0["sc"], 1)

            def copy_router(part):
                g0, g1 = PARTS[part]
                act.wait_ge(s0["wT"], START + part + 1)
                nc.scalar.activation(wT[:, g0 * GT:g1 * GT].rearrange("e (g n) -> e g n", n=GT), ps[0:E, 4 + g0:4 + g1, 0:GT],
                                     ACT.Copy).then_inc(s0["wT_copied"], 1)

            scores(0)
            act.wait_ge(sa[0]["x"], START + B)
            for rows, t in ((P, slice(0, 1)), (F - P, slice(1, 2)), (P, slice(2, NFT0))):
                high(s0, Wdh[0:rows, t, :], Wd[0:rows, t, :])

            def hidden_high(i, g):
                rows = tile_rows0(i)
                act.wait_ge(s0["y"], START + NFT0 * g + max(i - 1, 0))
                if i < 2:
                    act.wait_ge(s0["gu"], START + NFT0 * g + i + 1)
                else:
                    act.wait_ge(s0["h"], START + scaled(NFT0 - 1) * g + scaled(i))
                nc.scalar.activation(hhi[i % 2][0:rows, :], hh[i % 2][0:rows, :], ACT.Copy).then_inc(s0["hi"], 1)

            def group0(g, first, last):
                for i in range(NFT0):
                    rows = tile_rows0(i)
                    act.wait_ge(s0["g"], START + NFT0 * g + i + 1)
                    act.wait_ge(s0["gu"], START + NFT0 * g + max(i - 1, 0))
                    nc.scalar.activation(sg[i % 2][0:rows, :], ps[0:rows, i % 2, 0:GT], ACT.Silu).then_inc(s0["silu"], 1)
                    if first and i == 1:
                        copy_router(0)
                    if i > 0:
                        hidden_high(i - 1, g)
                    if first and i == 5:
                        norm(F0, GE)
                    if first and i == 7:
                        copy_logits(0, GE)
                    if first and i == 8:
                        scores(1)
                    if first and i == 12:
                        copy_router(1)
                    if last and i == NFT0 - 2:
                        split_first(1)
                        ctx_high(1, 1, 1, IB)
                    if last and i - 1 in NORM_AT:
                        norm(Q1, NORM_AT.index(i - 1))
                if not last:
                    tokens_high(s0, g + 1, "u", NFT0)
                hidden_high(NFT0 - 1, g)
                act.wait_ge(s0["y"], START + NFT0 * (g + 1))
                nc.scalar.activation(yT[:, :, :], ps[:, 4:4 + KT, 0:GT], ACT.Copy).then_inc(s0["y_copied"], 1)

            group0(0, True, False)
            with act.Fori(1, NG - 1) as g:
                group0(g, False, False)
            scale_q(1)
            group0(NG - 1, False, True)
            act.dma_start(wiT[:, :, :], io["wiT"].rearrange("(k p) n -> p k n", p=P)).then_inc(s_wf[1], 16)
            act.dma_start(woT[:, :, :], io["woT"].rearrange("(t p) n -> p t n", p=P)).then_inc(s_wf[1], 16)
            act.dma_start(BT[:, :], io["loraBT"]).then_inc(s_wf[1], 16)
            attn(1)
            high(s1, woh[:, :, :], woT[:, :, :])

            def copy_lora(run):
                g0, g1 = LORA_RUNS[run]
                act.wait_ge(s1["rT"], START + (2 if g0 == GE else 1))
                nc.scalar.activation(rTh[:, g0 * GT:g1 * GT].rearrange("e (g n) -> e g n", n=GT), ps[0:E1 * R1, 4 + g0:4 + g1, 0:GT],
                                     ACT.Copy).then_inc(s1["rT_copied"], 1)

            copy_lora(0)
            copy_lora(1)

            def group1(g, first, last):
                for i in range(NFT1):
                    act.wait_ge(s1["h_ready"], START + NFT1 * g + i + 1)
                    act.wait_ge(s1["y"], START + NFT1 * g + i + 1)
                    nc.scalar.activation(hh[i % 2][:, :], ps[:, i % 2, 0:GT], ACT.Relu, bias=wib[:, i:i + 1]).then_inc(s1["h"], 1)
                    act.wait_ge(s1["h"], START + NFT1 * g + i + 1)
                    nc.scalar.activation(hhi[i % 2][:, :], hh[i % 2][:, :], ACT.Copy).then_inc(s1["hi"], 1)
                    if first and i == 4:
                        norm(F1N, GE)
                    if first and i == 5:
                        copy_logits(1, GE)
                if first:
                    copy_lora(2)
                if not last:
                    tokens_high(s1, g + 1, "h_ready", NFT1)
                act.wait_ge(s1["y"], START + NFT1 * (g + 1) + 2)
                for k in range(KT):
                    nc.scalar.activation(yT[:, k, :], ps[:, 4 + k, 0:GT], ACT.Identity,
                                         bias=wob[:, k:k + 1]).then_inc(s1["y_copied"], 1)

            group1(0, True, False)
            with act.Fori(1, NG - 1) as g:
                group1(g, False, False)
            group1(NG - 1, False, True)

        @block.vector
        def _(dve):
            nc.vector.memset(bq4[1][:, :], 0.0).then_inc(s_setup, 1)
            nc.vector.memset(bk[1][:, :], 0.0).then_inc(s_setup, 1)
            nc.vector.memset(ps[:, 6, :], 0.0).then_inc(s_setup, 1)
            for p in range(2):
                nc.vector.memset(cT[p][:, :, S2:], 0.0).then_inc(s_setup, 1)

            def stats(p, b, done, count):
                dve.wait_ge(done, START + count)
                dve.sem_inc(s_held, 1)
                nc.vector.bn_stats(stat[:, b, :], x_sb[:, b, :]).then_inc(sn["stat"], 1)

            def stats_end(p, b0, b1):
                dve.wait_ge(sn["stat"], START + B * p + b1)
                for b in range(b0, b1):
                    nc.vector.bn_aggr(mean_var[:, b, :], stat[:, b, :]).then_inc(sn["mv"], 1)

            def norm(p, g):
                dve.wait_ge(sn["rstd"], START + NG * p + g + 1)
                if p > 0:
                    dve.wait_ge((sa[0], s0, sa[1])[p - 1]["x"], START + GB * (g + 1))
                for t in range(GB):
                    b = g * GB + t
                    dve.wait_ge(sn["xnT"], START + B * p + b + 1)
                    nc.vector.tensor_scalar(xn[:, t, :], x_sb[:, b, :], mean_var[:, b, 0:1], rstd[:, b:b + 1],
                                            ALU.subtract, ALU.mult).then_inc(sn["xn"], 1)

            def q_rest(l, g):
                u, j = g % 2, g // 2
                q = sq[u]
                dve.wait_ge(q["q3"], START + l * JQ + j)
                for m in range(KT):
                    dve.wait_ge(q["q1"], START + KT * (l * JQ + j) + m + 1)
                    nc.vector.scalar_tensor_tensor(qr[u][:, m, :], ps[:, QBANK[g] + m, 0:GT], bq4[l][:, m:m + 1], qp[u][:, 0, m, :],
                                                   ALU.add, ALU.subtract).then_inc(q["rest1"], 1)

            def pick(r, n, base, b0, b1):
                bs, sh = slice(b0, b1), [S, b1 - b0, E]
                dve.wait_ge(r, START + base + 1)
                for t in range(b0, b1):
                    x = nc.vector.max(mx8[:, t, :], bsc[:, t, :])
                x.then_inc(r, 1)
                dve.wait_ge(r, START + base + 2)
                for t in range(b0, b1):
                    x = nc.vector.max_index(ix8[:, t, :], mx8[:, t, :], bsc[:, t, :])
                x.then_inc(r, 1)
                dve.wait_ge(r, START + base + 3)
                nc.vector.tensor_copy(ixf[:, bs, :], ix8[:, bs, 0:2]).then_inc(r, 1)
                dve.wait_ge(r, START + base + 4)
                for j in range(n):
                    nc.vector.tensor_tensor(oh[:, j, bs, :], bc(iota8[:, :].unsqueeze(1), sh), bc(ixf[:, bs, j:j + 1], sh),
                                            ALU.is_equal).then_inc(r, 1)

            def route(part):
                r = s0["rt"]
                b0, b1 = (g * GB for g in PARTS[part])
                bs, sh, base = slice(b0, b1), [S, b1 - b0, E], 12 * part
                dve.wait_ge(s0["sc"], START + part + 1)
                nc.vector.tensor_tensor(bsc[:, bs, :], sc[:, bs, :], bc(ebias[:, :].unsqueeze(1), sh), ALU.add).then_inc(r, 1)
                pick(r, 2, base, b0, b1)
                dve.wait_ge(r, START + base + 6)
                nc.vector.tensor_tensor(wsel[:, bs, :], oh[:, 0, bs, :], oh[:, 1, bs, :], ALU.add).then_inc(r, 1)
                dve.wait_ge(r, START + base + 7)
                nc.vector.tensor_tensor(wsel[:, bs, :], wsel[:, bs, :], sc[:, bs, :], ALU.mult).then_inc(r, 1)
                dve.wait_ge(r, START + base + 8)
                nc.vector.reduce_sum(wsum[:, bs], wsel[:, bs, :], axis=AX.X).then_inc(r, 1)
                dve.wait_ge(r, START + base + 9)
                nc.vector.tensor_scalar(wsum[:, bs], wsum[:, bs], ROUTE_EPS, None, ALU.add).then_inc(r, 1)
                dve.wait_ge(r, START + base + 10)
                nc.vector.reciprocal(wrec[:, bs], wsum[:, bs]).then_inc(r, 1)
                dve.wait_ge(r, START + base + 11)
                nc.vector.tensor_tensor(wtok[:, bs, :], wsel[:, bs, :], bc(wrec[:, bs].unsqueeze(2), sh), ALU.mult).then_inc(r, 1)

            def choose(part):
                r = s1["rt"]
                b0, b1 = (g * GB for g in PARTS[part])
                nb, base = b1 - b0, 6 * part
                dve.wait_ge(s1["lg"], START + part + 1)
                lg = ps[0:S, 6 + part, 0:nb * GA].rearrange("s (t n) -> s t n", n=GA)
                nc.vector.tensor_tensor(bsc[:, b0:b1, :], lg[:, :, E1 * R1:GA],
                                        bc(gb_b[:, :].unsqueeze(1), [S, nb, E1]), ALU.add).then_inc(r, 1)
                pick(r, 1, base, b0, b1)
                dve.wait_ge(r, START + base + 5)
                for t in range(b0, b1):
                    x = nc.vector.tensor_tensor(rm[:, t, :].rearrange("s (e r) -> s e r", r=R1),
                                                lg[:, t - b0, 0:E1 * R1].rearrange("s (e r) -> s e r", r=R1),
                                                bc(oh[:, 0, t, :].unsqueeze(2), [S, E1, R1]), ALU.mult)
                x.then_inc(r, 1)

            def lora_low(run):
                g0, g1 = LORA_RUNS[run]
                t = slice(g0 * GT, g1 * GT)
                dve.wait_ge(s1["rT_copied"], START + run + 1)
                nc.vector.tensor_tensor(rTl[:, t].rearrange("e (g n) -> e g n", n=GT), ps[0:E1 * R1, 4 + g0:4 + g1, 0:GT],
                                        rTh[:, t].bitcast(F32).rearrange("e (g n) -> e g n", n=GT), ALU.subtract).then_inc(s1["rTl"], 1)

            def wv_low(l):
                dve.wait_ge(sc_hi, v_parts(l, -1))
                nc.vector.tensor_tensor(wvl[l][:, :, :], w_attn[l]["v"][:, :, :], wvh[:, :, :].bitcast(F32),
                                        ALU.subtract).then_inc(sc_lo, 1)

            def ctx_low(l, n, p):
                dve.wait_ge(sc_hi, v_parts(l, n))
                dve.wait_ge(sa[l]["k_ready"], START + KT * (n + 1))
                c = ctx_width(l, n)
                nc.vector.tensor_tensor(cTl[p][:, :, 0:c], cT[p][:, :, 0:c], cTh[p][:, :, 0:c].bitcast(F32),
                                        ALU.subtract).then_inc(sc_lo, 1)

            def k_rest(l, n, m):
                a = sa[l]
                if m == 0:
                    dve.wait_ge(a["k3"], START + n)
                dve.wait_ge(a["k1"], START + KT * n + m + 1)
                nc.vector.scalar_tensor_tensor(kr[:, m, :], ps[:, 4 + m, 0:S2], bk[l][:, m:m + 1], kp[:, 0, m, :],
                                               ALU.add, ALU.subtract).then_inc(a["k_rest1"], 1)

            def maxima(l, n, p, h0, h1, banks):
                a = sa[l]
                if h0 == 0:
                    if l == 0:
                        dve.wait_ge(a["bias"], START + n + 1)
                        dve.sem_inc(s_held, 1)
                    dve.wait_ge(a["mT"], START + n)
                    dve.sem_inc(s_held, 1)
                for h in range(h0, h1):
                    if l == 0:
                        dve.wait_ge(a["s_ready"], START + H * n + h + 1)
                        dve.sem_inc(s_held, 1)
                        nc.vector.tensor_tensor_reduce(ps[0:S, banks[h % len(banks)], 0:S2], ps[0:S, banks[h % len(banks)], 0:S2], biasq[p][:, :], 1.0,
                                                       -3.0e38, ALU.add, ALU.max, mx[:, h:h + 1]).then_inc(a["max"], 1)
                    else:
                        dve.wait_ge(a["s_ready"], START + H * n + h + 1)
                        nc.vector.reduce_max(mx[:, h:h + 1], ps[0:S, banks[h % len(banks)], 0:S2], axis=AX.X).then_inc(a["max"], 1)

            def split_max(l, n):
                a = sa[l]
                dve.wait_ge(a["max"], START + H * (n + 1))
                nc.vector.tensor_scalar(mxb[:, :], mx[:, :], -1.0, None, ALU.mult).then_inc(a["mhi"], 1)
                dve.wait_ge(a["mhi"], START + n + 1)
                dve.wait_ge(a["mT"], START + n)
                nc.vector.tensor_copy(mxs[:, 0:H], mxb[:, :]).then_inc(a["msplit"], 1)
                nc.vector.scalar_tensor_tensor(mxs[:, H:MROWS * H], mx[:, :], -1.0, mxb[:, :],
                                               ALU.mult, ALU.subtract).then_inc(a["msplit"], 1)

            def divide(l, b):
                a = sa[l]
                dve.wait_ge(a["oT"], START + b + 1)
                o = ps[0:S, 7, :].rearrange("q (h c) -> q h c", c=32)
                nc.vector.reciprocal(rec[:, :], o[:, :, HD]).then_inc(a["rec"], 1)
                dve.wait_ge(a["rec"], START + b + 1)
                dve.wait_ge(a["onT"], START + b)
                dst = on if l == 0 else onv
                nc.vector.tensor_tensor(dst[:, :].rearrange("q (h e) -> q h e", h=H), o[:, :, 0:HD],
                                        bc(rec[:, :].unsqueeze(2), [S, H, HD]), ALU.mult).then_inc(a["on"], 1)
                if l == 0:
                    dve.wait_ge(a["on"], START + b + 1)
                    nc.vector.tensor_tensor(onv[:, :], on[:, :], bv_b[:, :], ALU.add).then_inc(a["onv"], 1)

            def add_bias(l, b):
                a = sa[l]
                dve.wait_ge(a["wo"], START + b + 1)
                nc.vector.tensor_tensor(xb[:, :], ps[0:S, 7, D:2 * D], bo_b[l][:, :], ALU.add).then_inc(a["addb"], 1)

            def add_attention(l, b):
                a = sa[l]
                dve.wait_ge(a["addb"], START + b + 1)
                nc.vector.scalar_tensor_tensor(x_sb[:, b, :], xb[:, :], gates[0:S, l:l + 1], x_sb[:, b, :],
                                               ALU.mult, ALU.add).then_inc(a["x"], 1)
                stats(2 * l + 1, b, a["x"], b + 1)

            def step(l, b, u, i, has_o, has_k, has_2, has_b):
                if has_b:
                    maxima(l, b + 1, 1 - u, 0, 2, SBANKS)
                if has_2:
                    k_rest(l, b + 2, 1)
                if has_o:
                    divide(l, b - 1)
                if has_b:
                    maxima(l, b + 1, 1 - u, 2, 9, SBANKS)
                if has_o:
                    add_bias(l, b - 1)
                if has_b:
                    maxima(l, b + 1, 1 - u, 9, H, SBANKS)
                    split_max(l, b + 1)
                if has_o:
                    add_attention(l, b - 1)
                if has_2:
                    ctx_low(l, b + 2, u)
                if has_k:
                    k_rest(l, b + 3, 0)

            def attn(l):
                if l == 0:
                    stats_x(0)
                    stats_x(1)
                    stats_x(2)
                    for m in range(KT):
                        k_rest(l, 0, m)
                    norm(Q0, 0)
                    norm(Q0, 1)
                    stats_x(3)
                    wv_low(0)
                    ctx_low(0, 0, 0)
                    norm(Q0, 2)
                    q_rest(l, 0)
                    norm(Q0, 3)
                else:
                    for m in range(KT):
                        k_rest(l, 0, m)
                    ctx_low(1, 0, 0)
                    q_rest(l, 0)
                    norm(Q1, GE)
                for m in range(KT):
                    k_rest(l, 1, m)
                q_rest(l, 1)
                ctx_low(l, 1, 1)
                maxima(l, 0, 0, 0, 3, SBANKS0)
                q_rest(l, 2)
                maxima(l, 0, 0, 3, 8, SBANKS0)
                k_rest(l, 2, 0)
                maxima(l, 0, 0, 8, H, SBANKS0)
                split_max(l, 0)
                q_rest(l, 3)
                if l == 0:
                    dve.wait_ge(s_const, NCONST)
                    dve.wait_ge(s_gates, 2)
                step(l, 0, 0, l * IB, False, True, True, True)
                step(l, 1, 1, l * IB, True, True, True, True)
                with dve.Fori(1, B // 2 - 2) as i:
                    for u in range(2):
                        step(l, 2 * i + u, u, i + l * IB, True, True, True, True)
                for b in range(B - 4, B):
                    if b == B - 1:
                        norm(2 * l + 1, 0)
                    step(l, b, b % 2, b // 2 + l * IB, True, b + 3 < B, b + 2 < B, b + 1 < B)
                    if b == B - 3:
                        stats_end(2 * l + 1, 0, GE * GB)
                norm(2 * l + 1, 1)
                norm(2 * l + 1, 2)
                for j, (wh, w, wl) in enumerate(EARLY[l]):
                    low((s0, s1)[l], j + 1, wl, w, wh)
                stats_end(2 * l + 1, GE * GB, B - 1)
                divide(l, B - 1)
                if l == 0:
                    low(s0, KT + 1, Wul[:, 0, :], Wu[:, 0, :], Wuh[:, 0, :])
                else:
                    tokens_low(s1, 0)
                add_bias(l, B - 1)
                add_attention(l, B - 1)
                stats_end(2 * l + 1, B - 1, B)
                if l == 0:
                    low(s0, KT + 2, Wul[:, 1, :], Wu[:, 1, :], Wuh[:, 1, :])
                    tokens_low(s0, 0)

            def stats_x(g):
                dve.wait_ge(s_x[g], 16)
                for b in range(g * GB, (g + 1) * GB):
                    nc.vector.bn_stats(stat[:, b, :], x_sb[:, b, :]).then_inc(sn["stat"], 1)
                stats_end(Q0, g * GB, (g + 1) * GB)

            for c in COUNTED[1::3]:
                dve.sem_inc(c, START)
            dve.sem_inc(s_started, 1)
            dve.wait_ge(s_started, 3)
            def low(s, whole, dst, src, hi):
                dve.wait_ge(s["whi"], START + whole)
                nc.vector.tensor_tensor(dst, src, hi.bitcast(F32), ALU.subtract).then_inc(s["wlo"], 1)

            def tokens_low(s, g):
                dve.wait_ge(s["xh"], START + g + 1)
                dve.sem_inc(s_held, 1)
                nc.vector.tensor_tensor(xl[:, :, :], xT[:, :, bass.ds(g * GT, GT)], xh[:, :, :].bitcast(F32),
                                        ALU.subtract).then_inc(s["xl"], 1)

            def hidden_low(s, i, count, rows):
                dve.wait_ge(s["hi"], START + count + i + 1)
                nc.vector.tensor_tensor(hlo[i % 2][0:rows, :], hh[i % 2][0:rows, :], hhi[i % 2][0:rows, :].bitcast(F32),
                                        ALU.subtract).then_inc(s["lo"], 1)

            attn(0)
            dve.wait_ge(sa[0]["x"], START + B)
            route(0)

            def residual(s, l, g):
                for t in range(GB):
                    b = g * GB + t
                    dve.wait_ge(s["yT"], START + KT * g + t // 2 + 1)
                    nc.vector.scalar_tensor_tensor(x_sb[:, b, :], ps[0:S, 6 + t // 2, (t % 2) * D:(t % 2 + 1) * D],
                                                   gates[0:S, 2 + l:3 + l], x_sb[:, b, :],
                                                   ALU.mult, ALU.add).then_inc(s["x"], 1)
                if l == 0:
                    for t in range(GB):
                        stats(Q1, g * GB + t, s["x"], g * GB + t + 1)

            def group0(g, first, last):
                for i in range(NFT0):
                    rows = tile_rows0(i)
                    dve.wait_ge(s0["silu"], START + NFT0 * g + i + 1)
                    dve.wait_ge(s0["u"], START + NFT0 * g + i + 1)
                    if i < 2:
                        dve.wait_ge(s0["y"], START + NFT0 * g)
                        dst = hh[i % 2]
                    else:
                        dve.wait_ge(s0["h"], START + scaled(NFT0 - 1) * g + scaled(max(i - 2, 1)))
                        dst = gu[i % 2]
                    nc.vector.tensor_tensor(dst[0:rows, :], ps[0:rows, 2 + i % 2, 0:GT], sg[i % 2][0:rows, :],
                                            ALU.mult).then_inc(s0["gu"], 1)
                    if first and i == 0:
                        for j, (wrows, t) in enumerate(((P, slice(0, 1)), (F - P, slice(1, 2)), (P, slice(2, NFT0)))):
                            low(s0, 2 * KT + j + 1, Wdl[0:wrows, t, :], Wd[0:wrows, t, :], Wdh[0:wrows, t, :])
                    if i > 0:
                        hidden_low(s0, i - 1, NFT0 * g, tile_rows0(i - 1))
                    if i == 2 and not first:
                        residual(s0, 0, g - 1)
                    if i == 2 and last:
                        stats_end(Q1, 0, B - GB)
                    if first and i == 3:
                        norm(F0, GE)
                    if first and i == 9:
                        route(1)
                    if last and i == NFT0 - 2:
                        wv_low(1)
                    if last and i + 1 in NORM_AT:
                        norm(Q1, NORM_AT.index(i + 1))
                if not last:
                    tokens_low(s0, g + 1)
                hidden_low(s0, NFT0 - 1, NFT0 * g, P)
                if last:
                    residual(s0, 0, g)

            group0(0, True, False)
            with dve.Fori(1, NG - 1) as g:
                group0(g, False, False)
            group0(NG - 1, False, True)
            stats_end(Q1, B - GB, B)
            dve.wait_ge(s0["x"], START + B)
            attn(1)
            dve.wait_ge(sa[1]["x"], START + B)
            choose(0)
            lora_low(0)
            low(s1, 3, wol[:, :, :], woT[:, :, :], woh[:, :, :])
            lora_low(1)

            def group1(g, first, last):
                for i in range(NFT1):
                    hidden_low(s1, i, NFT1 * g, P)
                    if i == 2 and not first:
                        residual(s1, 1, g - 1)
                    if first and i == 1:
                        norm(F1N, GE)
                    if first and i == 5:
                        choose(1)
                if first:
                    lora_low(2)
                if not last:
                    tokens_low(s1, g + 1)
                if last:
                    residual(s1, 1, g)

            group1(0, True, False)
            with dve.Fori(1, NG - 1) as g:
                group1(g, False, False)
            group1(NG - 1, False, True)

        @block.tensor
        def _(pe):
            mm = nc.tensor.matmul

            def split_mm(dst, w_parts, x_parts, first, last):
                for j, (wp, xp) in enumerate(((0, 0), (0, 1), (1, 0))):
                    x = mm(dst, w_parts[wp], x_parts[xp], start=first and j == 0, stop=last and j == 2)
                return x

            def norm(p, g):
                banks = NBANKS[p]
                before = [j for j in range(g) if banks[j] == banks[g]]
                if before:
                    pe.wait_ge(sn["xT"], START + NG * p + before[-1] + 1)
                for t in range(GB):
                    pe.wait_ge(sn["xn"], START + B * p + GB * g + t + 1)
                    for k in range(KT):
                        x = nc.tensor.transpose(ps[:, banks[g] + k, t * S:(t + 1) * S],
                                                xn[:, t, k * P:(k + 1) * P], ident[0:S, 0:S])
                    x.then_inc(sn["xnT"], 1)

            def project_q(l, g, m):
                q = sq[g % 2]
                if m == 0:
                    pe.wait_ge(sn["xT"], START + NG * 2 * l + (g + 1 if g < 1 + l else NG))
                    if g == 3:
                        pe.wait_ge(sq[0]["rest1"], START + KT * JQ * (l + 1))
                for k in range(KT):
                    x = mm(ps[:, QBANK[g] + m, 0:GT], w_attn[l]["q"][:, k, m * P:(m + 1) * P],
                           xT[:, k, g * GT:(g + 1) * GT], start=k == 0, stop=k == KT - 1)
                x.then_inc(q["ready"], 1)

            def logits(l, g):
                s, w, n = ((s0, Wr, E), (s1, WgA, GA))[l]
                if g == 0 and l == 0:
                    pe.wait_ge(s_wg, 16 * 4)
                elif g == 0:
                    pe.wait_ge(s_wf[1], 16 * 6)
                pe.wait_ge(sn["xT"], START + NG * (2 * l + 1) + g + 1)
                if g == 2:
                    pe.wait_ge(s["lg_copied"], START + g - 1)
                elif g < 2:
                    pe.wait_ge(sa[l]["v_copied"], START + 2 * B)
                for k in range(KT):
                    x = mm(ps[0:n, LBANK[g], 0:GT], w[:, k, :], xT[:, k, g * GT:(g + 1) * GT], start=k == 0, stop=k == KT - 1)
                x.then_inc(s["lgT"], 1)

            def turn_logits(l, part):
                s, n = ((s0, E), (s1, GA))[l]
                g0, g1 = PARTS[part]
                pe.wait_ge(s["lg_copied"], START + g1)
                for b in range(g0 * GB, g1 * GB):
                    c = (b - g0 * GB) * n
                    x = nc.tensor.transpose(ps[0:S, 6 + part, c:c + n], lgT[0:n, b * S:(b + 1) * S], ident[0:n, 0:n])
                x.then_inc(s["lg"], 1)

            def project_k(l, n, p, idx, m):
                a, d = sa[l], sd
                if m == 0:
                    pe.wait_ge(d["ctx"][p], 16 * (idx + 1))
                if isinstance(n, int) and n == 2:
                    pe.wait_ge(a["k_rest1"], START + KT + m + 1)
                elif not isinstance(n, int) or n > 2:
                    pe.wait_ge(a["v_copied"], START + 2 * (n - 2) + m + 1)
                elif n == 1:
                    pe.wait_ge(a["v_copied"], START + m + 1)
                for k in range(KT):
                    x = mm(ps[:, 4 + m, 0:S2], w_attn[l]["k"][:, k, m * P:(m + 1) * P], cT[p][:, k, 0:S2],
                           start=k == 0, stop=k == KT - 1)
                x.then_inc(a["k_ready"], 1)

            def project_v(l, n, p, t, k, last_k):
                a = sa[l]
                if t != 1 and k == 0:
                    pe.wait_ge(a["k_rest1"], START + KT * last_k + t // 2 + 1)
                if t == 0 and k == 0:
                    pe.wait_ge(sc_lo, v_parts(l, n))
                rows = slice(t * P, (t + 1) * P)
                x = split_mm(ps[:, 4 + t // 2, (t % 2) * D:(t % 2 + 1) * D], (cTh[p][:, k, rows], cTl[p][:, k, rows]),
                             (wvh[:, k, :], wvl[l][:, k, :]), k == 0, k == KT - 1)
                if t > 0 and k == KT - 1:
                    x.then_inc(a["v_ready"], 1)

            def score(l, n, p, h, banks):
                a = sa[l]
                if not isinstance(n, int) or H * n + h >= len(banks):
                    pe.wait_ge(a["max"], START + H * n + h + 1 - len(banks))
                mm(ps[0:S, banks[h % len(banks)], 0:S2], QS[p][0:SROWS, h, :], KS[p][0:SROWS, h * S2:(h + 1) * S2],
                   start=True, stop=True).then_inc(a["s_ready"], 1)

            def turn_max(l, n, done, bank):
                a = sa[l]
                pe.wait_ge(a["msplit"], START + MROWS * (n + 1))
                if done is not None:
                    pe.wait_ge(a["mp"], START + n)
                    pe.wait_ge(a["addb"], START + done)
                nc.tensor.transpose(ps[0:MROWS * H, bank, 0:S], mxs[:, :], ident[0:S, 0:S]).then_inc(a["mT"], 1)

            def score_T(l, b, p, hg, t):
                a = sa[l]
                c = hg * NKT + t
                pe.wait_ge(a["exp"], START + NKT * NHG * b + c + 1)
                dst = ps[:, c % 2, 0:HQ * S]
                if l == 0:
                    rows = KROWS[t]
                    mm(dst, ident_bf[0:rows, :], bc(biasT[p][0:rows, t, :].unsqueeze(1), [rows, HQ, S]),
                       start=True, stop=False)
                for j in range(HQ):
                    h = HQ * hg + j
                    x = mm(ps[:, c % 2, j * S:(j + 1) * S], KS[p][:, h * S2 + t * P:h * S2 + (t + 1) * P], QS[p][:, h, :],
                           start=l == 1, stop=l == 1 or j == HQ - 1)
                x.then_inc(a["sT"], 1)

            def weigh(l, b, p, hg):
                a = sa[l]
                for t in range(NKT):
                    pe.wait_ge(a["exp"], START + NKT * NHG * b + hg * NKT + t + 1 + 2)
                    for j in range(HQ):
                        x = mm(ps[32 * j:32 * j + HD + 1, 6, hg * S:(hg + 1) * S], V1[p][0:KROWS[t], t, HQ * hg + j, :],
                               prob[0:KROWS[t], t, hg, j * S:(j + 1) * S], start=t == 0, stop=t == NKT - 1)
                x.then_inc(a["pv"], 1)

            def turn_o(l, b, last_n):
                a = sa[l]
                pe.wait_ge(a["o_copied"], START + b + 1)
                pe.wait_ge(a["mp"], START + last_n + 1)
                pe.wait_ge(a["addb"], START + b)
                for hg in range(NHG):
                    x = nc.tensor.transpose(ps[0:S, 7, hg * P:(hg + 1) * P], oT_sb[:, hg * S:(hg + 1) * S], ident[:, :])
                x.then_inc(a["oT"], 1)

            def turn_on(l, b):
                a = sa[l]
                pe.wait_ge(a["on"], START + b + 1)
                if l == 0:
                    pe.wait_ge(a["onv"], START + b + 1)
                for k in range(KT):
                    x = nc.tensor.transpose(ps[:, 7, k * S:(k + 1) * S], onv[:, k * P:(k + 1) * P], ident[0:S, 0:S])
                x.then_inc(a["onT"], 1)

            def project_o(l, b):
                a = sa[l]
                pe.wait_ge(a["onT_copied"], START + b + 1)
                for k in range(KT):
                    x = mm(ps[0:S, 7, D:2 * D], onT[:, k, :], w_attn[l]["o"][:, k, :], start=k == 0, stop=k == KT - 1)
                x.then_inc(a["wo"], 1)

            def step(l, b, u, i, has_o, has_k, has_2, has_b):
                a, d = sa[l], sd

                def next_score(h):
                    if has_b:
                        if h % HH == 0:
                            pe.wait_ge(d["kload"][h // HH][1 - u], 32 * (i + u + 1))
                        score(l, b + 1, 1 - u, h, SBANKS)

                next_score(0)
                next_score(1)
                if has_o:
                    turn_o(l, b - 1, b)
                if l == 0:
                    pe.wait_ge(a["biasT"], START + b + 1)
                pe.wait_ge(d["mload"][u], 16 * (i + 1))
                score_T(l, b, u, 0, 0)
                score_T(l, b, u, 0, 1)
                next_score(2)
                next_score(3)
                score_T(l, b, u, 0, 2)
                if has_o:
                    turn_on(l, b - 1)
                for t in range(NKT):
                    next_score(4 + t)
                    score_T(l, b, u, 1, t)
                weigh(l, b, u, 0)
                next_score(7)
                if has_o:
                    project_o(l, b - 1)
                if not has_b:
                    norm(2 * l + 1, 0)
                next_score(8)
                for t in range(NKT):
                    for k in range(KT):
                        if has_b:
                            project_v(l, b + 1, 1 - u, t, k, b + 2 if has_2 else B - 1)
                        if k == t % 2:
                            next_score(9 + t)
                next_score(12)
                for t in range(NKT):
                    score_T(l, b, u, 2, t)
                    next_score(13 + t)
                if not has_b:
                    norm(2 * l + 1, 1)
                    logits(l, 0)
                weigh(l, b, u, 1)
                for t in range(NKT):
                    score_T(l, b, u, 3, t)
                    if t == 1 and has_b:
                        turn_max(l, b + 1, b, 7)
                if not has_b:
                    norm(2 * l + 1, 2)
                    logits(l, 1)
                if has_k:
                    project_k(l, b + 3, 1 - u, i + 1 + u, 0)
                weigh(l, b, u, 2)
                weigh(l, b, u, 3)
                if has_k:
                    project_k(l, b + 3, 1 - u, i + 1 + u, 1)

            def attn(l):
                pe.wait_ge(s_wa[l]["k"], 16)
                for m in range(KT):
                    project_k(l, 0, 0, l * IB, m)
                def values():
                    for t in range(NKT):
                        for k in range(KT):
                            project_v(l, 0, 0, t, k, 0)

                def queries(g):
                    for m in range(KT):
                        project_q(l, g, m)

                if l == 0:
                    pe.wait_ge(s_setup, NSETUP)
                    norm(Q0, 0)
                    norm(Q0, 1)
                pe.wait_ge(s_wq[l], 2 - l)
                queries(0)
                if l == 0:
                    norm(Q0, 2)
                    norm(Q0, 3)
                values()
                for m in range(KT):
                    project_k(l, 1, 1, l * IB, m)
                queries(1)
                if l == 1:
                    norm(Q1, GE)
                for m in range(KT):
                    project_k(l, 2, 0, 1 + l * IB, m)
                queries(2)
                pe.wait_ge(s_wa[l]["o"], 16)
                pe.wait_ge(sq[1]["rest1"], START + KT * (l * JQ + 1))
                pe.sem_inc(sa[l]["exp"], 2)
                pe.sem_inc(sa[l]["pv"], NHG)
                for half in range(2):
                    pe.wait_ge(sd["kload"][half][0], 32 * (l * IB + 1))
                for h in range(H):
                    score(l, 0, 0, h, SBANKS0)
                    if h in Q3_AT:
                        project_q(l, 3, Q3_AT.index(h))
                turn_max(l, 0, None, 0)
                for u in range(2):
                    pe.wait_ge(sq[u]["rest1"], START + KT * JQ * (l + 1))
                pe.wait_ge(s_rows, 32 if l == 0 else 32 + 64)
                if l == 1:
                    pe.wait_ge(s_vones, 2)
                if l == 0:
                    pe.wait_ge(s_gates, 1)
                step(l, 0, 0, l * IB, False, True, True, True)
                step(l, 1, 1, l * IB, True, True, True, True)
                with pe.Fori(1, B // 2 - 2) as i:
                    for u in range(2):
                        step(l, 2 * i + u, u, i + l * IB, True, True, True, True)
                for b in range(B - 4, B):
                    step(l, b, b % 2, b // 2 + l * IB, True, b + 3 < B, b + 2 < B, b + 1 < B)
                turn_o(l, B - 1, B - 1)
                turn_on(l, B - 1)
                logits(l, 2)
                project_o(l, B - 1)
                turn_logits(l, 0)

            def turn_y(s, g, copies):
                pe.wait_ge(s["y_copied"], START + copies * (g + 1))
                pe.wait_ge(s["x"], START + GB * g)
                for t in range(GB):
                    for k in range(KT):
                        x = nc.tensor.transpose(ps[0:S, 6 + t // 2, (t % 2) * D + k * P:(t % 2) * D + (k + 1) * P],
                                                yT[:, k, t * S:(t + 1) * S], ident[:, :])
                    if t % 2:
                        x.then_inc(s["yT"], 1)

            for c in COUNTED[2::3]:
                pe.sem_inc(c, START)
            pe.sem_inc(s_started, 1)
            pe.wait_ge(s_started, 3)
            pe.sem_inc(sn["xnT"], GB)
            pe.wait_ge(s_ident, 16)
            attn(0)

            def spread_weights(part):
                g0, g1 = PARTS[part]
                pe.wait_ge(s0["rt"], START + 12 * (part + 1))
                for b in range(g0 * GB, g1 * GB):
                    x = nc.tensor.transpose(ps[0:E, 4 + b // GB, (b % GB) * S:(b % GB + 1) * S], wtok[:, b, :], ident[0:S, 0:S])
                x.then_inc(s0["wT"], 1)

            def up0(i, g):
                cols = slice(tile_col0(i), tile_col0(i) + P)
                if i == 0:
                    pe.wait_ge(s0["xl"], START + g + 1)
                pe.wait_ge(s0["silu"], START + NFT0 * g + max(i - 1, 0))
                for k in range(KT):
                    x = split_mm(ps[:, i % 2, 0:GT], (Wgh[:, k, cols], Wgl[:, k, cols]), (xh[:, k, :], xl[:, k, :]),
                                 k == 0, k == KT - 1)
                x.then_inc(s0["g"], 1)
                pe.wait_ge(s0["gu"], START + NFT0 * g + max(i - 1, 0))
                for k in range(KT):
                    x = split_mm(ps[:, 2 + i % 2, 0:GT], (Wuh[:, k, cols], Wul[:, k, cols]), (xh[:, k, :], xl[:, k, :]),
                                 k == 0, k == KT - 1)
                x.then_inc(s0["u"], 1)

            def down0(i, g):
                rows = tile_rows0(i)
                if i == 0:
                    pe.wait_ge(s0["y_copied"], START + g)
                pe.wait_ge(s0["lo"], START + NFT0 * g + i + 1)
                for m in range(KT):
                    cols = slice(m * P, (m + 1) * P)
                    x = split_mm(ps[:, 4 + m, 0:GT], (Wdh[0:rows, i, cols], Wdl[0:rows, i, cols]),
                                 (hhi[i % 2][0:rows, :], hlo[i % 2][0:rows, :]), i == 0, i == NFT0 - 1)
                x.then_inc(s0["y"], 1)

            def group0(g, first, last):
                for i in range(NFT0):
                    if i > 0 or first:
                        up0(i, g)
                    if last and i in NORM_AT:
                        if i == NORM_AT[0]:
                            pe.wait_ge(s0["x"], START + GB * (NG - 1))
                        norm(Q1, NORM_AT.index(i))
                    if first and i == 1:
                        spread_weights(0)
                    if first and i == 5:
                        norm(F0, GE)
                    if first and i == 7:
                        logits(0, GE)
                    if first and i == 8:
                        turn_logits(0, 1)
                    if first and i == 12:
                        spread_weights(1)
                    if first and i == 2:
                        pe.wait_ge(s0["wT_copied"], START + 1)
                        pe.wait_ge(s0["wlo"], START + 7)
                    if i == 2 and not first:
                        turn_y(s0, g - 1, 1)
                    if i > 1:
                        down0(i - 2, g)
                down0(NFT0 - 2, g)
                if not last:
                    up0(0, g + 1)
                down0(NFT0 - 1, g)
                if first:
                    pe.wait_ge(s0["wT_copied"], START + 2)
                if last:
                    pe.wait_ge(sn["xT"], START + NG * Q1 + GE)
                    turn_y(s0, g, 1)

            pe.wait_ge(s0["wlo"], START + 4)
            group0(0, True, False)
            with pe.Fori(1, NG - 1) as g:
                group0(g, False, False)
            group0(NG - 1, False, True)
            attn(1)
            pe.sem_inc(s1["y"], 2)

            def turn_lora(part):
                g0, g1 = PARTS[part]
                pe.wait_ge(s1["rt"], START + 6 * (part + 1))
                for b in range(g0 * GB, g1 * GB):
                    x = nc.tensor.transpose(ps[0:E1 * R1, 4 + b // GB, (b % GB) * S:(b % GB + 1) * S], rm[:, b, :], ident[0:S, 0:S])
                x.then_inc(s1["rT"], 1)

            def up1(i, g):
                cols = slice(i * P, (i + 1) * P)
                if i == 0:
                    pe.wait_ge(s1["xl"], START + g + 1)
                pe.wait_ge(s1["h"], START + NFT1 * g + max(i - 1, 0))
                for k in range(KT):
                    split_mm(ps[:, i % 2, 0:GT], (wih[:, k, cols], wil[:, k, cols]), (xh[:, k, :], xl[:, k, :]), k == 0, False)

            def lora1(i, g):
                cols, tok = slice(i * P, (i + 1) * P), bass.ds(g * GT, GT)
                split_mm(ps[:, i % 2, 0:GT], (BTh[:, cols], BTl[:, cols]), (rTh[:, tok], rTl[:, tok]),
                         False, True).then_inc(s1["h_ready"], 1)

            def down1(i, g):
                if i == 0:
                    pe.wait_ge(s1["y_copied"], START + KT * g)
                pe.wait_ge(s1["lo"], START + NFT1 * g + i + 1)
                for m in range(KT):
                    cols = slice(m * P, (m + 1) * P)
                    x = split_mm(ps[:, 4 + m, 0:GT], (woh[:, i, cols], wol[:, i, cols]), (hhi[i % 2][:, :], hlo[i % 2][:, :]),
                                 i == 0, i == NFT1 - 1)
                x.then_inc(s1["y"], 1)

            def group1(g, first, last):
                if first:
                    for i in range(2):
                        up1(i, g)
                    turn_lora(0)
                    pe.wait_ge(s1["rTl"], START + 1)
                    for i in range(2):
                        lora1(i, g)
                for i in range(2 if first else 0, NFT1):
                    up1(i, g)
                    lora1(i, g)
                    if first and i == 2:
                        pe.wait_ge(s1["wlo"], START + 3)
                        pe.wait_ge(s1["rTl"], START + 2)
                    if first and i == 4:
                        norm(F1N, GE)
                    if first and i == 5:
                        logits(1, GE)
                    if first and i == 6:
                        turn_logits(1, 1)
                    if i == 2 and not first:
                        turn_y(s1, g - 1, KT)
                    if i > 1:
                        down1(i - 2, g)
                down1(NFT1 - 2, g)
                if first:
                    turn_lora(1)
                down1(NFT1 - 1, g)
                if first:
                    pe.wait_ge(s1["rTl"], START + 3)
                if last:
                    turn_y(s1, g, KT)

            pe.wait_ge(s1["wlo"], START + 2)
            group1(0, True, False)
            with pe.Fori(1, NG - 1) as g:
                group1(g, False, False)
            group1(NG - 1, False, True)


_DIRECT = ["x", "g_xattn", "g_ffn", "L0_xattn_Wv", "L0_xattn_bv", "L0_xattn_Wo", "L0_xattn_bo",
           "L0_ffn_W_gate_router", "L0_ffn_expert_bias", "L0_ffn_Wg", "L0_ffn_Wu", "L0_ffn_Wd", "L0_ffn_Wg_s",
           "L0_ffn_Wu_s", "L0_ffn_Wd_s", "L1_xattn_W_v", "L1_xattn_W_o", "L1_xattn_b_o", "L1_ffn_gate_b",
           "L1_ffn_wi_b", "L1_ffn_wo_b"]


def kernel(**inputs):
    import numpy as np
    import concourse.bacc as bacc
    from concourse.bass_utils import run_bass_kernel_spmd

    a = {n: np.asarray(v) for n, v in inputs.items()}
    lay = {n: a[n] for n in _DIRECT}

    def by_dim(w):
        return w.reshape(w.shape[:-1] + (H, HD)).swapaxes(-1, -2).reshape(w.shape)

    for n in ("L0_xattn_Wq", "L0_xattn_bq", "L0_xattn_Wk", "L0_xattn_bk", "L1_xattn_W_q", "L1_xattn_W_k"):
        lay[n] = by_dim(a[n])
    for n in ("L0_xattn_bq", "L0_xattn_bk"):
        lay[n] = lay[n].reshape(-1, P).T
    for n in ("L1_ffn_wi_b", "L1_ffn_wo_b"):
        lay[n] = a[n].reshape(-1, P).T
    lay["ctxT"] = a["ctx_1024"].reshape(B, S2, KT, P).transpose(0, 3, 2, 1)
    mask = a["mask_Bx1xSxS2_bk1"].reshape(B, S, S2)
    lay["mask"] = mask
    rows = np.zeros((B, NKT * P, S), mask.dtype)
    rows[:, :S2] = mask.transpose(0, 2, 1)
    lay["maskT"] = rows.reshape(B, NKT, P, S).transpose(0, 2, 1, 3)
    lay["gateT"] = a["L1_ffn_gate_W"].T
    lay["loraAT"] = a["L1_ffn_lora_A"].reshape(E1 * R1, D).T
    lay["loraBT"] = a["L1_ffn_lora_B"].transpose(0, 2, 1).reshape(E1 * R1, F1)
    lay["wiT"], lay["woT"] = a["L1_ffn_wi_W"].T, a["L1_ffn_wo_W"].T
    lay["ident"] = np.eye(P, dtype=np.float32)
    lay["iota8"] = np.arange(E, dtype=np.float32)

    nc = bacc.Bacc("TRN2", target_bir_lowering=False, num_devices=1)
    arrays, io = {}, {}
    for n, v in lay.items():
        v = np.ascontiguousarray(v)
        arrays[f"in_{n}"] = v
        io[n] = nc.dram_tensor(f"in_{n}", v.shape, mybir.dt.from_np(v.dtype), kind="ExternalInput").ap()
    out = nc.dram_tensor("out", (B, S, D), F32, kind="ExternalOutput").ap()
    build(nc, io, out)
    r = run_bass_kernel_spmd(nc, [arrays], core_ids=[0])
    return r.results[0]["out"]
```
